# Optimizing a Trainium2 kernel written in Bass

```python
import numpy as np
import jax
import jax.numpy as jnp

def _softmax(x, axis=-1):
    return jax.nn.softmax(x, axis=axis)

def _gelu(x):
    return jax.nn.gelu(x, approximate=True)

def _silu(x):
    return jax.nn.silu(x)

def _sigmoid(x):
    return jax.nn.sigmoid(x)

def _layernorm(x, axis=-1, eps=1e-05):
    m = jnp.mean(x, axis=axis, keepdims=True)
    v = jnp.var(x, axis=axis, keepdims=True)
    return (x - m) / jnp.sqrt(v + eps)

def _scatter_add(tgt, idx, src, axis=0):
    return tgt.at[idx].add(src)

def _segment_sum(src, seg, n):
    return jax.ops.segment_sum(src, seg, n)
kernel_name = 'mk_xattn_ffn_d4_seqx_r8_b4a5d9'

def setup_inputs(seed: int=0):
    np.random.seed(seed)
    _w = jnp.asarray

    def _rec_inputs():
        import jax
        import jax.numpy as jnp
        _rk = jax.random.key(seed)
        x = -0.0005207 + 1.001 * jax.random.normal(jax.random.fold_in(_rk, 1), (4, 256, 128), jnp.float32)
        _lenS = 256 - jax.random.randint(jax.random.fold_in(_rk, 7), (4,), 0, max(1, 256 // 4) + 1, jnp.int32)
        _lenS2 = 64 - jax.random.randint(jax.random.fold_in(_rk, 8), (4,), 0, max(1, 64 // 4) + 1, jnp.int32)
        _ctx_1024P = jax.random.normal(jax.random.fold_in(_rk, 11), (4, 16, 128), jnp.float32)
        _ctx_1024c = jax.random.dirichlet(jax.random.fold_in(_rk, 511), 0.3 * jnp.ones((16,), jnp.float32), (4, 64))
        _ctx_1024t = jnp.einsum('bsk,bkd->bsd', _ctx_1024c, _ctx_1024P)
        _ctx_1024t = _ctx_1024t * jax.lax.rsqrt(jnp.mean(jnp.square(_ctx_1024t)) + 1e-12) * 0.953939
        ctx_1024 = -1.39393e-06 + 0.999914 * (_ctx_1024t + 0.3 * jax.random.normal(jax.random.fold_in(_rk, 611), (4, 64, 128), jnp.float32))
        _validS = jnp.arange(256)[None, :] < _lenS[:, None]
        _validS2 = jnp.arange(64)[None, :] < _lenS2[:, None]
        _causal = jnp.tril(jnp.ones((256, 256), dtype=bool))
        mask_BxS2_bf1 = jnp.ones((4, 64), dtype=bool)
        mask_Bx1xSxS2_ik1 = jnp.where(jnp.broadcast_to(_validS2[:, None, None, :], (4, 1, 256, 64)), 1, 0).astype(jnp.int32)
        mask_Bx1x1xS2_ik0 = jnp.where(jnp.broadcast_to(_validS2[:, None, None, :], (4, 1, 1, 64)), 0, 1).astype(jnp.int32)
        return (x, ctx_1024, mask_BxS2_bf1, mask_Bx1xSxS2_ik1, mask_Bx1x1xS2_ik0)
    x, ctx_1024, mask_BxS2_bf1, mask_Bx1xSxS2_ik1, mask_Bx1x1xS2_ik0 = _rec_inputs()

    def _L0_xattn_setup():
        import jax, jax.numpy as jnp
        import numpy as np
        B, M, N = (2, 128, 256)
        D_MODEL = 128
        H, HKV, D = (16, 4, 64)
        GROUPS = H // HKV
        THETA = 10000.0
        MAX_REL = M + N

        def _freqs_cis(dim, seq_len, theta):
            inv = 1.0 / theta ** (jnp.arange(0, dim, 2, dtype=jnp.float32) / dim)
            f = jnp.outer(jnp.arange(seq_len, dtype=jnp.float32), inv)
            f = jnp.repeat(f, 2, axis=-1)
            return (jnp.cos(f), jnp.sin(f))

        def _apply_rope(x, cos, sin):
            cos = cos[None, None]
            sin = sin[None, None]
            d = x.shape[-1]
            x1, x2 = (x[..., :d // 2], x[..., d // 2:])
            c1, c2 = (cos[..., :d // 2], cos[..., d // 2:])
            s1, s2 = (sin[..., :d // 2], sin[..., d // 2:])
            return jnp.concatenate([x1 * c1 - x2 * s1, x1 * s2 + x2 * c2], axis=-1)
        key = jax.random.key(seed)
        ks = jax.random.split(key, 8)
        sc = lambda fan_in: 1.0 / np.sqrt(fan_in)
        return {'q': jax.random.normal(ks[0], (B, M, D_MODEL), jnp.float32), 'kv': jax.random.normal(ks[1], (B, N, D_MODEL), jnp.float32), 'Wq': jax.random.normal(ks[2], (D_MODEL, H * D), jnp.float32) * sc(D_MODEL), 'Wk': jax.random.normal(ks[3], (D_MODEL, HKV * D), jnp.float32) * sc(D_MODEL), 'Wv': jax.random.normal(ks[4], (D_MODEL, HKV * D), jnp.float32) * sc(D_MODEL), 'Wo': jax.random.normal(ks[5], (H * D, D_MODEL), jnp.float32) * sc(H * D), 'rel_pos_bias': jnp.zeros((H, MAX_REL), jnp.float32), 'mask': jnp.ones((B, N), dtype=bool)}
    _L0_xattn_all = _L0_xattn_setup()
    _L0_xattn_in = {k: v for k, v in _L0_xattn_all.items() if k in ('Wq', 'Wk', 'Wv', 'Wo', 'rel_pos_bias')}
    del _L0_xattn_all

    def _L0_ffn_setup():
        import jax, jax.numpy as jnp
        import numpy as np
        B, S, H, I, E = (2, 512, 128, 64, 8)
        key = jax.random.key(seed)
        ks = jax.random.split(key, 5)
        scale_h = 1.0 / np.sqrt(H)
        scale_i = 1.0 / np.sqrt(I)
        return {'hidden_states': jax.random.normal(ks[0], (B, S, H), dtype=jnp.float32), 'gate_w': jax.random.normal(ks[1], (E, H), dtype=jnp.float32) * scale_h, 'w_gate': jax.random.normal(ks[2], (E, I, H), dtype=jnp.float32) * scale_h, 'w_up': jax.random.normal(ks[3], (E, I, H), dtype=jnp.float32) * scale_h, 'w_down': jax.random.normal(ks[4], (E, H, I), dtype=jnp.float32) * scale_i}
    _L0_ffn_all = _L0_ffn_setup()
    _L0_ffn_in = {k: v for k, v in _L0_ffn_all.items() if k in ('gate_w', 'w_gate', 'w_up', 'w_down')}
    del _L0_ffn_all

    def _L1_xattn_setup():
        import jax, jax.numpy as jnp
        import numpy as np
        EMBED = 128
        HEADS = 16
        HEAD_DIM = EMBED // HEADS
        NEG = -1e+20
        key = jax.random.key(seed)
        k1, k2, k3, k4, k5, k6 = jax.random.split(key, 6)
        N, S = (2, 256)
        values = jax.random.normal(k1, (N, S, EMBED), dtype=jnp.float32)
        keys = jax.random.normal(k2, (N, S, EMBED), dtype=jnp.float32)
        query = jax.random.normal(k3, (N, S, EMBED), dtype=jnp.float32)
        mask = jax.random.randint(k4, (N, 1, S, S), 0, 2, dtype=jnp.int32)
        W_fc = jax.random.normal(k5, (EMBED, EMBED), dtype=jnp.float32) * (1.0 / np.sqrt(EMBED))
        b_fc = jax.random.normal(k6, (EMBED,), dtype=jnp.float32) * 0.01
        return {'values': values, 'keys': keys, 'query': query, 'mask': mask, 'W_fc': W_fc, 'b_fc': b_fc}
    _L1_xattn_all = _L1_xattn_setup()
    _L1_xattn_in = {k: v for k, v in _L1_xattn_all.items() if k in ('W_fc', 'b_fc')}
    del _L1_xattn_all

    def _L1_ffn_setup():
        import jax, jax.numpy as jnp
        import numpy as np
        D_MODEL = 128
        D_HIDDEN = 512
        NUM_EXPERTS = 8
        B, T = (2, 256)
        key = jax.random.key(seed)
        ks = jax.random.split(key, 8)
        s = 0.02
        x = jax.random.normal(ks[0], (B, T, D_MODEL), dtype=jnp.float32)
        Wg = jax.random.normal(ks[1], (D_MODEL, NUM_EXPERTS), dtype=jnp.float32) * s
        bg = jnp.zeros((NUM_EXPERTS,), dtype=jnp.float32)
        W1 = jax.random.normal(ks[2], (NUM_EXPERTS, D_MODEL, D_HIDDEN), dtype=jnp.float32) * s
        b1 = jnp.zeros((NUM_EXPERTS, D_HIDDEN), dtype=jnp.float32)
        W2 = jax.random.normal(ks[3], (NUM_EXPERTS, D_HIDDEN, D_MODEL), dtype=jnp.float32) * s
        b2 = jnp.zeros((NUM_EXPERTS, D_MODEL), dtype=jnp.float32)
        return {'x': x, 'Wg': Wg, 'bg': bg, 'W1': W1, 'b1': b1, 'W2': W2, 'b2': b2}
    _L1_ffn_all = _L1_ffn_setup()
    _L1_ffn_in = {k: v for k, v in _L1_ffn_all.items() if k in ('Wg', 'bg', 'W1', 'b1', 'W2', 'b2')}
    del _L1_ffn_all

    def _L2_xattn_setup():
        import jax, jax.numpy as jnp
        import numpy as np
        FEATURE_DIM = 128
        HEAD_NUM = 16
        HIDDEN_DIM = FEATURE_DIM // HEAD_NUM
        key = jax.random.key(seed)
        ks = jax.random.split(key, 12)
        B, S, D = (4, 256, FEATURE_DIM)
        s = 1.0 / np.sqrt(D)
        inp = {'query': jax.random.normal(ks[0], (B, S, D), jnp.float32), 'key': jax.random.normal(ks[1], (B, S, D), jnp.float32), 'value': jax.random.normal(ks[2], (B, S, D), jnp.float32), 'mask': jax.random.randint(ks[3], (B, 1, 1, S), 0, 2, jnp.int32), 'Wq': jax.random.normal(ks[4], (D, D), jnp.float32) * s, 'bq': jnp.zeros((D,), jnp.float32), 'Wk': jax.random.normal(ks[5], (D, D), jnp.float32) * s, 'bk': jnp.zeros((D,), jnp.float32), 'Wv': jax.random.normal(ks[6], (D, D), jnp.float32) * s, 'bv': jnp.zeros((D,), jnp.float32), 'Wo': jax.random.normal(ks[7], (D, D), jnp.float32) * s, 'bo': jnp.zeros((D,), jnp.float32)}
        return inp
    _L2_xattn_all = _L2_xattn_setup()
    _L2_xattn_in = {k: v for k, v in _L2_xattn_all.items() if k in ('Wq', 'bq', 'Wk', 'bk', 'Wv', 'bv', 'Wo', 'bo')}
    del _L2_xattn_all

    def _L2_ffn_setup():
        import jax, jax.numpy as jnp
        import numpy as np
        MICRO_BATCHES = 2
        TOP_K = 2
        NUM_EXPERTS = 8
        B, S, D = (4, 512, 128)
        H = 4 * D
        key = jax.random.key(seed)
        ks = jax.random.split(key, 8)
        s = 0.02
        return {'x': jax.random.normal(ks[0], (B, S, D), jnp.float32), 'ln_scale': jnp.ones((D,), jnp.float32), 'ln_bias': jnp.zeros((D,), jnp.float32), 'attn_w': jax.random.normal(ks[1], (D, D), jnp.float32) * s, 'attn_b': jnp.zeros((D,), jnp.float32), 'gate_w': jax.random.normal(ks[2], (NUM_EXPERTS, D), jnp.float32) * s, 'w1': jax.random.normal(ks[3], (NUM_EXPERTS, D, H), jnp.float32) * s, 'b1': jnp.zeros((NUM_EXPERTS, H), jnp.float32), 'w2': jax.random.normal(ks[4], (NUM_EXPERTS, H, D), jnp.float32) * s, 'b2': jnp.zeros((NUM_EXPERTS, D), jnp.float32), 'next_w': jax.random.normal(ks[5], (D, D), jnp.float32) * s, 'next_b': jnp.zeros((D,), jnp.float32)}
    _L2_ffn_all = _L2_ffn_setup()
    _L2_ffn_in = {k: v for k, v in _L2_ffn_all.items() if k in ('ln_scale', 'ln_bias', 'attn_w', 'attn_b', 'gate_w', 'w1', 'b1', 'w2', 'b2', 'next_w', 'next_b')}
    del _L2_ffn_all

    def _L3_xattn_setup():
        import jax, jax.numpy as jnp
        import numpy as np
        D_MODEL = 128
        N_HEADS = 16
        D_K = D_MODEL // N_HEADS
        NEG_INF = -1000000000.0

        def _split_heads(x):
            B, S, _ = x.shape
            return x.reshape(B, S, N_HEADS, D_K).transpose(0, 2, 1, 3)
        key = jax.random.key(seed)
        ks = jax.random.split(key, 12)
        B, S = (2, 256)
        inp = {'q': jax.random.normal(ks[0], (B, S, D_MODEL), dtype=jnp.float32), 'k': jax.random.normal(ks[1], (B, S, D_MODEL), dtype=jnp.float32), 'v': jax.random.normal(ks[2], (B, S, D_MODEL), dtype=jnp.float32), 'mask': jax.random.randint(ks[3], (B, 1, S, S), 0, 2, dtype=jnp.int32), 'Wq': jax.random.normal(ks[4], (D_MODEL, D_MODEL), dtype=jnp.float32) / np.sqrt(D_MODEL), 'bq': jnp.zeros((D_MODEL,), dtype=jnp.float32), 'Wk': jax.random.normal(ks[5], (D_MODEL, D_MODEL), dtype=jnp.float32) / np.sqrt(D_MODEL), 'bk': jnp.zeros((D_MODEL,), dtype=jnp.float32), 'Wv': jax.random.normal(ks[6], (D_MODEL, D_MODEL), dtype=jnp.float32) / np.sqrt(D_MODEL), 'bv': jnp.zeros((D_MODEL,), dtype=jnp.float32), 'Wo': jax.random.normal(ks[7], (D_MODEL, D_MODEL), dtype=jnp.float32) / np.sqrt(D_MODEL), 'bo': jnp.zeros((D_MODEL,), dtype=jnp.float32)}
        return inp
    _L3_xattn_all = _L3_xattn_setup()
    _L3_xattn_in = {k: v for k, v in _L3_xattn_all.items() if k in ('Wq', 'bq', 'Wk', 'bk', 'Wv', 'bv', 'Wo', 'bo')}
    del _L3_xattn_all

    def _L3_ffn_setup():
        import jax, jax.numpy as jnp
        import numpy as np
        HIDDEN = 128
        NUM_EXPERTS = 8
        TOP_K = 2
        B, S = (4, 128)
        key = jax.random.key(seed)
        ks = jax.random.split(key, 8)
        H, E = (HIDDEN, NUM_EXPERTS)
        sc = lambda fan_in: 1.0 / np.sqrt(fan_in)
        x = jax.random.normal(ks[0], (B, S, H), dtype=jnp.float32)
        Wr = jax.random.uniform(ks[1], (H, E), minval=-sc(H), maxval=sc(H), dtype=jnp.float32)
        br = jax.random.uniform(ks[2], (E,), minval=-sc(H), maxval=sc(H), dtype=jnp.float32)
        W1 = jax.random.uniform(ks[3], (E, H, 2 * H), minval=-sc(H), maxval=sc(H), dtype=jnp.float32)
        b1 = jax.random.uniform(ks[4], (E, 2 * H), minval=-sc(H), maxval=sc(H), dtype=jnp.float32)
        W2 = jax.random.uniform(ks[5], (E, 2 * H, H), minval=-sc(2 * H), maxval=sc(2 * H), dtype=jnp.float32)
        b2 = jax.random.uniform(ks[6], (E, H), minval=-sc(2 * H), maxval=sc(2 * H), dtype=jnp.float32)
        return {'x': x, 'Wr': Wr, 'br': br, 'W1': W1, 'b1': b1, 'W2': W2, 'b2': b2}
    _L3_ffn_all = _L3_ffn_setup()
    _L3_ffn_in = {k: v for k, v in _L3_ffn_all.items() if k in ('Wr', 'br', 'W1', 'b1', 'W2', 'b2')}
    del _L3_ffn_all
    return {'x': x, 'ctx_1024': ctx_1024, 'mask_BxS2_bf1': mask_BxS2_bf1, 'mask_Bx1xSxS2_ik1': mask_Bx1xSxS2_ik1, 'mask_Bx1x1xS2_ik0': mask_Bx1x1xS2_ik0, 'L0_xattn_Wq': _L0_xattn_in['Wq'], 'L0_xattn_Wk': _L0_xattn_in['Wk'], 'L0_xattn_Wv': _L0_xattn_in['Wv'], 'L0_xattn_Wo': _L0_xattn_in['Wo'], 'L0_xattn_rel_pos_bias': _L0_xattn_in['rel_pos_bias'], 'L0_ffn_gate_w': _L0_ffn_in['gate_w'], 'L0_ffn_w_gate': _L0_ffn_in['w_gate'], 'L0_ffn_w_up': _L0_ffn_in['w_up'], 'L0_ffn_w_down': _L0_ffn_in['w_down'], 'L1_xattn_W_fc': _L1_xattn_in['W_fc'], 'L1_xattn_b_fc': _L1_xattn_in['b_fc'], 'L1_ffn_Wg': _L1_ffn_in['Wg'], 'L1_ffn_bg': _L1_ffn_in['bg'], 'L1_ffn_W1': _L1_ffn_in['W1'], 'L1_ffn_b1': _L1_ffn_in['b1'], 'L1_ffn_W2': _L1_ffn_in['W2'], 'L1_ffn_b2': _L1_ffn_in['b2'], 'L2_xattn_Wq': _L2_xattn_in['Wq'], 'L2_xattn_bq': _L2_xattn_in['bq'], 'L2_xattn_Wk': _L2_xattn_in['Wk'], 'L2_xattn_bk': _L2_xattn_in['bk'], 'L2_xattn_Wv': _L2_xattn_in['Wv'], 'L2_xattn_bv': _L2_xattn_in['bv'], 'L2_xattn_Wo': _L2_xattn_in['Wo'], 'L2_xattn_bo': _L2_xattn_in['bo'], 'L2_ffn_ln_scale': _L2_ffn_in['ln_scale'], 'L2_ffn_ln_bias': _L2_ffn_in['ln_bias'], 'L2_ffn_attn_w': _L2_ffn_in['attn_w'], 'L2_ffn_attn_b': _L2_ffn_in['attn_b'], 'L2_ffn_gate_w': _L2_ffn_in['gate_w'], 'L2_ffn_w1': _L2_ffn_in['w1'], 'L2_ffn_b1': _L2_ffn_in['b1'], 'L2_ffn_w2': _L2_ffn_in['w2'], 'L2_ffn_b2': _L2_ffn_in['b2'], 'L2_ffn_next_w': _L2_ffn_in['next_w'], 'L2_ffn_next_b': _L2_ffn_in['next_b'], 'L3_xattn_Wq': _L3_xattn_in['Wq'], 'L3_xattn_bq': _L3_xattn_in['bq'], 'L3_xattn_Wk': _L3_xattn_in['Wk'], 'L3_xattn_bk': _L3_xattn_in['bk'], 'L3_xattn_Wv': _L3_xattn_in['Wv'], 'L3_xattn_bv': _L3_xattn_in['bv'], 'L3_xattn_Wo': _L3_xattn_in['Wo'], 'L3_xattn_bo': _L3_xattn_in['bo'], 'L3_ffn_Wr': _L3_ffn_in['Wr'], 'L3_ffn_br': _L3_ffn_in['br'], 'L3_ffn_W1': _L3_ffn_in['W1'], 'L3_ffn_b1': _L3_ffn_in['b1'], 'L3_ffn_W2': _L3_ffn_in['W2'], 'L3_ffn_b2': _L3_ffn_in['b2']}

def reference(x, ctx_1024, mask_BxS2_bf1, mask_Bx1xSxS2_ik1, mask_Bx1x1xS2_ik0, L0_xattn_Wq, L0_xattn_Wk, L0_xattn_Wv, L0_xattn_Wo, L0_xattn_rel_pos_bias, L0_ffn_gate_w, L0_ffn_w_gate, L0_ffn_w_up, L0_ffn_w_down, L1_xattn_W_fc, L1_xattn_b_fc, L1_ffn_Wg, L1_ffn_bg, L1_ffn_W1, L1_ffn_b1, L1_ffn_W2, L1_ffn_b2, L2_xattn_Wq, L2_xattn_bq, L2_xattn_Wk, L2_xattn_bk, L2_xattn_Wv, L2_xattn_bv, L2_xattn_Wo, L2_xattn_bo, L2_ffn_ln_scale, L2_ffn_ln_bias, L2_ffn_attn_w, L2_ffn_attn_b, L2_ffn_gate_w, L2_ffn_w1, L2_ffn_b1, L2_ffn_w2, L2_ffn_b2, L2_ffn_next_w, L2_ffn_next_b, L3_xattn_Wq, L3_xattn_bq, L3_xattn_Wk, L3_xattn_bk, L3_xattn_Wv, L3_xattn_bv, L3_xattn_Wo, L3_xattn_bo, L3_ffn_Wr, L3_ffn_br, L3_ffn_W1, L3_ffn_b1, L3_ffn_W2, L3_ffn_b2):
    import jax
    import jax.numpy as jnp

    def _L0_xattn_ref(q, kv, Wq, Wk, Wv, Wo, rel_pos_bias, mask):
        import jax, jax.numpy as jnp
        import numpy as np
        B, M, N = (2, 128, 256)
        D_MODEL = 128
        H, HKV, D = (16, 4, 64)
        GROUPS = H // HKV
        THETA = 10000.0
        MAX_REL = M + N

        def _freqs_cis(dim, seq_len, theta):
            inv = 1.0 / theta ** (jnp.arange(0, dim, 2, dtype=jnp.float32) / dim)
            f = jnp.outer(jnp.arange(seq_len, dtype=jnp.float32), inv)
            f = jnp.repeat(f, 2, axis=-1)
            return (jnp.cos(f), jnp.sin(f))

        def _apply_rope(x, cos, sin):
            cos = cos[None, None]
            sin = sin[None, None]
            d = x.shape[-1]
            x1, x2 = (x[..., :d // 2], x[..., d // 2:])
            c1, c2 = (cos[..., :d // 2], cos[..., d // 2:])
            s1, s2 = (sin[..., :d // 2], sin[..., d // 2:])
            return jnp.concatenate([x1 * c1 - x2 * s1, x1 * s2 + x2 * c2], axis=-1)
        Bq, Mq, _ = q.shape
        Nk = kv.shape[1]
        Q = (q @ Wq).reshape(Bq, Mq, H, D).transpose(0, 2, 1, 3)
        K = (kv @ Wk).reshape(Bq, Nk, HKV, D).transpose(0, 2, 1, 3)
        V = (kv @ Wv).reshape(Bq, Nk, HKV, D).transpose(0, 2, 1, 3)
        cos_q, sin_q = _freqs_cis(D, Mq, THETA)
        cos_k, sin_k = _freqs_cis(D, Nk, THETA)
        Q = _apply_rope(Q, cos_q, sin_q)
        K = _apply_rope(K, cos_k, sin_k)
        K = jnp.repeat(K, GROUPS, axis=1)
        V = jnp.repeat(V, GROUPS, axis=1)
        scale = D ** (-0.5)
        scores = jnp.einsum('bhqd,bhkd->bhqk', Q, K) * scale
        rel = jnp.abs(jnp.arange(Mq)[:, None] - jnp.arange(Nk)[None, :])
        rel = jnp.clip(rel, 0, MAX_REL - 1)
        scores = scores + rel_pos_bias[:, rel][None]
        m = mask[:, None, None, :]
        scores = jnp.where(m, scores, -1000000000.0)
        attn = jax.nn.softmax(scores, axis=-1)
        out = jnp.einsum('bhqk,bhkd->bhqd', attn, V)
        out = out.transpose(0, 2, 1, 3).reshape(Bq, Mq, H * D)
        return out @ Wo

    def _L0_ffn_ref(hidden_states, gate_w, w_gate, w_up, w_down):
        import jax, jax.numpy as jnp
        import numpy as np
        B, S, H, I, E = (2, 512, 128, 64, 8)
        b, s, h = hidden_states.shape
        x = hidden_states.reshape(-1, h)
        logits = x @ gate_w.T
        top_v = jnp.max(logits, axis=-1)
        sel = jnp.argmax(logits, axis=-1)
        rw = jax.nn.sigmoid(top_v)
        out = jnp.zeros_like(x)
        n_exp = gate_w.shape[0]
        for e in range(n_exp):
            mask = (sel == e).astype(x.dtype)
            xs = x * (rw * mask)[:, None]
            g = xs @ w_gate[e].T
            u = xs @ w_up[e].T
            out = out + u * jax.nn.silu(g) @ w_down[e].T
        return out.reshape(b, s, h)

    def _L1_xattn_ref(values, keys, query, mask, W_fc, b_fc):
        import jax, jax.numpy as jnp
        import numpy as np
        EMBED = 128
        HEADS = 16
        HEAD_DIM = EMBED // HEADS
        NEG = -1e+20
        N, Q, E = query.shape
        K = keys.shape[1]
        H, D = (HEADS, HEAD_DIM)
        v = values.reshape(N, K, H, D)
        k = keys.reshape(N, K, H, D)
        q = query.reshape(N, Q, H, D)
        energy = jnp.einsum('nqhd,nkhd->nhqk', q, k)
        energy = jnp.where(mask == 0, NEG, energy)
        attn = jax.nn.softmax(energy / jnp.sqrt(jnp.float32(E)), axis=3)
        out = jnp.einsum('nhqk,nkhd->nqhd', attn, v).reshape(N, Q, H * D)
        return out @ W_fc.T + b_fc

    def _L1_ffn_ref(x, Wg, bg, W1, b1, W2, b2):
        import jax, jax.numpy as jnp
        import numpy as np
        D_MODEL = 128
        D_HIDDEN = 512
        NUM_EXPERTS = 8
        B, T = (2, 256)
        gate_logits = jnp.einsum('btd,de->bte', x, Wg) + bg
        gate_scores = jax.nn.softmax(gate_logits, axis=-1)
        top1_idx = jnp.argmax(gate_scores, axis=-1)
        top1_mask = jax.nn.one_hot(top1_idx, NUM_EXPERTS, dtype=x.dtype)
        top1_weight = jnp.sum(gate_scores * top1_mask, axis=-1, keepdims=True)
        h = jax.nn.silu(jnp.einsum('btd,edh->bteh', x, W1) + b1)
        o = jnp.einsum('bteh,ehd->bted', h, W2) + b2
        y = jnp.sum(o * top1_mask[..., None], axis=2) * top1_weight
        return y

    def _L2_xattn_ref(query, key, value, mask, Wq, bq, Wk, bk, Wv, bv, Wo, bo):
        import jax, jax.numpy as jnp
        import numpy as np
        FEATURE_DIM = 128
        HEAD_NUM = 16
        HIDDEN_DIM = FEATURE_DIM // HEAD_NUM
        B, Sq, D = query.shape
        H, Hd = (HEAD_NUM, HIDDEN_DIM)
        scale = jnp.sqrt(jnp.asarray(Hd, query.dtype))

        def split_heads(x):
            b, s, _ = x.shape
            return x.reshape(b, s, H, Hd).transpose(0, 2, 1, 3)
        Q = split_heads(query @ Wq.T + bq)
        K = split_heads(key @ Wk.T + bk)
        V = split_heads(value @ Wv.T + bv)
        scores = jnp.einsum('bhqd,bhkd->bhqk', Q, K) / scale
        scores = jnp.where(mask == 0, jnp.asarray(-10000000000.0, scores.dtype), scores)
        attn = jax.nn.softmax(scores, axis=-1)
        h = jnp.einsum('bhqk,bhkd->bhqd', attn, V)
        h = h.transpose(0, 2, 1, 3).reshape(B, Sq, D)
        return h @ Wo.T + bo

    def _L2_ffn_ref(x, ln_scale, ln_bias, attn_w, attn_b, gate_w, w1, b1, w2, b2, next_w, next_b):
        import jax, jax.numpy as jnp
        import numpy as np
        MICRO_BATCHES = 2
        TOP_K = 2
        NUM_EXPERTS = 8
        B, S, D = (4, 512, 128)
        H = 4 * D
        b, s, d = x.shape
        flat = x.reshape(b * s, d)
        mu = jnp.mean(flat, axis=-1, keepdims=True)
        var = jnp.mean((flat - mu) ** 2, axis=-1, keepdims=True)
        xn = (flat - mu) * jax.lax.rsqrt(var + 1e-05) * ln_scale + ln_bias
        x_attn = xn @ attn_w.T + attn_b + flat
        logits = x_attn @ gate_w.T
        _vals, _idx = jax.lax.top_k(logits, TOP_K)
        e = w1.shape[0]
        n = b * s // (MICRO_BATCHES * e)
        xe = x_attn.reshape(MICRO_BATCHES, e, n, d)
        h = jax.nn.gelu(jnp.einsum('mend,edh->menh', xe, w1) + b1[None, :, None, :], approximate=False)
        eo = jnp.einsum('menh,ehd->mend', h, w2) + b2[None, :, None, :]
        eo = eo.reshape(b * s, d)
        out = jax.nn.gelu(eo @ next_w.T + next_b, approximate=False)
        return out.reshape(b, s, d)

    def _L3_xattn_ref(q, k, v, mask, Wq, bq, Wk, bk, Wv, bv, Wo, bo):
        import jax, jax.numpy as jnp
        import numpy as np
        D_MODEL = 128
        N_HEADS = 16
        D_K = D_MODEL // N_HEADS
        NEG_INF = -1000000000.0

        def _split_heads(x):
            B, S, _ = x.shape
            return x.reshape(B, S, N_HEADS, D_K).transpose(0, 2, 1, 3)
        query = _split_heads(q @ Wq + bq)
        key_ = _split_heads(k @ Wk + bk)
        value = _split_heads(v @ Wv + bv)
        scale = 1.0 / np.sqrt(D_K).astype(np.float32)
        scores = jnp.einsum('bhqd,bhkd->bhqk', query, key_) * scale
        scores = jnp.where(mask == 0, NEG_INF, scores)
        attn = jax.nn.softmax(scores, axis=-1)
        ctx = jnp.einsum('bhqk,bhkd->bhqd', attn, value)
        B, H, S, Dk = ctx.shape
        ctx = ctx.transpose(0, 2, 1, 3).reshape(B, S, H * Dk)
        return ctx @ Wo + bo

    def _L3_ffn_ref(x, Wr, br, W1, b1, W2, b2):
        import jax, jax.numpy as jnp
        import numpy as np
        HIDDEN = 128
        NUM_EXPERTS = 8
        TOP_K = 2
        B, S = (4, 128)
        B_, S_, H = x.shape
        xf = x.reshape(-1, H)
        logits = xf @ Wr + br
        topk_w, topk_idx = jax.lax.top_k(logits, TOP_K)
        topk_w = jax.nn.softmax(topk_w, axis=-1)
        gate = jnp.sum(jax.nn.one_hot(topk_idx, NUM_EXPERTS, dtype=xf.dtype) * topk_w[..., None], axis=1)
        h = jax.nn.relu(jnp.einsum('th,ehf->etf', xf, W1) + b1[:, None, :])
        y = jnp.einsum('etf,efh->eth', h, W2) + b2[:, None, :]
        out = jnp.einsum('te,eth->th', gate, y)
        return out.reshape(B_, S_, H)
    x = x + _L0_xattn_ref(_layernorm(x, axis=-1), ctx_1024, L0_xattn_Wq, L0_xattn_Wk, L0_xattn_Wv, L0_xattn_Wo, L0_xattn_rel_pos_bias, mask_BxS2_bf1)
    x = x + _L0_ffn_ref(_layernorm(x, axis=-1), L0_ffn_gate_w, L0_ffn_w_gate, L0_ffn_w_up, L0_ffn_w_down)
    x = x + _L1_xattn_ref(ctx_1024, ctx_1024, _layernorm(x, axis=-1), mask_Bx1xSxS2_ik1, L1_xattn_W_fc, L1_xattn_b_fc)
    x = x + _L1_ffn_ref(_layernorm(x, axis=-1), L1_ffn_Wg, L1_ffn_bg, L1_ffn_W1, L1_ffn_b1, L1_ffn_W2, L1_ffn_b2)
    x = x + _L2_xattn_ref(_layernorm(x, axis=-1), ctx_1024, ctx_1024, mask_Bx1x1xS2_ik0, L2_xattn_Wq, L2_xattn_bq, L2_xattn_Wk, L2_xattn_bk, L2_xattn_Wv, L2_xattn_bv, L2_xattn_Wo, L2_xattn_bo)
    x = x + _L2_ffn_ref(_layernorm(x, axis=-1), L2_ffn_ln_scale, L2_ffn_ln_bias, L2_ffn_attn_w, L2_ffn_attn_b, L2_ffn_gate_w, L2_ffn_w1, L2_ffn_b1, L2_ffn_w2, L2_ffn_b2, L2_ffn_next_w, L2_ffn_next_b)
    x = x + _L3_xattn_ref(_layernorm(x, axis=-1), ctx_1024, ctx_1024, mask_Bx1xSxS2_ik1, L3_xattn_Wq, L3_xattn_bq, L3_xattn_Wk, L3_xattn_bk, L3_xattn_Wv, L3_xattn_bv, L3_xattn_Wo, L3_xattn_bo)
    x = x + _L3_ffn_ref(_layernorm(x, axis=-1), L3_ffn_Wr, L3_ffn_br, L3_ffn_W1, L3_ffn_b1, L3_ffn_W2, L3_ffn_b2)
    return x

_drawn_inputs = setup_inputs


def setup_inputs(seed=0):
    import zlib

    import numpy as np

    out = dict(_drawn_inputs(seed))
    spreads = {'L0_xattn_rel_pos_bias': (0.0, 0.1),
     'L1_ffn_bg': (0.0, 0.626),
     'L1_ffn_b1': (0.0, 0.8),
     'L1_ffn_b2': (0.0, 0.432),
     'L2_xattn_bq': (0.0, 0.322),
     'L2_xattn_bk': (0.0, 2.0),
     'L2_xattn_bv': (0.0, 0.1),
     'L2_xattn_bo': (0.0, 0.1),
     'L2_ffn_ln_scale': (1.0, 0.6),
     'L2_ffn_ln_bias': (0.0, 0.8),
     'L2_ffn_attn_b': (0.0, 0.8),
     'L2_ffn_b1': (0.0, 0.8),
     'L2_ffn_b2': (0.0, 0.594),
     'L2_ffn_next_b': (0.0, 0.8),
     'L3_xattn_bq': (0.0, 2.0),
     'L3_xattn_bk': (0.0, 2.0),
     'L3_xattn_bv': (0.0, 0.759),
     'L3_xattn_bo': (0.0, 0.734)}
    factors = {'L1_xattn_b_fc': 4.362,
     'L1_ffn_Wg': 3.287,
     'L1_ffn_W1': 5.508,
     'L1_ffn_W2': 4.996,
     'L2_ffn_attn_w': 8.0,
     'L2_ffn_w1': 8.0,
     'L2_ffn_w2': 7.104,
     'L2_ffn_next_w': 4.234,
     'L3_ffn_b1': 39.108,
     'L3_ffn_b2': 20.214,
     'L3_ffn_Wr': 2.947,
     'L3_ffn_br': 8.0,
     'L3_ffn_W1': 3.616,
     'L3_ffn_W2': 2.822}
    for name, (base, spread) in spreads.items():
        noise = np.random.default_rng([zlib.crc32(name.encode()), seed]).standard_normal(out[name].shape)
        drawn = base * np.exp(spread * noise) if base else spread * noise
        out[name] = jnp.asarray(drawn.astype(out[name].dtype))
    for name, factor in factors.items():
        out[name] = (out[name] * factor).astype(out[name].dtype)
    return out
```

```python
from contextlib import ExitStack

import numpy as np
import concourse.bass as bass
from concourse import mybir

F32 = mybir.dt.float32
I32 = mybir.dt.int32
U32 = mybir.dt.uint32
U8 = mybir.dt.uint8
ALU = mybir.AluOpType
ACT = mybir.ActivationFunctionType
X_AXIS = mybir.AxisListType.X

P = 128
B, SQ, D = 4, 256, 128
SK = 64
T = B * SQ // P
TPB = SQ // P
H = 16
D0, KV0 = 64, 4
DH = D // H
NPAIR = H // 2
E = 8
I0 = 64
HID = {3: 512, 5: 512, 7: 256}
EPS = 1e-5
FILL = -float(2.0 ** 100)
RSQRT_SEED = float(0x5F3759DF)
VX = D + H

ATT, FFN = (0, 2, 4, 6), (1, 3, 5, 7)
START = {0: 0, 1: 8, 2: 16, 3: 24, 4: 32, 5: 40, 6: 54, 7: 62}


def make_schedule():
    out = []

    def put(p, slot, place, stage, index):
        out.append((START[p] + slot, place, len(out), stage, p, index))

    for p in range(8):
        for t in range(T):
            odd = t % TPB == TPB - 1
            b = t // TPB
            if p == 0:
                for place, lead, stage in ((0, 0, "probsT"), (1, -3, "query0"), (2, -2, "queryT"), (3, 0, "values"),
                                           (3.5, -1, "exp"), (4, 1, "outT"), (5, -2, "scores"), (6, -4, "xT"),
                                           (7, 1, "project")):
                    put(p, t + lead, place, stage, t)
                if odd:
                    put(p, t + 1, 8, "norm", b)
            elif p in ATT:
                for place, lead, stage in ((0, 0, "probsT"), (1, 1, "outT"), (2, -3, "xT"), (3, -2, "scores"),
                                           (3.5, -1, "exp"), (4, 0, "values"), (6, 1, "project")):
                    put(p, t + lead, place, stage, t)
                if p != 2:
                    put(p, t - 3, 5, "query", t)
                if not odd:
                    put(p, t - 4, -1, "keys", b)
                    put(p, t - 2, 4.6, "context", b)
                if odd:
                    put(p, t + 1, 7, "norm", b)
            elif p == 1:
                for place, lead, stage in ((2, -3, "xT"), (1, -2, "logits"), (3, -1, "hidden0"), (3.5, -1, "tanh"),
                                           (1.5, 0, "gated"), (0, 1, "gatedT"), (4.5, 1, "down0")):
                    put(p, t + lead, place, stage, t)
                if odd:
                    put(p, t + 1, 7, "norm", b)
            elif p in (3, 7):
                for place, lead, stage in ((2, -3, "xT"), (1.2, -2, "logits"), (0.5, -1, "gateT"), (2.5, -1, "bias2")):
                    put(p, t + lead, place, stage, t)
                if odd:
                    for e in range(E):
                        put(p, t, 0.6, "hidden", (b, e))
                        if e:
                            put(p, t, 0.6, "expert", (b, e - 1))
                    put(p, t, 0.6, "expert", (b, E - 1))
                    if p == 3:
                        put(p, t, 0.7, "norm", b)
            else:
                put(p, t - 3, 2, "xT", t)
                if odd:
                    put(p, t - 3, 2.5, "mix", b)
                put(p, 9 + t, 2.5, "back", t)
                if odd:
                    put(p, 9 + t, 2.6, "norm", b)
        if p == 5:
            for e in range(E):
                put(p, 8, 0, "hidden5", e)
                if e:
                    put(p, 8, 0, "expert5", e - 1)
            put(p, 8, 0, "expert5", E - 1)
            for m in range(2):
                put(p, 8, 1, "next5", m)
    for b, slot in ((2, -2), (3, 0)):
        out.append((slot, 8, len(out), "norm", -1, b))
    first = [("keys0", 0, g) for g in range(KV0)] + [("values0", 0, b) for b in range(B)]
    return [("norm", -1, b) for b in range(TPB)] + first + \
        [x[3:] for x in sorted(out)]


SCHEDULE = make_schedule()

JOBS = {
    "keys0": [("S", "keys0", "dve")], "values0": [("M", "values0", "act")],
    "xT": [("T", "xT", "act")], "query0": [("S", "query0", "dve")],
    "queryT": [("T", "queryT0", "act"), ("T", "queryT1", "act")], "query": [("M", "query", "act")],
    "scores": [("S", "scores", "dve")], "probsT": [("T", "probsT0", "act"), ("T", "probsT1", "act")],
    "project": [("M", "project", "dve")], "logits": [("M", "logits", "dve")],
    "hidden0": [("S", "hidden0", "dve")], "gatedT": [("T", "gatedT", "act")], "down0": [("M", "down0", "dve")],
    "gateT": [("T", "gateT", "act")], "bias2": [("M", "bias2", "dve")],
    "hidden": [("S", "hidden", "act")], "expert": [("M", "expert", "dve")],
    "mix": [("M", "mix", "act")], "hidden5": [("S", "hidden5", "act")], "expert5": [("M", "expert5", "act")],
    "next5": [("S", "next5", "act")], "back": [("T", "back", "dve")],
}


def jobs_of(stage, p, i):
    if stage == "values":
        return [("S" if p == 0 else "M", "values", "dve")]
    if stage == "outT":
        return [("T", "outT0", "act"), ("T", "outT1", "act")] if p == 0 else [("T", "outT0", "act")]
    if stage == "keys":
        return [("M", "keys", "act")] if p in (4, 6) and i == 0 else []
    if stage == "context":
        return [("M", "ctxv", "act")] if p in (4, 6) else []
    return JOBS.get(stage, [])


class Ring:

    def __init__(self, name, slots, filled, emptied):
        self.slots, self.filled, self.emptied = slots, filled, emptied
        self.number, self.turn = {}, []
        for stage, p, i in SCHEDULE:
            for ring, job, reader in jobs_of(stage, p, i):
                if ring == name:
                    self.number[job, p, i] = len(self.turn)
                    self.turn.append((reader, 1 + sum(r == reader for r, _ in self.turn)))

    def slot(self, *job):
        return self.slots[self.number[job] % len(self.slots)]

    def full(self, *job):
        return self.filled, self.number[job] + 1

    def read(self, *job):
        reader, n = self.turn[self.number[job]]
        return self.emptied[reader], n

    def reused(self, *job):
        return self.number[job] >= len(self.slots)

    def vacated(self, *job):
        reader, n = self.turn[self.number[job] - len(self.slots)]
        return self.emptied[reader], n


class Mark:

    def __init__(self, sem, keys):
        self.sem, self.nth = sem, {k: n + 1 for n, k in enumerate(keys)}

    def at(self, *key):
        return self.sem, self.nth[key]


COLS = {"bq4": 0, "bk4": 1, "bq6": 2, "bk6": 3, "ln_scale": 4, "ln_bias": 5, "attn_b": 6, "next_b": 7,
        "b1_3": 8, "b1_5": 40, "b2_5": 72, "b1_7": 80}
NCOLS = 96
MATS = ["w2", "q4", "k4", "v4", "w4", "attn", "next", "q6", "k6", "v6", "w6", "gate1", "gate3", "gate7"]
ROWS = ["b2", "v4", "b4", "v6", "b6"]
CONSTS = {"ident": (0, 128), "row0": (128, 128), "heads": (256, 16), "iota": (272, 8), "cosq": (280, 128),
          "sinq": (408, 128), "cosk": (536, 64), "sink": (600, 64)}
NCONST = 664


def build(nc, x, ctxT, ctx2, consts, cols, mats, rows, bias2, gbias, relpos, mask0, mask1, mask2,
          wq0, wk0, wk0r, wv0, wo0, wg0, wu0, wd0, w1_3, w2_3, w1_5, w2_5, w1_7, w2_7, out):
    with ExitStack() as ctx:
        def sb(name, shape, dt=F32):
            return ctx.enter_context(nc.sbuf_tensor(name, [P] + shape, dt))

        def sem(name):
            return ctx.enter_context(nc.semaphore(name))

        X = sb("X", [T, D])
        CST = sb("CST", [NCONST])
        COL = sb("COL", [NCOLS])
        MAT = sb("MAT", [len(MATS), P])
        ROW = sb("ROW", [len(ROWS), P])
        BIAS2 = sb("BIAS2", [2, P])
        GB = sb("GB", [2, E])
        CTXT = sb("CTXT", [B, 2, SK])
        CTX2 = sb("CTX2", [B, D])
        M0 = sb("M0", [B, SK], U8)
        M1 = sb("M1", [T, SK], I32)
        M2 = sb("M2", [B, SK], I32)
        FILL0 = sb("FILL0", [B, SK])
        FILL1, FILL2 = M1[:, :, :].bitcast(F32), M2[:, :, :].bitcast(F32)
        W1_3 = sb("W1_3", [E, HID[3]])
        W2_3 = sb("W2_3", [E, HID[3] // P, D])
        W0 = sb("W0", [4864])
        TAB0 = sb("TAB0", [8192])
        XN = sb("XN", [T, D])
        XT = sb("XT", [T, P])
        QT = sb("QT", [2, P])
        SM = sb("SM", [3, H, SK])
        PT = sb("PT", [2, NPAIR, P])
        KBD = sb("KBD", [2, H, SK])
        VEX = sb("VEX", [2, NPAIR, VX])
        KT = sb("KT", [B, SK])
        WORK = sb("WORK", [8704])
        HALF = sb("HALF", [4, 512])
        AO = sb("AO", [2, D])
        OT = sb("OT", [2, P])
        GATE = sb("GATE", [4, P])
        GT = sb("GT", [2, P])
        ST = sb("ST", [2, 6])
        MV = sb("MV", [2, 2])
        VAR = sb("VAR", [2])
        SHIFT = sb("SHIFT", [2], I32)
        RS = sb("RS", [2])
        SQ2 = sb("SQ2", [2])
        HV = sb("HV", [2])
        MX = sb("MX", [3, H])
        SUM = sb("SUM", [2, H])
        RCP = sb("RCP", [2, H])
        LG = sb("LG", [2, E])
        TOP = sb("TOP", [2, E])
        IDX = sb("IDX", [2, E], U32)
        IDF = sb("IDF", [2, E])
        HOT = sb("HOT", [2, 2, E])
        GV = sb("GV", [2, 8])
        GE = sb("GE", [2, E])
        GE2 = sb("GE2", [2, E])

        def const(name):
            o, n = CONSTS[name]
            return CST[:, o:o + n]

        def col(name, k=0):
            o = COLS[name] + k
            return COL[:, o:o + 1]

        def mat(name):
            return MAT[:, MATS.index(name), :]

        def row(name):
            return ROW[:, ROWS.index(name), :]

        def diagonal(half, r, first, step, n):
            flat = VEX[half, r, :, :].rearrange("p c v -> p (c v)")
            return bass.AP(flat.tensor, flat.offset + first, [list(flat.ap[0]), [VX + step, NPAIR], [1, n]])

        IDENT, ROW0 = const("ident"), const("row0")
        HEADS = const("heads").unsqueeze(2).broadcast_to([P, H, SK])
        COSQ = const("cosq").rearrange("p (j d) -> p j d", j=TPB)
        SINQ = const("sinq").rearrange("p (j d) -> p j d", j=TPB)
        COSK = const("cosk").unsqueeze(1).broadcast_to([P, B, SK])
        SINK = const("sink").unsqueeze(1).broadcast_to([P, B, SK])

        WQ0, WO0 = W0[:, 0:1024], W0[:, 1024:2048].rearrange("p (c n) -> p c n", c=NPAIR)
        WK0 = W0[:, 2048:2560].rearrange("p (g d) -> p g d", g=KV0)
        WK0R = W0[:, 2560:3072].rearrange("p (g d) -> p g d", g=KV0)
        WV0 = W0[:, 3072:3328]
        WG0, WU0 = W0[:, 3328:3840], W0[:, 3840:4352]
        WD0 = W0[:, 4352:4864].rearrange("p (c n) -> p c n", c=4)
        W1_7 = W0[:, 0:2048].rearrange("p (e f) -> p e f", e=E)
        W2_7 = W0[:, 2048:4096].rearrange("p (e c n) -> p e c n", e=E, c=2)
        REL = TAB0[:, 0:2048].rearrange("p (j h k) -> p j h k", j=TPB, h=H)
        RELM = TAB0[:, 2048:4096].rearrange("p (j h k) -> p j h k", j=2, h=H)
        KBD0 = TAB0[:, 4096:6144].rearrange("p (b g k) -> p b g k", b=B, g=KV0)
        VBD0 = TAB0[:, 6144:8192].rearrange("p (b g k) -> p b g k", b=B, g=KV0)
        W1_5 = TAB0[:, 0:4096].rearrange("p (e f) -> p e f", e=E)
        W2_5 = TAB0[:, 4096:8192].rearrange("p (e c n) -> p e c n", e=E, c=4)
        T1, T2 = WORK[:, 0:1024], WORK[:, 1024:2048]
        QR = WORK[:, 2048:4096].rearrange("p (r n) -> p r n", r=2)
        QT0 = WORK[:, 4096:5120].rearrange("p (c q) -> p c q", c=NPAIR)
        AO0 = WORK[:, 5120:7168].rearrange("p (r n) -> p r n", r=2)
        OT0 = WORK[:, 7168:8192].rearrange("p (c q) -> p c q", c=NPAIR)
        K1, K2 = WORK[:, 8192:8448], WORK[:, 8448:8704]
        HT = WORK[:, 0:2048].rearrange("p (r c q) -> p r c q", r=2, c=4)
        XAT = WORK[:, 2048:3072]
        EOT = WORK[:, 3072:4096]
        YT = WORK[:, 4096:5120]
        HT5 = WORK[:, 5120:6144].rearrange("p (r c q) -> p r c q", r=2, c=4)
        XN2 = WORK[:, 6144:7168].rearrange("p (t n) -> p t n", t=T)
        GP, UP = (WORK[:, 8192:8704], W0[:, 2048:2560]), (HALF[:, 0, :], W0[:, 2560:3072])
        TH, AT = (HALF[:, 1, :], HALF[:, 2, :]), HALF[:, 3, :]

        psS = [ctx.enter_context(nc.psum_tensor(f"psS{k}", [P, 1024], F32)) for k in range(2)]
        psT = [ctx.enter_context(nc.psum_tensor(f"psT{k}", [P, 512], F32)) for k in range(2)]
        psM = [ctx.enter_context(nc.psum_tensor(f"psM{k}", [P, 512], F32)) for k in range(2)]
        rings = {}
        for name, slots in (("S", psS), ("T", psT), ("M", psM)):
            rings[name] = Ring(name, slots, sem(f"filled_{name}"),
                               {"act": sem(f"emptied_{name}_by_act"), "dve": sem(f"emptied_{name}_by_dve")})
        S, TR, M = rings["S"], rings["T"], rings["M"]

        def staged(*names):
            return [(p, i) for s, p, i in SCHEDULE if s in names]

        normed = Mark(sem("normed"), [(p + 1, b) for p, b in staged("norm")])
        masked = Mark(sem("masked"), staged("scores"))
        shifted = Mark(sem("shifted"), staged("scores"))
        exped = Mark(sem("exped"), staged("exp"))
        rotated = Mark(sem("rotated"), staged("query0"))
        relmasked = Mark(sem("relmasked"), staged("query0"))
        kbd_ready = Mark(sem("kbd_ready"), staged("keys"))
        vex_ready = Mark(sem("vex_ready"), [(p, b) for p, b in staged("context") if p == 2])
        keys0_ready = Mark(sem("keys0_ready"), staged("keys0"))
        gate_top = Mark(sem("gate_top"), staged("logits"))
        gate_exp = Mark(sem("gate_exp"), staged("logits"))
        gate_ready = Mark(sem("gate_ready"), staged("logits"))
        hid0_ready = Mark(sem("hid0_ready"), staged("hidden0"))
        tanh_ready = Mark(sem("tanh_ready"), staged("tanh"))
        half_ready = Mark(sem("half_ready"), staged("gated"))
        gated_ready = Mark(sem("gated_ready"), staged("gated"))
        zeroed_tables = sem("zeroed_tables")
        zeroed_rows = sem("zeroed_rows")
        zeroed_values = sem("zeroed_values")
        fills = sem("fills")
        stored = sem("stored")
        act_chain = sem("act_chain")
        dve_chain = sem("dve_chain")

        def pv(t):
            return t.rearrange("(a n) -> a n", a=1)

        loads = [
            ("x01", X[:, 0:4, :], x[:, 0:4, :]), ("consts", CST[:, :], consts), ("ctxT", CTXT[:, :, :, :], ctxT),
            ("wk0", WK0, wk0), ("wk0r", WK0R, wk0r), ("wv0", WV0, wv0),
            ("wq0", WQ0, wq0), ("x23", X[:, 4:8, :], x[:, 4:8, :]),
            ("mask0", M0[:, :, :], mask0), ("rel", REL, relpos), ("wo0", WO0, wo0),
            ("cols", COL[:, :], cols), ("mats", MAT[:, :, :], mats),
            ("wg0", WG0, wg0), ("wu0", WU0, wu0), ("wd0", WD0, wd0),
            ("ctx2", CTX2[:, :, :], ctx2), ("mask1", M1[:, :, :], mask1), ("mask2", M2[:, :, :], mask2),
            ("gbias", GB[:, :, :], gbias),
            ("rows", ROW[0:1, :, :], rows), ("bias2", BIAS2[0:E, :, :], bias2),
            ("w1_3", W1_3[:, :, :], w1_3), ("w2_3", W2_3[:, :, :, :], w2_3),
            ("w1_5", W1_5, w1_5), ("w2_5", W2_5, w2_5), ("w1_7", W1_7, w1_7), ("w2_7", W2_7, w2_7)]
        loaded = {name: sem(f"loaded_{name}") for name, _, _ in loads}

        block = ctx.enter_context(nc.Block())

        def cat(t):
            return t % TPB, t // TPB

        @block.sync
        def _(sp):
            for name, dst, src in loads:
                if name == "rows":
                    sp.wait_ge(zeroed_rows, 2)
                if name == "w1_5":
                    sp.wait_ge(*S.full("values", 0, T - 1))
                    sp.wait_ge(*masked.at(0, T - 1))
                    sp.wait_ge(*relmasked.at(0, T - 1))
                if name == "w1_7":
                    sp.wait_ge(*M.full("down0", 1, T - 1))
                sp.dma_start(dst, src).then_inc(loaded[name], 16)
            for b in range(B):
                sp.wait_ge(*M.read("expert", 7, (b, E - 1)))
                sp.dma_start(out[:, TPB * b:TPB * (b + 1), :], X[:, TPB * b:TPB * (b + 1), :]).then_inc(stored, 16)
            sp.wait_ge(stored, 16 * B)

        @block.tensor
        def _(pe):
            mm, tr = nc.tensor.matmul, nc.tensor.transpose

            def claim(ring, *job):
                if ring.reused(*job):
                    pe.wait_ge(*ring.vacated(*job))
                return ring.slot(*job)

            def load_wait(*names):
                for n in names:
                    pe.wait_ge(loaded[n], 16)

            for stage, p, i in SCHEDULE:
                if stage == "keys0":
                    if i == 0:
                        load_wait("ctxT", "wk0", "wk0r", "consts")
                    o = claim(S, "keys0", p, i)
                    for n, w in enumerate((WK0, WK0R)):
                        last = mm(o[:, 512 * n:512 * n + 256], w[:, i, :],
                                  CTXT[:, :, 0, :], start=True, stop=True)
                    last.then_inc(S.filled, 1)
                elif stage == "values0":
                    if i == 0:
                        load_wait("wv0")
                    o = claim(M, "values0", p, i)
                    mm(o[:, 0:256], CTXT[:, i, :, :].rearrange("p h k -> p (h k)"), WV0,
                       start=True, stop=True).then_inc(M.filled, 1)
                elif stage == "xT":
                    pe.wait_ge(*normed.at(p, i // TPB))
                    o = claim(TR, "xT", p, i)
                    src = XN2 if p == 5 else XN
                    tr(o[:, 0:P], src[:, i, :], IDENT).then_inc(TR.filled, 1)
                elif stage == "query0":
                    if i == 0:
                        load_wait("wq0")
                    o = claim(S, "query0", p, i)
                    pe.wait_ge(*TR.read("xT", p, i))
                    for n in range(2):
                        last = mm(o[:, 512 * n:512 * n + 512], XT[:, i, :], WQ0[:, 512 * n:512 * n + 512],
                                  start=True, stop=True)
                    last.then_inc(S.filled, 1)
                elif stage == "queryT":
                    pe.wait_ge(*rotated.at(p, i))
                    for n in range(2):
                        o = claim(TR, f"queryT{n}", p, i)
                        for c in range(4):
                            last = tr(o[:, c * P:c * P + P], QR[:, i % 2, (4 * n + c) * P:(4 * n + c + 1) * P], IDENT)
                        last.then_inc(TR.filled, 1)
                elif stage == "query":
                    if p == 4 and i == 0:
                        load_wait("mats")
                    o = claim(M, "query", p, i)
                    pe.wait_ge(*TR.read("xT", p, i))
                    mm(o[:, 0:P], mat(f"q{p}"), XT[:, i, :], start=True, stop=True).then_inc(M.filled, 1)
                elif stage == "scores":
                    b = i // TPB
                    o = claim(S, "scores", p, i)
                    if p == 0:
                        if i == 0:
                            pe.wait_ge(*keys0_ready.at(0, KV0 - 1))
                        pe.wait_ge(*TR.read("queryT1", p, i))
                        for c in range(NPAIR):
                            last = mm(o[:, c * P:c * P + P], QT0[:, c, :], KBD0[:, b, c // 2, :],
                                      start=True, stop=True)
                    else:
                        if p == 2:
                            pe.wait_ge(*TR.read("xT", p, i))
                            q = XT[:, i, :]
                        else:
                            pe.wait_ge(*M.read("query", p, i))
                            q = QT[:, i % 2, :]
                        pe.wait_ge(*kbd_ready.at(p, b))
                        for n in range(2):
                            last = mm(o[:, 512 * n:512 * n + 512], q, KBD[:, b % 2, 8 * n:8 * n + 8, :],
                                      start=True, stop=True)
                    last.then_inc(S.filled, 1)
                elif stage == "probsT":
                    pe.wait_ge(*exped.at(p, i))
                    a = ATT.index(p) * T + i
                    for n in range(2):
                        o = claim(TR, f"probsT{n}", p, i)
                        for c in range(4):
                            pair = 4 * n + c
                            last = tr(o[:, c * P:c * P + P],
                                      SM[:, a % 3, 2 * pair:2 * pair + 2, :].rearrange("p h k -> p (h k)"), IDENT)
                        last.then_inc(TR.filled, 1)
                elif stage == "values":
                    b = i // TPB
                    a = ATT.index(p) * T + i
                    ring = S if p == 0 else M
                    o = claim(ring, "values", p, i)
                    if p == 0:
                        if i == 0:
                            pe.wait_ge(*M.read("values0", 0, B - 1))
                    elif i % TPB == 0:
                        pe.wait_ge(*(vex_ready.at(p, b) if p == 2 else M.read("ctxv", p, b)))
                    for c in range(NPAIR):
                        if c % 4 == 0:
                            pe.wait_ge(*TR.read(f"probsT{c // 4}", p, i))
                        if p == 0:
                            last = mm(o[:, c * P:c * P + P], PT[:, a % 2, c, :], VBD0[:, b, c // 2, :],
                                      start=True, stop=True)
                        else:
                            last = mm(o[:, 0:VX], PT[:, a % 2, c, :], VEX[:, b % 2, c, :],
                                      start=(c == 0), stop=(c == NPAIR - 1))
                    last.then_inc(ring.filled, 1)
                elif stage == "outT":
                    pe.wait_ge(*(S if p == 0 else M).read("values", p, i))
                    if p == 0:
                        for n in range(2):
                            o = claim(TR, f"outT{n}", p, i)
                            for c in range(4):
                                last = tr(o[:, c * P:c * P + P], AO0[:, i % 2, (4 * n + c) * P:(4 * n + c + 1) * P],
                                          IDENT)
                            last.then_inc(TR.filled, 1)
                    else:
                        o = claim(TR, "outT0", p, i)
                        tr(o[:, 0:P], AO[:, i % 2, :], IDENT).then_inc(TR.filled, 1)
                elif stage == "project":
                    o = claim(M, "project", p, i)
                    if p == 0:
                        if i == 0:
                            load_wait("wo0")
                        pe.wait_ge(*TR.read("outT1", p, i))
                        for c in range(NPAIR):
                            last = mm(o[:, 0:D], OT0[:, c, :], WO0[:, c, :], start=(c == 0), stop=(c == NPAIR - 1))
                    else:
                        if p == 2 and i == 0:
                            load_wait("mats", "rows")
                        pe.wait_ge(*TR.read("outT0", p, i))
                        mm(o[:, 0:D], OT[:, i % 2, :], mat(f"w{p}"), start=True, stop=False)
                        last = mm(o[:, 0:D], ROW0, row(f"b{p}"), start=False, stop=True)
                    last.then_inc(M.filled, 1)
                elif stage == "keys" and p in (4, 6) and i == 0:
                    o = claim(M, "keys", p, i)
                    mm(o[:, 0:256], mat(f"k{p}"), CTXT[:, :, 0, :], start=True, stop=True).then_inc(M.filled, 1)
                elif stage == "context" and p in (4, 6):
                    o = claim(M, "ctxv", p, i)
                    mm(o[:, 0:D], CTXT[:, i, :, :].rearrange("p h k -> p (h k)"), mat(f"v{p}"),
                       start=True, stop=False)
                    mm(o[:, 0:D], ROW0, row(f"v{p}"), start=False, stop=True).then_inc(M.filled, 1)
                elif stage == "logits":
                    if p == 1 and i == 0:
                        load_wait("mats")
                    o = claim(M, "logits", p, i)
                    pe.wait_ge(*TR.read("xT", p, i))
                    mm(o[:, 0:P], XT[:, i, :], mat(f"gate{p}"), start=True, stop=True).then_inc(M.filled, 1)
                elif stage == "hidden0":
                    if i == 0:
                        load_wait("wg0", "wu0")
                    o = claim(S, "hidden0", p, i)
                    for n, w in enumerate((WG0, WU0)):
                        last = mm(o[:, 512 * n:512 * n + 512], XT[:, i, :], w, start=True, stop=True)
                    last.then_inc(S.filled, 1)
                elif stage == "gatedT":
                    pe.wait_ge(*gated_ready.at(p, i))
                    o = claim(TR, "gatedT", p, i)
                    for c in range(4):
                        last = tr(o[:, c * P:c * P + P], TH[i % 2][:, c * P:c * P + P], IDENT)
                    last.then_inc(TR.filled, 1)
                elif stage == "down0":
                    if i == 0:
                        load_wait("wd0")
                    o = claim(M, "down0", p, i)
                    pe.wait_ge(*TR.read("gatedT", p, i))
                    for c in range(4):
                        last = mm(o[:, 0:D], AT[:, c * P:c * P + P], WD0[:, c, :], start=(c == 0), stop=(c == 3))
                    last.then_inc(M.filled, 1)
                elif stage == "gateT":
                    pe.wait_ge(*gate_ready.at(p, i))
                    o = claim(TR, "gateT", p, i)
                    tr(o[:, 0:P], GATE[:, i % 4, :], IDENT).then_inc(TR.filled, 1)
                elif stage == "bias2":
                    if i == 0:
                        load_wait("bias2")
                    o = claim(M, "bias2", p, i)
                    pe.wait_ge(*TR.read("gateT", p, i))
                    mm(o[:, 0:D], GT[:, i % 2, :], BIAS2[:, (3, 7).index(p), :], start=True, stop=True)\
                        .then_inc(M.filled, 1)
                elif stage == "hidden":
                    b, e = i
                    if b == 0 and e == 0:
                        load_wait(f"w1_{p}")
                    o = claim(S, "hidden", p, i)
                    if e == 0:
                        pe.wait_ge(*TR.read("xT", p, TPB * b + 1))
                    xt = XT[:, TPB * b:TPB * b + TPB, :]
                    w = W1_3 if p == 3 else W1_7
                    for c in range(HID[p] // P):
                        last = mm(o[:, 256 * c:256 * c + 256], w[:, e, c * P:c * P + P], xt, start=True, stop=True)
                    last.then_inc(S.filled, 1)
                elif stage == "expert":
                    b, e = i
                    if b == 0 and e == 0:
                        load_wait(f"w2_{p}")
                    o = claim(M, "expert", p, i)
                    pe.wait_ge(*S.read("hidden", p, i))
                    w = W2_3 if p == 3 else W2_7
                    nc_ = HID[p] // P
                    for j in range(TPB):
                        for c in range(nc_):
                            last = mm(o[:, j * D:j * D + D], HT[:, e % 2, c, j * P:j * P + P], w[:, e, c, :],
                                      start=(c == 0), stop=(c == nc_ - 1))
                    last.then_inc(M.filled, 1)
                elif stage == "mix":
                    o = claim(M, "mix", p, i)
                    t = TPB * i
                    pe.wait_ge(*TR.read("xT", p, t + 1))
                    mm(o[:, 0:256], mat("attn"), XT[:, t:t + TPB, :], start=True, stop=False)
                    for j in range(TPB):
                        last = mm(o[:, j * P:j * P + P], XN[:, t + j, :], IDENT, start=False, stop=(j == 1))
                    last.then_inc(M.filled, 1)
                elif stage == "hidden5":
                    if i == 0:
                        load_wait("w1_5")
                        pe.wait_ge(*M.read("mix", p, B - 1))
                    o = claim(S, "hidden5", p, i)
                    xa = XAT.rearrange("p (m q) -> p m q", m=2)[:, :, 64 * i:64 * i + 64]
                    for c in range(4):
                        last = mm(o[:, c * P:c * P + P], W1_5[:, i, c * P:c * P + P], xa, start=True, stop=True)
                    last.then_inc(S.filled, 1)
                elif stage == "expert5":
                    if i == 0:
                        load_wait("w2_5")
                    o = claim(M, "expert5", p, i)
                    pe.wait_ge(*S.read("hidden5", p, i))
                    for c in range(4):
                        last = mm(o[:, 0:P], W2_5[:, i, c, :], HT5[:, i % 2, c, :], start=(c == 0), stop=(c == 3))
                    last.then_inc(M.filled, 1)
                elif stage == "next5":
                    o = claim(S, "next5", p, i)
                    if i == 0:
                        pe.wait_ge(*M.read("expert5", p, E - 1))
                    mm(o[:, 0:512], mat("next"), EOT[:, 512 * i:512 * i + 512], start=True, stop=True)\
                        .then_inc(S.filled, 1)
                elif stage == "back":
                    o = claim(TR, "back", p, i)
                    pe.wait_ge(*S.read("next5", p, i // 4))
                    tr(o[:, 0:P], YT[:, i * P:i * P + P], IDENT).then_inc(TR.filled, 1)

        @block.scalar
        def _(act):
            def run(out_, in_, func, bias=0.0, scale=1.0):
                return nc.scalar.activation(out_, in_, func, bias=bias, scale=scale)

            for stage, p, i in SCHEDULE:
                if stage == "values0":
                    act.wait_ge(*M.full("values0", p, i))
                    if i == 0:
                        act.wait_ge(zeroed_tables, 2)
                    ps = M.slot("values0", p, i)
                    for h in range(2):
                        last = run(VBD0[64 * h:64 * h + 64, i, :, 64 * h:64 * h + 64],
                                   ps[64 * h:64 * h + 64, 0:256].rearrange("p (g d) -> p g d", g=KV0), ACT.Copy)
                        if h == 0:
                            last.then_inc(act_chain, 1)
                    last.then_inc(M.emptied["act"], 1)
                elif stage == "xT":
                    act.wait_ge(*TR.full("xT", p, i))
                    ps = TR.slot("xT", p, i)[:, 0:P]
                    if p == 5:
                        if i == 0:
                            act.wait_ge(loaded["cols"], 16)
                        ins = run(XT[:, i, :], ps, ACT.Identity, bias=col("ln_bias"), scale=col("ln_scale"))
                    else:
                        ins = run(XT[:, i, :], ps, ACT.Copy)
                    ins.then_inc(TR.emptied["act"], 1)
                elif stage == "queryT":
                    if i > 0:
                        act.wait_ge(*S.full("scores", p, i - 1))
                    for n in range(2):
                        act.wait_ge(*TR.full(f"queryT{n}", p, i))
                        run(QT0[:, 4 * n:4 * n + 4, :].rearrange("p c q -> p (c q)"), TR.slot(f"queryT{n}", p, i)[:, :],
                            ACT.Copy).then_inc(TR.emptied["act"], 1)
                elif stage == "query":
                    act.wait_ge(*M.full("query", p, i))
                    if p == 4 and i == 0:
                        act.wait_ge(loaded["cols"], 16)
                    if i >= 2:
                        act.wait_ge(*S.full("scores", p, i - 2))
                    elif p == 6:
                        act.wait_ge(*S.full("scores", 4, T - 2 + i))
                    run(QT[:, i % 2, :], M.slot("query", p, i)[:, 0:P], ACT.Identity, bias=col(f"bq{p}"))\
                        .then_inc(M.emptied["act"], 1)
                elif stage == "exp":
                    a = ATT.index(p) * T + i
                    act.wait_ge(*shifted.at(p, i))
                    scale = {0: 1.0, 2: 1.0 / float(np.sqrt(np.float32(D))), 4: 1.0 / float(np.sqrt(np.float32(DH))),
                             6: 1.0 / float(np.sqrt(np.float32(DH)))}[p]
                    run(SM[:, a % 3, :, :], SM[:, a % 3, :, :], ACT.Exp, scale=scale).then_inc(exped.sem, 1)
                elif stage == "probsT":
                    a = ATT.index(p) * T + i
                    if a >= 2:
                        q, t = (p, i - 2) if i >= 2 else (ATT[ATT.index(p) - 1], T - 2 + i)
                        act.wait_ge(*(S if q == 0 else M).full("values", q, t))
                    for n in range(2):
                        act.wait_ge(*TR.full(f"probsT{n}", p, i))
                        run(PT[:, a % 2, 4 * n:4 * n + 4, :].rearrange("p c q -> p (c q)"),
                            TR.slot(f"probsT{n}", p, i)[:, :], ACT.Copy).then_inc(TR.emptied["act"], 1)
                elif stage == "outT":
                    if p == 0:
                        if i > 0:
                            act.wait_ge(*M.full("project", p, i - 1))
                        for n in range(2):
                            act.wait_ge(*TR.full(f"outT{n}", p, i))
                            run(OT0[:, 4 * n:4 * n + 4, :].rearrange("p c q -> p (c q)"),
                                TR.slot(f"outT{n}", p, i)[:, :], ACT.Copy).then_inc(TR.emptied["act"], 1)
                    else:
                        act.wait_ge(*TR.full("outT0", p, i))
                        if i >= 2:
                            act.wait_ge(*M.full("project", p, i - 2))
                        run(OT[:, i % 2, :], TR.slot("outT0", p, i)[:, 0:P], ACT.Copy).then_inc(TR.emptied["act"], 1)
                elif stage == "keys" and p in (4, 6) and i == 0:
                    if p == 4:
                        act.wait_ge(loaded["cols"], 16)
                    act.wait_ge(*M.full("keys", p, i))
                    if p == 6:
                        act.wait_ge(*kbd_ready.at(4, B - 1))
                    run(KT[:, :, :].rearrange("p b k -> p (b k)"), M.slot("keys", p, i)[:, 0:256],
                        ACT.Identity, bias=col(f"bk{p}")).then_inc(M.emptied["act"], 1)
                elif stage == "context":
                    b = i
                    if p == 2 and b == 0:
                        act.wait_ge(zeroed_values, 5)
                        act.wait_ge(loaded["ctx2"], 16)
                    if b >= 2 or p > 2:
                        q, c = (p, b - 2) if b >= 2 else (p - 2, b + 2)
                        act.wait_ge(*M.full("values", q, TPB * c + 1))
                    if p in (4, 6):
                        act.wait_ge(*M.full("ctxv", p, b))
                    for h in range(2):
                        half = slice(64 * h, 64 * h + 64)
                        src = CTX2[half, b, :] if p == 2 else M.slot("ctxv", p, b)[half, 0:D]
                        ins = run(diagonal(half, b % 2, DH * h, 2 * DH, DH),
                                  src.rearrange("p (c h d) -> p c h d", h=2, d=DH)[:, :, h, :], ACT.Copy)
                        if h == 0:
                            ins.then_inc(act_chain, 1)
                        elif p == 2:
                            ins.then_inc(vex_ready.sem, 1)
                        else:
                            ins.then_inc(M.emptied["act"], 1)
                elif stage == "logits":
                    k = i % 2
                    act.wait_ge(*gate_top.at(p, i))
                    if p == 1:
                        ins = run(GV[:, k, 1:2], GV[:, k, 0:1], ACT.Tanh, scale=0.5)
                    elif p == 3:
                        ins = run(GE[:, k, :], LG[:, k, :], ACT.Tanh, scale=0.5)
                    else:
                        ins = run(GV[:, k, 1:2], GV[:, k, 0:1], ACT.Exp)
                    ins.then_inc(gate_exp.sem, 1)
                elif stage == "tanh":
                    act.wait_ge(*hid0_ready.at(p, i))
                    if i >= 2:
                        act.wait_ge(*TR.full("gatedT", p, i - 2))
                    run(TH[i % 2], GP[i % 2], ACT.Tanh, scale=0.5).then_inc(tanh_ready.sem, 1)
                elif stage == "gatedT":
                    act.wait_ge(*TR.full("gatedT", p, i))
                    if i > 0:
                        act.wait_ge(*M.full("down0", p, i - 1))
                    run(AT, TR.slot("gatedT", p, i)[:, :], ACT.Copy).then_inc(TR.emptied["act"], 1)
                elif stage == "gateT":
                    act.wait_ge(*TR.full("gateT", p, i))
                    if i >= 2:
                        act.wait_ge(*M.full("bias2", p, i - 2))
                    elif p == 7:
                        act.wait_ge(*M.full("bias2", 3, T - 2 + i))
                    run(GT[:, i % 2, :], TR.slot("gateT", p, i)[:, 0:P], ACT.Copy).then_inc(TR.emptied["act"], 1)
                elif stage == "hidden":
                    b, e = i
                    if (p, b, e) == (3, 0, 0):
                        act.wait_ge(loaded["cols"], 16)
                    act.wait_ge(*S.full("hidden", p, i))
                    if b > 0 or e >= 2:
                        n = b * E + e - 2
                        act.wait_ge(*M.full("expert", p, (n // E, n % E)))
                    elif p == 3:
                        act.wait_ge(*M.full("project", 0, T - 1))
                    for c in range(HID[p] // P):
                        ins = run(HT[:, e % 2, c, :], S.slot("hidden", p, i)[:, 256 * c:256 * c + 256],
                                  ACT.Silu if p == 3 else ACT.Relu,
                                  bias=col(f"b1_{p}", e * (HID[p] // P) + c))
                        if c < HID[p] // P - 1:
                            ins.then_inc(act_chain, 1)
                    ins.then_inc(S.emptied["act"], 1)
                elif stage == "mix":
                    act.wait_ge(*M.full("mix", p, i))
                    run(XAT[:, 256 * i:256 * i + 256], M.slot("mix", p, i)[:, 0:256], ACT.Identity,
                        bias=col("attn_b")).then_inc(M.emptied["act"], 1)
                elif stage == "hidden5":
                    act.wait_ge(*S.full("hidden5", p, i))
                    if i >= 2:
                        act.wait_ge(*M.full("expert5", p, i - 2))
                    for c in range(4):
                        ins = run(HT5[:, i % 2, c, :], S.slot("hidden5", p, i)[:, c * P:c * P + P], ACT.Gelu,
                                  bias=col("b1_5", 4 * i + c))
                        if c < 3:
                            ins.then_inc(act_chain, 1)
                    ins.then_inc(S.emptied["act"], 1)
                elif stage == "expert5":
                    act.wait_ge(*M.full("expert5", p, i))
                    run(EOT.rearrange("p (m q) -> p m q", m=2)[:, :, 64 * i:64 * i + 64],
                        M.slot("expert5", p, i)[:, 0:P].rearrange("p (m q) -> p m q", m=2), ACT.Identity,
                        bias=col("b2_5", i)).then_inc(M.emptied["act"], 1)
                elif stage == "next5":
                    act.wait_ge(*S.full("next5", p, i))
                    run(YT[:, 512 * i:512 * i + 512], S.slot("next5", p, i)[:, 0:512], ACT.Gelu,
                        bias=col("next_b")).then_inc(S.emptied["act"], 1)

        @block.vector
        def _(dve):
            v = nc.vector
            steps = [0]

            def step(ins):
                steps[0] += 1
                ins.then_inc(dve_chain, 1)
                dve.wait_ge(dve_chain, steps[0])

            def sure(ins, sem_, n):
                ins.then_inc(sem_, 1)
                dve.wait_ge(sem_, n)

            def rsqrt_of_variance():
                step(v.tensor_scalar(VAR[:, :], MV[:, :, 1], EPS, None, ALU.add))
                step(v.tensor_scalar(SHIFT[:, :], VAR[:, :].bitcast(I32), 1, None, ALU.logical_shift_right))
                step(v.tensor_scalar(RS[:, :].bitcast(I32), SHIFT[:, :], -1.0, RSQRT_SEED, ALU.mult, ALU.add))
                for _ in range(3):
                    step(v.tensor_tensor(SQ2[:, :], RS[:, :], RS[:, :], ALU.mult))
                    step(v.scalar_tensor_tensor(HV[:, :], SQ2[:, :], -0.5, VAR[:, :], ALU.mult, ALU.mult))
                    step(v.scalar_tensor_tensor(RS[:, :], HV[:, :], 1.5, RS[:, :], ALU.add, ALU.mult))

            def normalise(src, dst, t0):
                for j in range(TPB):
                    step(v.bn_stats(ST[:, j, :], src(t0 + j)))
                    step(v.bn_aggr(MV[:, j, :], ST[:, j, :]))
                rsqrt_of_variance()
                for j in range(TPB):
                    ins = v.tensor_scalar(dst(t0 + j), src(t0 + j), MV[:, j, 0:1], RS[:, j:j + 1],
                                          ALU.subtract, ALU.mult)
                    if j < TPB - 1:
                        step(ins)
                return ins

            def gate(p, i):
                k, k4 = i % 2, i % 4
                ps = M.slot("logits", p, i)[:, 0:E]
                dve.wait_ge(*M.full("logits", p, i))
                if p == 1:
                    sure(v.tensor_copy(LG[:, k, :], ps), *M.read("logits", p, i))
                else:
                    if i == 0:
                        dve.wait_ge(loaded["gbias"], 16)
                    sure(v.tensor_tensor(LG[:, k, :], ps, GB[:, (3, 7).index(p), :], ALU.add),
                         *M.read("logits", p, i))
                step(v.max(TOP[:, k, :], LG[:, k, :]))
                step(v.max_index(IDX[:, k, :], TOP[:, k, :], LG[:, k, :]))
                step(v.tensor_copy(IDF[:, k, :], IDX[:, k, :]))
                for n in range(2 if p == 7 else 1):
                    step(v.tensor_scalar(HOT[:, k, n, :], const("iota"), IDF[:, k, n:n + 1], None, ALU.is_equal))
                if p == 1:
                    sure(v.tensor_copy(GV[:, k, 0:1], TOP[:, k, 0:1]), *gate_top.at(p, i))
                    dve.wait_ge(*gate_exp.at(p, i))
                    step(v.tensor_scalar(GV[:, k, 2:3], GV[:, k, 1:2], 1.0, 0.5, ALU.add, ALU.mult))
                    step(v.tensor_scalar(GATE[:, k4, 0:E], HOT[:, k, 0, :], GV[:, k, 2:3], None, ALU.mult))
                    sure(v.tensor_scalar(GATE[:, k4, E:2 * E], HOT[:, k, 0, :], GV[:, k, 2:3], 0.5,
                                         ALU.mult, ALU.mult), *gate_ready.at(p, i))
                elif p == 3:
                    sure(v.tensor_scalar(LG[:, k, :], LG[:, k, :], TOP[:, k, 0:1], None, ALU.subtract),
                         *gate_top.at(p, i))
                    dve.wait_ge(*gate_exp.at(p, i))
                    step(v.tensor_scalar(GE2[:, k, :], GE[:, k, :], -1.0, 1.0, ALU.mult, ALU.add))
                    step(v.reciprocal(GE2[:, k, :], GE2[:, k, :]))
                    step(v.scalar_tensor_tensor(GE[:, k, :], GE[:, k, :], 1.0, GE2[:, k, :], ALU.add, ALU.mult))
                    step(v.tensor_reduce(GV[:, k, 0:1], GE[:, k, :], X_AXIS, ALU.add))
                    step(v.reciprocal(GV[:, k, 1:2], GV[:, k, 0:1]))
                    if i >= 4:
                        dve.wait_ge(*TR.full("gateT", p, i - 4))
                    sure(v.tensor_scalar(GATE[:, k4, 0:E], HOT[:, k, 0, :], GV[:, k, 1:2], None, ALU.mult),
                         *gate_ready.at(p, i))
                else:
                    sure(v.tensor_tensor(GV[:, k, 0:1], TOP[:, k, 1:2], TOP[:, k, 0:1], ALU.subtract),
                         *gate_top.at(p, i))
                    dve.wait_ge(*gate_exp.at(p, i))
                    step(v.tensor_scalar(GV[:, k, 2:3], GV[:, k, 1:2], 1.0, None, ALU.add))
                    step(v.reciprocal(GV[:, k, 3:4], GV[:, k, 2:3]))
                    step(v.tensor_tensor(GV[:, k, 4:5], GV[:, k, 1:2], GV[:, k, 3:4], ALU.mult))
                    step(v.tensor_scalar(GE[:, k, :], HOT[:, k, 0, :], GV[:, k, 3:4], None, ALU.mult))
                    if i >= 4:
                        dve.wait_ge(*TR.full("gateT", p, i - 4))
                    sure(v.scalar_tensor_tensor(GATE[:, k4, 0:E], HOT[:, k, 1, :], GV[:, k, 4:5], GE[:, k, :],
                                                ALU.mult, ALU.add), *gate_ready.at(p, i))

            def add_to_x(ring, job, p, i, t):
                dve.wait_ge(*ring.full(job, p, i))
                sure(v.tensor_tensor(X[:, t, :], ring.slot(job, p, i)[:, 0:D], X[:, t, :], ALU.add),
                     *ring.read(job, p, i))

            step(v.memset(GATE[:, :, :], 0.0))

            for stage, p, i in SCHEDULE:
                if stage == "norm":
                    t0 = TPB * i
                    if p == -1:
                        dve.wait_ge(loaded["x01" if i < 2 else "x23"], 16)
                    ins = normalise(lambda t: X[:, t, :], lambda t: XN[:, t, :], t0)
                    if p + 1 == 5:
                        step(ins)
                        ins = normalise(lambda t: XN[:, t, :], lambda t: XN2[:, t, :], t0)
                    sure(ins, *normed.at(p + 1, i))
                elif stage == "keys0":
                    dve.wait_ge(*S.full("keys0", p, i))
                    if i == 0:
                        dve.wait_ge(loaded["consts"], 16)
                        dve.wait_ge(zeroed_tables, 2)
                    ps = S.slot("keys0", p, i)
                    step(v.tensor_tensor(K1.rearrange("p (b k) -> p b k", b=B),
                                         ps[:, 0:256].rearrange("p (b k) -> p b k", b=B), COSK, ALU.mult))
                    sure(v.tensor_tensor(K2.rearrange("p (b k) -> p b k", b=B),
                                         ps[:, 512:768].rearrange("p (b k) -> p b k", b=B), SINK, ALU.mult),
                         *S.read("keys0", p, i))
                    for h in range(2):
                        half = slice(64 * h, 64 * h + 64)
                        ins = v.tensor_tensor(KBD0[half, :, i, 64 * h:64 * h + 64],
                                              K1[half, :].rearrange("p (b k) -> p b k", b=B),
                                              K2[half, :].rearrange("p (b k) -> p b k", b=B), ALU.add)
                        if h == 0:
                            step(ins)
                    sure(ins, *keys0_ready.at(p, i))
                    if i == KV0 - 1:
                        dve.wait_ge(loaded["mask0"], 16)
                        sure(v.tensor_scalar(FILL0[:, :, :], M0[:, :, :], 0.0, FILL, ALU.is_equal, ALU.mult), fills, 1)
                elif stage == "query0":
                    j = i % TPB
                    dve.wait_ge(*S.full("query0", p, i))
                    if i > 0:
                        dve.wait_ge(*rotated.at(p, i - 1))
                    ps = S.slot("query0", p, i)[:, :].rearrange("p (h d) -> p h d", h=H)
                    t1, t2 = (t.rearrange("p (h d) -> p h d", h=H) for t in (T1, T2))

                    def table(t, lo, hi):
                        return t[:, j, lo:hi].unsqueeze(1).broadcast_to([P, H, hi - lo])
                    step(v.tensor_tensor(t1, ps, table(COSQ, 0, D0), ALU.mult))
                    step(v.tensor_tensor(t2[:, :, 0:32], ps[:, :, 32:64], table(SINQ, 0, 32), ALU.mult))
                    sure(v.tensor_tensor(t2[:, :, 32:64], ps[:, :, 0:32], table(SINQ, 32, 64), ALU.mult),
                         *S.read("query0", p, i))
                elif stage == "scores":
                    a = ATT.index(p) * T + i
                    b = i // TPB
                    dve.wait_ge(*S.full("scores", p, i))
                    if a >= 3:
                        q, t = (p, i - 3) if i >= 3 else (ATT[ATT.index(p) - 1], T - 3 + i)
                        dve.wait_ge(*TR.full("probsT1", q, t))
                    ps = S.slot("scores", p, i)[:, :].rearrange("p (h k) -> p h k", h=H)
                    sm = SM[:, a % 3, :, :]
                    if p == 0:
                        dve.wait_ge(*relmasked.at(p, i))
                        sure(v.scalar_tensor_tensor(sm, ps, float(D0) ** -0.5, RELM[:, i % 2, :, :],
                                                    ALU.mult, ALU.add), *S.read("scores", p, i))
                    else:
                        fill = FILL2[:, b, :] if p == 4 else FILL1[:, i, :]
                        sure(v.tensor_tensor(sm, ps, fill.unsqueeze(1).broadcast_to([P, H, SK]), ALU.add),
                             *S.read("scores", p, i))
                    sure(v.tensor_reduce(MX[:, a % 3, :], sm, X_AXIS, ALU.max), *masked.at(p, i))
                elif stage == "values":
                    k = i % 2
                    a = ATT.index(p) * T + i
                    if p == 0:
                        dve.wait_ge(*exped.at(p, i))
                        step(v.tensor_reduce(SUM[:, k, :], SM[:, a % 3, :, :], X_AXIS, ALU.add))
                        step(v.reciprocal(RCP[:, k, :], SUM[:, k, :]))
                        dve.wait_ge(*S.full("values", p, i))
                        if i >= 2:
                            dve.wait_ge(*TR.full("outT1", p, i - 2))
                        ps = S.slot("values", p, i)[:, :].rearrange("p (h d) -> p h d", h=H)
                        sure(v.tensor_tensor(AO0[:, k, :].rearrange("p (h d) -> p h d", h=H), ps,
                                             RCP[:, k, :].unsqueeze(2).broadcast_to([P, H, D0]), ALU.mult),
                             *S.read("values", p, i))
                    else:
                        dve.wait_ge(*M.full("values", p, i))
                        ps = M.slot("values", p, i)
                        step(v.reciprocal(RCP[:, k, :], ps[:, D:VX]))
                        if i >= 2:
                            dve.wait_ge(*TR.full("outT0", p, i - 2))
                        sure(v.tensor_tensor(AO[:, k, :].rearrange("p (h d) -> p h d", h=H),
                                             ps[:, 0:D].rearrange("p (h d) -> p h d", h=H),
                                             RCP[:, k, :].unsqueeze(2).broadcast_to([P, H, DH]), ALU.mult),
                             *M.read("values", p, i))
                elif stage == "project":
                    add_to_x(M, "project", p, i, i)
                    if p == 0 and i == 0:
                        dve.wait_ge(loaded["mask1"], 16)
                        dve.wait_ge(loaded["mask2"], 16)
                        step(v.tensor_scalar(FILL1, M1[:, :, :], 0.0, FILL, ALU.is_equal, ALU.mult))
                        step(v.tensor_scalar(FILL2, M2[:, :, :], 0.0, FILL, ALU.is_equal, ALU.mult))
                elif stage == "logits":
                    gate(p, i)
                elif stage == "hidden0":
                    dve.wait_ge(*gate_ready.at(p, i))
                    dve.wait_ge(*S.full("hidden0", p, i))
                    if i >= 2:
                        dve.wait_ge(*gated_ready.at(p, i - 2))
                    ps = S.slot("hidden0", p, i)
                    for n, (dst, g) in enumerate(((GP[i % 2], GATE[:, i % 4, 0:E]), (UP[i % 2], GATE[:, i % 4, E:2 * E]))):
                        ins = v.tensor_tensor(dst.rearrange("p (e f) -> p e f", e=E),
                                              ps[:, 512 * n:512 * n + 512].rearrange("p (e f) -> p e f", e=E),
                                              g.unsqueeze(2).broadcast_to([P, E, I0]), ALU.mult)
                        if n == 0:
                            sure(ins, *hid0_ready.at(p, i))
                    sure(ins, *S.read("hidden0", p, i))
                elif stage == "gated":
                    dve.wait_ge(*tanh_ready.at(p, i))
                    sure(v.scalar_tensor_tensor(GP[i % 2], TH[i % 2], 1.0, GP[i % 2], ALU.add, ALU.mult), *half_ready.at(p, i))
                elif stage == "down0":
                    add_to_x(M, "down0", p, i, i)
                    if i == T - 1:
                        step(v.memset(GATE[:, :, E:2 * E], 0.0))
                elif stage == "bias2":
                    add_to_x(M, "bias2", p, i, i)
                elif stage == "expert":
                    b, e = i
                    dve.wait_ge(*M.full("expert", p, i))
                    for j in range(TPB):
                        t = TPB * b + j
                        ins = v.scalar_tensor_tensor(X[:, t, :], M.slot("expert", p, i)[:, j * D:j * D + D],
                                                     GATE[:, t % 4, e:e + 1], X[:, t, :], ALU.mult, ALU.add)
                        if j < TPB - 1:
                            step(ins)
                    sure(ins, *M.read("expert", p, i))
                elif stage == "back":
                    add_to_x(TR, "back", p, i, i)

        @block.gpsimd
        def _(pool):
            g = nc.gpsimd
            def sure(ins, sem_, n):
                ins.then_inc(sem_, 1)
                pool.wait_ge(sem_, n)

            sure(g.memset(KBD0, 0.0), zeroed_tables, 1)
            sure(g.memset(VBD0, 0.0), zeroed_tables, 2)
            sure(g.memset(ROW[:, :, :], 0.0), zeroed_rows, 1)
            sure(g.memset(BIAS2[:, :, :], 0.0), zeroed_rows, 2)
            sure(g.memset(VEX[:, :, :, :], 0.0), zeroed_values, 1)
            for r in range(2):
                for h in range(2):
                    sure(g.memset(diagonal(slice(64 * h, 64 * h + 64), r, D + h, 2, 1), 1.0),
                         zeroed_values, 2 + 2 * r + h)

            for stage, p, i in SCHEDULE:
                if stage == "query0":
                    b, j = i // TPB, i % TPB
                    if i == 0:
                        pool.wait_ge(loaded["rel"], 16)
                        pool.wait_ge(fills, 1)
                    if i >= 2:
                        pool.wait_ge(*masked.at(p, i - 2))
                    sure(g.tensor_tensor(RELM[:, i % 2, :, :], REL[:, j, :, :],
                                         FILL0[:, b, :].unsqueeze(1).broadcast_to([P, H, SK]), ALU.add),
                         *relmasked.at(p, i))
                    pool.wait_ge(*S.read("query0", p, i))
                    if i >= 2:
                        pool.wait_ge(*TR.full("queryT1", p, i - 2))
                    sure(g.tensor_tensor(QR[:, i % 2, :], T1, T2, ALU.add), *rotated.at(p, i))
                elif stage == "keys":
                    b = i
                    if (p, b) == (2, 0):
                        pool.wait_ge(loaded["consts"], 16)
                        pool.wait_ge(loaded["ctxT"], 16)
                    if p > 2 and b == 0:
                        pool.wait_ge(*M.read("keys", p, 0))
                    if b >= 2 or p > 2:
                        q, c = (p, b - 2) if b >= 2 else (p - 2, b + 2)
                        pool.wait_ge(*S.full("scores", q, TPB * c + 1))
                    src = CTXT[:, b, 0, :] if p == 2 else KT[:, b, :]
                    sure(g.tensor_tensor(KBD[:, b % 2, :, :], src.unsqueeze(1).broadcast_to([P, H, SK]), HEADS,
                                         ALU.mult), *kbd_ready.at(p, b))
                elif stage == "scores":
                    a = ATT.index(p) * T + i
                    pool.wait_ge(*masked.at(p, i))
                    sure(g.tensor_tensor(SM[:, a % 3, :, :], SM[:, a % 3, :, :],
                                         MX[:, a % 3, :].unsqueeze(2).broadcast_to([P, H, SK]), ALU.subtract),
                         *shifted.at(p, i))
                elif stage == "gated":
                    pool.wait_ge(*half_ready.at(p, i))
                    sure(g.tensor_tensor(TH[i % 2], GP[i % 2], UP[i % 2], ALU.mult), *gated_ready.at(p, i))


def _constants():
    c = np.zeros((P, NCONST), np.float32)

    def put(name, a):
        o, n = CONSTS[name]
        c[:, o:o + n] = np.asarray(a, np.float32).reshape(P, n)

    put("ident", np.eye(P))
    row0 = np.zeros((P, P))
    row0[0] = 1
    put("row0", row0)
    put("heads", np.arange(P)[:, None] // DH == np.arange(H)[None, :])
    put("iota", np.tile(np.arange(E), (P, 1)))
    inv = (1.0 / np.float32(10000.0) ** (np.arange(0, D0, 2, dtype=np.float32) / np.float32(D0))).astype(np.float32)
    angle = np.repeat(np.outer(np.arange(SQ, dtype=np.float32), inv).astype(np.float32), 2, axis=-1)
    cos, sin = np.cos(angle), np.sin(angle)
    sin[:, :D0 // 2] *= -1
    put("cosq", cos.reshape(TPB, P, D0).transpose(1, 0, 2))
    put("sinq", sin.reshape(TPB, P, D0).transpose(1, 0, 2))
    put("cosk", np.tile(cos[:SK].T, (2, 1)))
    put("sink", np.tile(sin[:SK].T, (2, 1)))
    return c


def _layout(a):
    f = {}
    f["x"] = a["x"].reshape(T, P, D).transpose(1, 0, 2)
    ctx = a["ctx_1024"]
    f["ctxT"] = np.tile(ctx.transpose(2, 0, 1)[:, :, None], (1, 1, 2, 1))
    f["ctx2"] = np.tile(ctx.transpose(1, 0, 2), (2, 1, 1))
    f["consts"] = _constants()
    zero = np.zeros((P, NCOLS), np.float32)

    def cols(v):
        return v.reshape(-1, P).T

    for name, v in (("bq4", a["L2_xattn_bq"]), ("bk4", a["L2_xattn_bk"]), ("bq6", a["L3_xattn_bq"]),
                    ("bk6", a["L3_xattn_bk"]), ("ln_scale", a["L2_ffn_ln_scale"]), ("ln_bias", a["L2_ffn_ln_bias"]),
                    ("attn_b", a["L2_ffn_attn_b"]), ("next_b", a["L2_ffn_next_b"]), ("b1_3", a["L1_ffn_b1"]),
                    ("b1_5", a["L2_ffn_b1"]), ("b2_5", a["L2_ffn_b2"]), ("b1_7", a["L3_ffn_b1"])):
        v = cols(v)
        zero[:, COLS[name]:COLS[name] + v.shape[1]] = v
    f["cols"] = zero
    m = {"w2": a["L1_xattn_W_fc"].T, "q4": a["L2_xattn_Wq"].T, "k4": a["L2_xattn_Wk"].T, "v4": a["L2_xattn_Wv"].T,
         "w4": a["L2_xattn_Wo"].T, "attn": a["L2_ffn_attn_w"].T, "next": a["L2_ffn_next_w"].T,
         "q6": a["L3_xattn_Wq"], "k6": a["L3_xattn_Wk"], "v6": a["L3_xattn_Wv"], "w6": a["L3_xattn_Wo"],
         "gate1": a["L0_ffn_gate_w"].T, "gate3": a["L1_ffn_Wg"], "gate7": a["L3_ffn_Wr"]}
    mats = np.zeros((P, len(MATS), P), np.float32)
    for n, name in enumerate(MATS):
        mats[:, n, :m[name].shape[1]] = m[name]
    f["mats"] = mats
    r = {"b2": "L1_xattn_b_fc", "v4": "L2_xattn_bv", "b4": "L2_xattn_bo", "v6": "L3_xattn_bv", "b6": "L3_xattn_bo"}
    f["rows"] = np.stack([a[r[n]] for n in ROWS])[None]
    f["bias2"] = np.stack([a["L1_ffn_b2"], a["L3_ffn_b2"]], axis=1)
    f["gbias"] = np.tile(np.stack([a["L1_ffn_bg"], a["L3_ffn_br"]])[None], (P, 1, 1))
    away = np.abs(np.arange(SQ)[:, None] - np.arange(SK)[None, :])
    rel = a["L0_xattn_rel_pos_bias"][:, away]
    f["relpos"] = rel.reshape(H, TPB, P, SK).transpose(2, 1, 0, 3)
    f["mask0"] = np.tile(a["mask_BxS2_bf1"].view(np.uint8)[None], (P, 1, 1))
    f["mask1"] = a["mask_Bx1xSxS2_ik1"].reshape(T, P, SK).transpose(1, 0, 2)
    f["mask2"] = np.tile(a["mask_Bx1x1xS2_ik0"].reshape(1, B, SK), (P, 1, 1))
    f["wq0"] = a["L0_xattn_Wq"]
    wk = a["L0_xattn_Wk"].reshape(D, KV0, D0)
    f["wk0"] = np.tile(wk, (1, 1, 2))
    f["wk0r"] = np.tile(np.roll(wk, D0 // 2, axis=-1), (1, 1, 2))
    f["wv0"] = a["L0_xattn_Wv"]
    f["wo0"] = a["L0_xattn_Wo"].reshape(NPAIR, P, D).transpose(1, 0, 2)
    f["wg0"] = a["L0_ffn_w_gate"].transpose(2, 0, 1).reshape(D, E * I0)
    f["wu0"] = a["L0_ffn_w_up"].transpose(2, 0, 1).reshape(D, E * I0)
    f["wd0"] = a["L0_ffn_w_down"].transpose(0, 2, 1).reshape(4, P, D).transpose(1, 0, 2)
    for p, n in ((3, "L1_ffn_W1"), (5, "L2_ffn_w1"), (7, "L3_ffn_W1")):
        f[f"w1_{p}"] = a[n].transpose(1, 0, 2)
    for p, n in ((3, "L1_ffn_W2"), (5, "L2_ffn_w2"), (7, "L3_ffn_W2")):
        f[f"w2_{p}"] = a[n].reshape(E, HID[p] // P, P, D).transpose(2, 0, 1, 3)
    return {k: np.ascontiguousarray(v) for k, v in f.items()}


NAMES = ["x", "ctxT", "ctx2", "consts", "cols", "mats", "rows", "bias2", "gbias", "relpos", "mask0", "mask1", "mask2",
         "wq0", "wk0", "wk0r", "wv0", "wo0", "wg0", "wu0", "wd0", "w1_3", "w2_3", "w1_5", "w2_5", "w1_7", "w2_7"]


def kernel(**inputs):
    import concourse.bacc as bacc
    from concourse.bass_utils import run_bass_kernel_spmd

    laid = _layout({k: np.asarray(v) for k, v in inputs.items()})
    nc = bacc.Bacc("TRN2", target_bir_lowering=False, num_devices=1)
    arrays, args = {}, []
    for name in NAMES:
        v = laid[name]
        arrays[f"in_{name}"] = v
        args.append(nc.dram_tensor(f"in_{name}", v.shape, mybir.dt.from_np(v.dtype), kind="ExternalInput").ap())
    args.append(nc.dram_tensor("out_x", (P, T, D), F32, kind="ExternalOutput").ap())
    build(nc, *args)
    r = run_bass_kernel_spmd(nc, [arrays], core_ids=[0])
    return np.ascontiguousarray(r.results[0]["out_x"].transpose(1, 0, 2)).reshape(B, SQ, D)
```

```python
from contextlib import ExitStack

import numpy as np
import concourse.bass as bass
from concourse import mybir

F32 = mybir.dt.float32
I32 = mybir.dt.int32
U32 = mybir.dt.uint32
U8 = mybir.dt.uint8
ALU = mybir.AluOpType
ACT = mybir.ActivationFunctionType
X_AXIS = mybir.AxisListType.X

P = 128
B, SQ, D = 4, 256, 128
ORDER = [0, 2, 1, 3]
SK = 64
T = B * SQ // P
TPB = SQ // P
H = 16
D0, KV0 = 64, 4
DH = D // H
NPAIR = H // 2
E = 8
I0 = 64
HID = {3: 512, 5: 512, 7: 256}
EPS = 1e-5
FILL = -float(2.0 ** 100)
RSQRT_SEED = float(0x5F3759DF)
VX = D + H

ATT, FFN = (0, 2, 4, 6), (1, 3, 5, 7)
START = {0: 0, 1: 7.5, 2: 16, 3: 23.5, 4: 31.25, 5: 38.25, 6: 49.75, 7: 56.25}
PL = {
    ("probsT", 0): 0.3, ("query0", 0): -2.9, ("queryT", 0): -1.8, ("values", 0): 0.7, ("exp", 0): -0.65,
    ("sum", 0): -0.3, ("scores", 0): -1.7, ("xT", 0): -3.4, ("finish", 0): 0.9,
    ("xT", 1): -2.8, ("logits", 1): -2.7, ("hidden0", 1): -0.7, ("tanh", 1): -0.65, ("gated", 1): 0.15,
    ("gatedT", 1): 1, ("down0", 1): 1.45, ("finish", 1): 2.3,
    ("probsT", 2): 0, ("outT", 2): 1.1, ("xT", 2): -2.3, ("scores", 2): -1.85, ("exp", 2): -0.65, ("values", 2): 0.4,
    ("project", 2): 1.6, ("finish", 2): 1.7,
    ("xT", 3): -1.8, ("logits", 3): -0.5, ("gateT", 3): 1, ("bias2", 3): 1.5,
    ("probsT", 4): 0, ("outT", 4): 1.1, ("xT", 4): -2.8, ("scores", 4): -1.7, ("exp", 4): -0.8, ("values", 4): 0.4,
    ("project", 4): 1.6, ("finish", 4): 1.7, ("query", 4): -2.65,
    ("xT", 5): -3.15, ("hidden5", 5): 0, ("expert5", 5): 0.6, ("next5", 5): 2.7, ("back", 5): 6.15,
    ("probsT", 6): 0, ("outT", 6): 1.1, ("xT", 6): -2.8, ("scores", 6): -1.7, ("exp", 6): -0.65, ("values", 6): 0.4,
    ("project", 6): 1.6, ("finish", 6): 2.15, ("query", 6): -2.35,
    ("xT", 7): -2.8, ("logits", 7): -1.5, ("gateT", 7): 1, ("bias2", 7): 1.5,
    "fold": -1.2, "bias": -2, "keys": -4.1, "context": -1.24, "norm": 0.05, "norm2": 0.3, "mix": -2.75, "step5": 0.2,
}
LAG = 2


def make_schedule():
    out = []

    def put(p, time, stage, index):
        out.append((START[p] + time, len(out), stage, p, index))

    def finish(p, b, time):
        put(p, time, "stats", b)
        put(p, time + PL["norm"], "norm", b)
        if p + 1 == 5:
            put(p, time + PL["norm"] + 0.01, "stats2", b)
            put(p, time + PL["norm"] + PL["norm2"], "norm2", b)

    for p in range(8):
        for t in range(T):
            odd = t % TPB == TPB - 1
            b = t // TPB
            if p in ATT:
                for stage in ("probsT", "query0", "queryT", "values", "exp", "sum", "outT", "scores", "xT", "project",
                              "query"):
                    if (stage, p) in PL:
                        put(p, t + PL[stage, p], stage, t)
                if not odd and p > 0:
                    put(p, t + PL["keys"], "keys", b)
                    put(p, t + PL["context"], "context", b)
                    put(p, t + PL["bias"], "bias", b)
                if not odd and p == 0 and b > 0:
                    put(p, t + PL["fold"], "fold", b)
                if odd:
                    finish(p, b, t + PL["finish", p])
            elif p == 1:
                for stage in ("xT", "hidden0", "tanh", "gated", "gatedT", "down0"):
                    put(p, t + PL[stage, p], stage, t)
                if odd:
                    put(p, t + PL["logits", p], "logits", b)
                    finish(p, b, t + PL["finish", p])
            elif p in (3, 7):
                put(p, t + PL["xT", p], "xT", t)
                if odd:
                    put(p, t + PL["logits", p], "logits", b)
                    for e in range(E):
                        put(p, t + e / 4, "hidden", (b, e))
                        put(p, t + (e + LAG) / 4 + 0.01, "expert", (b, e))
                    put(p, t + PL["gateT", p], "gateT", b)
                    put(p, t + PL["bias2", p], "bias2", b)
                    if p == 3:
                        finish(p, b, t + (E - 1 + LAG) / 4 + 0.02)
            else:
                put(p, t + PL["xT", p], "xT", t)
                if odd:
                    put(p, t + PL["mix"], "mix", b)
                put(p, t + PL["back", p], "back", t)
                if odd:
                    finish(p, b, t + PL["back", p] + 0.01)
                if t % 4 == 3:
                    half = t // 4
                    for e in range(E // 2):
                        put(p, t + PL["hidden5", p] + e * PL["step5"], "hidden5", E // 2 * half + e)
                        put(p, t + PL["expert5", p] + e * PL["step5"], "expert5", E // 2 * half + e)
                    put(p, t + PL["next5", p], "next5", half)
    for b, time in ((2, -2), (3, 0)):
        out.append((time + 0.8, len(out), "stats", -1, b))
        out.append((time + 0.85, len(out), "norm", -1, b))
    first = [("keys0", 0, g) for g in range(KV0)] + [("values0", 0, g) for g in range(KV0)] + [("fold", 0, 0)]
    return [("stats", -1, 0), ("stats", -1, 1), ("norm", -1, 0), ("norm", -1, 1)] + first + \
        [x[2:] for x in sorted(out)]


SCHEDULE = make_schedule()

JOBS = {
    "keys0": [("S", "keys0", "dve")], "values0": [("M", "values0", "act")],
    "xT": [("T", "xT", "act")], "query0": [("S", "query0", "dve")],
    "queryT": [("T", "queryT0", "act"), ("T", "queryT1", "act")], "query": [("M", "query", "act")],
    "scores": [("S", "scores", "dve")], "probsT": [("T", "probsT0", "act"), ("T", "probsT1", "act")],
    "fold": [("S", "fold", "act")], "values": [("M", "values", "dve")], "outT": [("T", "outT", "act")],
    "project": [("M", "project", "dve")], "logits": [("M", "logits", "dve")],
    "hidden0": [("S", "hidden0", "late")], "gatedT": [("T", "gatedT", "act")], "down0": [("M", "down0", "dve")],
    "gateT": [("T", "gateT", "act")], "bias2": [("M", "bias2", "dve")],
    "hidden": [("S", "hidden", "act")], "expert": [("M", "expert", "dve")],
    "mix": [("M", "mix", "act")], "hidden5": [("S", "hidden5", "act")], "expert5": [("M", "expert5", "act")],
    "next5": [("S", "next5", "act")], "back": [("T", "back", "dve")],
}


def jobs_of(stage, p, i):
    if stage == "keys":
        return [("M", "keys", "act")] if p in (4, 6) and i == 0 else []
    if stage == "context":
        return [("M", "ctxv", "act")] if p in (4, 6) else []
    return JOBS.get(stage, [])


class Ring:

    def __init__(self, name, slots, filled, emptied):
        self.slots, self.filled, self.emptied = slots, filled, emptied
        self.number, self.turn = {}, []
        for stage, p, i in SCHEDULE:
            for ring, job, reader in jobs_of(stage, p, i):
                if ring == name:
                    self.number[job, p, i] = len(self.turn)
                    self.turn.append((reader, 1 + sum(r == reader for r, _ in self.turn)))

    def slot(self, *job):
        return self.slots[self.number[job] % len(self.slots)]

    def full(self, *job):
        return self.filled, self.number[job] + 1

    def read(self, *job):
        reader, n = self.turn[self.number[job]]
        return self.emptied[reader], n

    def reused(self, *job):
        return self.number[job] >= len(self.slots)

    def vacated(self, *job):
        reader, n = self.turn[self.number[job] - len(self.slots)]
        return self.emptied[reader], n


class Mark:

    def __init__(self, sem, keys):
        self.sem, self.nth = sem, {k: n + 1 for n, k in enumerate(keys)}

    def at(self, *key):
        return self.sem, self.nth[key]


COLS = {"bq4": 0, "bk4": 1, "bq6": 2, "bk6": 3, "ln_scale": 4, "ln_bias": 5, "attn_b": 6, "next_b": 7,
        "b1_3": 8, "b1_5": 40, "b2_5": 72, "b1_7": 80}
NCOLS = 96
MATS = ["w2", "q4", "k4", "v4", "w4", "attn", "next", "q6", "k6", "v6", "w6", "gate1", "gate3", "gate7"]
ROWS = ["v4", "v6"]
XBIASES = ["b2", "b4", "b6"]
CONSTS = {"ident": (0, 128), "row0": (128, 128), "heads": (256, 16), "iota": (272, 8), "cosq": (280, 128),
          "sinq": (408, 128), "cosk": (536, 64), "sink": (600, 64)}
NCONST = 664


def build(nc, x, ctxT, ctx2, consts, cols, mats, rows, xbias, bias2, gbias, relpos, mask0, mask1, mask2,
          wq0, wk0, wk0r, wv0, wo0, wg0, wu0, wd0, w1_3, w2_3, w1_5, w2_5, w1_7, w2_7, out):
    with ExitStack() as ctx:
        def sb(name, shape, dt=F32):
            return ctx.enter_context(nc.sbuf_tensor(name, [P] + shape, dt))

        def sem(name):
            return ctx.enter_context(nc.semaphore(name))

        X = sb("X", [T, D])
        CST = sb("CST", [NCONST])
        COL = sb("COL", [NCOLS])
        MAT = sb("MAT", [len(MATS), P])
        ROW = sb("ROW", [len(ROWS), P])
        XBIAS = sb("XBIAS", [len(XBIASES), D])
        BIAS2 = sb("BIAS2", [2, P])
        GB = sb("GB", [2, E])
        CTXT = sb("CTXT", [B, 2, SK])
        CTX2 = sb("CTX2", [B, D])
        M0 = sb("M0", [B, SK], U8)
        M1 = sb("M1", [T, SK], I32)
        M2 = sb("M2", [B, SK], I32)
        FILL0 = sb("FILL0", [B, SK])
        FILL1, FILL2 = M1[:, :, :].bitcast(F32), M2[:, :, :].bitcast(F32)
        W1_3 = sb("W1_3", [E, HID[3]])
        W2_3 = sb("W2_3", [E, HID[3] // P, D])
        W0 = sb("W0", [4608])
        TAB0 = sb("TAB0", [8192])
        XN = sb("XN", [T, D])
        XT = sb("XT", [T, P])
        QT = sb("QT", [2, P])
        SM = sb("SM", [3, H, SK])
        PT = sb("PT", [2, NPAIR, P])
        KBD = sb("KBD", [2, H, SK])
        VEX = sb("VEX", [2, NPAIR, VX])
        KT = sb("KT", [B, SK])
        WORK = sb("WORK", [8704])
        HALF = sb("HALF", [4, 512])
        AO = sb("AO", [2, D])
        OT = sb("OT", [2, P])
        GATE = sb("GATE", [2, TPB, P])
        GSCALE = sb("GSCALE", [2, TPB])
        GT = sb("GT", [2, TPB, P])
        ST = sb("ST", [TPB, 6])
        MV = sb("MV", [3, TPB, 2])
        VAR = sb("VAR", [TPB])
        RS = sb("RS", [3, TPB])
        SQ2 = sb("SQ2", [TPB])
        HV = sb("HV", [TPB])
        MX = sb("MX", [3, H])
        SUM = sb("SUM", [2, H])
        RCP = sb("RCP", [2, H])
        LG = sb("LG", [TPB, E])
        TOP = sb("TOP", [TPB, E])
        IDX = sb("IDX", [TPB, E], U32)
        IDF = sb("IDF", [TPB, E])
        HOT = sb("HOT", [2, TPB, E])
        GV = sb("GV", [8, TPB])
        GE = sb("GE", [TPB, E])
        GE2 = sb("GE2", [TPB, E])

        def const(name):
            o, n = CONSTS[name]
            return CST[:, o:o + n]

        def col(name, k=0):
            o = COLS[name] + k
            return COL[:, o:o + 1]

        def mat(name):
            return MAT[:, MATS.index(name), :]

        def row(name):
            return ROW[:, ROWS.index(name), :]

        def diagonal(half, r, first, step, n):
            flat = VEX[half, r, :, :].rearrange("p c v -> p (c v)")
            return bass.AP(flat.tensor, flat.offset + first, [list(flat.ap[0]), [VX + step, NPAIR], [1, n]])

        IDENT, ROW0 = const("ident"), const("row0")
        HEADS = const("heads").unsqueeze(2).broadcast_to([P, H, SK])
        COSQ = const("cosq").rearrange("p (j d) -> p j d", j=TPB)
        SINQ = const("sinq").rearrange("p (j d) -> p j d", j=TPB)
        COSK = const("cosk").unsqueeze(1).broadcast_to([P, B, SK])
        SINK = const("sink").unsqueeze(1).broadcast_to([P, B, SK])

        WQ0, WO0 = W0[:, 0:1024], W0[:, 1024:2048].rearrange("p (c n) -> p c n", c=NPAIR)
        WK0 = W0[:, 2048:2560].rearrange("p (g d) -> p g d", g=KV0)
        WK0R = W0[:, 2560:3072].rearrange("p (g d) -> p g d", g=KV0)
        WG0, WU0 = W0[:, 3072:3584], W0[:, 3584:4096]
        WD0 = W0[:, 4096:4608].rearrange("p (c n) -> p c n", c=4)
        W1_7 = W0[:, 0:2048].rearrange("p (e f) -> p e f", e=E)
        W2_7 = W0[:, 2048:4096].rearrange("p (e c n) -> p e c n", e=E, c=2)
        REL = TAB0[:, 0:2048].rearrange("p (j h k) -> p j h k", j=TPB, h=H)
        RELM = TAB0[:, 2048:4096].rearrange("p (j h k) -> p j h k", j=2, h=H)
        KBD0 = TAB0[:, 4096:6144].rearrange("p (b g k) -> p b g k", b=B, g=KV0)
        VTD0 = TAB0[:, 6144:8192].rearrange("p (b g k) -> p b g k", b=B, g=KV0)
        W1_5 = TAB0[:, 0:4096].rearrange("p (e f) -> p e f", e=E)
        W2_5 = TAB0[:, 4096:8192].rearrange("p (e c n) -> p e c n", e=E, c=4)
        T1, T2 = WORK[:, 0:1024], WORK[:, 1024:2048]
        QR = WORK[:, 2048:4096].rearrange("p (r n) -> p r n", r=2)
        QT0 = WORK[:, 4096:5120].rearrange("p (c q) -> p c q", c=NPAIR)
        VW = WORK[:, 5120:7168].rearrange("p (r c n) -> p r c n", r=2, c=NPAIR)
        WV0 = WORK[:, 7168:7680].rearrange("p (g d) -> p g d", g=KV0)
        K1, K2 = WORK[:, 8192:8448], WORK[:, 8448:8704]
        HT = WORK[:, 0:3072].rearrange("p (r c q) -> p r c q", r=3, c=4)
        XAT = WORK[:, 2048:3072]
        EOT = WORK[:, 3072:4096]
        YT = WORK[:, 4096:5120]
        HT5 = WORK[:, 5120:6144].rearrange("p (r c q) -> p r c q", r=2, c=4)
        XN2 = WORK[:, 6144:7168].rearrange("p (t n) -> p t n", t=T)
        GP, UP = (WORK[:, 8192:8704], W0[:, 2048:2560]), (HALF[:, 0, :], W0[:, 2560:3072])
        TH, AT = (HALF[:, 1, :], HALF[:, 2, :]), HALF[:, 3, :]

        psS = [ctx.enter_context(nc.psum_tensor(f"psS{k}", [P, 1024], F32)) for k in range(2)]
        psT = [ctx.enter_context(nc.psum_tensor(f"psT{k}", [P, 512], F32)) for k in range(2)]
        psM = [ctx.enter_context(nc.psum_tensor(f"psM{k}", [P, 512], F32)) for k in range(2)]
        rings = {}
        for name, slots in (("S", psS), ("T", psT), ("M", psM)):
            rings[name] = Ring(name, slots, sem(f"filled_{name}"),
                               {who: sem(f"emptied_{name}_by_{who}") for who in ("act", "dve", "late")})
        S, TR, M = rings["S"], rings["T"], rings["M"]

        def staged(*names):
            return [(p, i) for s, p, i in SCHEDULE if s in names]

        normed = Mark(sem("normed"), [(p + 1, b) for s, p, b in SCHEDULE if s == ("norm2" if p == 4 else "norm")])
        variances = [(s, p, b) for s, p, b in SCHEDULE if s in ("stats", "stats2")]
        masked = Mark(sem("masked"), staged("scores"))
        shifted = Mark(sem("shifted"), staged("scores"))
        exped = Mark(sem("exped"), staged("exp"))
        summed = Mark(sem("summed"), staged("sum"))
        weighed = Mark(sem("weighed"), staged("sum"))
        biased = Mark(sem("biased"), staged("bias"))
        rotated = Mark(sem("rotated"), staged("query0"))
        relmasked = Mark(sem("relmasked"), staged("query0"))
        kbd_ready = Mark(sem("kbd_ready"), staged("keys"))
        vex_ready = Mark(sem("vex_ready"), [(p, b) for p, b in staged("context") if p == 2])
        keys0_ready = Mark(sem("keys0_ready"), staged("keys0"))
        gate_top = Mark(sem("gate_top"), staged("logits"))
        gate_exp = Mark(sem("gate_exp"), staged("logits"))
        gate_ready = Mark(sem("gate_ready"), staged("logits"))
        tanh_ready = Mark(sem("tanh_ready"), staged("tanh"))
        gated_ready = Mark(sem("gated_ready"), staged("gated"))
        zeroed_tables = sem("zeroed_tables")
        zeroed_rows = sem("zeroed_rows")
        zeroed_values = sem("zeroed_values")
        fills = sem("fills")
        stored = sem("stored")
        act_chain = sem("act_chain")
        dve_chain = sem("dve_chain")

        def pv(t):
            return t.rearrange("(a n) -> a n", a=1)

        loads = [
            ("x01", X[:, 0:4, :], x[:, 0:4, :]), ("consts", CST[:, :], consts), ("ctxT", CTXT[:, :, :, :], ctxT),
            ("wk0", WK0, wk0), ("wk0r", WK0R, wk0r), ("wq0", WQ0, wq0), ("wv0", WV0, wv0),
            ("mask0", M0[:, :, :], mask0), ("rel", REL, relpos), ("wo0", WO0, wo0), ("x23", X[:, 4:8, :], x[:, 4:8, :]),
            ("cols", COL[:, :], cols), ("mats", MAT[:, :, :], mats),
            ("wg0", WG0, wg0), ("wu0", WU0, wu0), ("wd0", WD0, wd0),
            ("ctx2", CTX2[:, :, :], ctx2), ("mask1", M1[:, :, :], mask1), ("mask2", M2[:, :, :], mask2),
            ("gbias", GB[:, :, :], gbias), ("xbias", XBIAS[:, :, :], xbias),
            ("rows", ROW[0:1, :, :], rows), ("bias2", BIAS2[0:E, :, :], bias2),
            ("w1_3", W1_3[:, :, :], w1_3), ("w2_3", W2_3[:, :, :, :], w2_3),
            ("w1_5", W1_5, w1_5), ("w2_5", W2_5, w2_5), ("w1_7", W1_7, w1_7), ("w2_7", W2_7, w2_7)]
        loaded = {name: sem(f"loaded_{name}") for name, _, _ in loads}

        block = ctx.enter_context(nc.Block())

        def group(t, e):
            return t.rearrange("p (f m g q) -> p f m g q", f=2, m=2, g=4)[:, e // 4, :, e % 4, :]

        @block.sync
        def _(sp):
            for name, dst, src in loads:
                if name == "rows":
                    sp.wait_ge(zeroed_rows, 2)
                if name == "w1_5":
                    sp.wait_ge(*S.full("fold", 0, B - 1))
                    sp.wait_ge(*masked.at(0, T - 1))
                    sp.wait_ge(*relmasked.at(0, T - 1))
                if name == "w1_7":
                    sp.wait_ge(*M.full("down0", 1, T - 1))
                sp.dma_start(dst, src).then_inc(loaded[name], 16)
            for b in range(B):
                sp.wait_ge(*M.read("expert", 7, (b, E - 1)))
                sp.dma_start(out[:, TPB * b:TPB * (b + 1), :], X[:, TPB * b:TPB * (b + 1), :]).then_inc(stored, 16)
            sp.wait_ge(stored, 16 * B)

        @block.tensor
        def _(pe):
            mm, tr = nc.tensor.matmul, nc.tensor.transpose

            def claim(ring, *job):
                if ring.reused(*job):
                    pe.wait_ge(*ring.vacated(*job))
                return ring.slot(*job)

            def load_wait(*names):
                for n in names:
                    pe.wait_ge(loaded[n], 16)

            for stage, p, i in SCHEDULE:
                if stage == "keys0":
                    if i == 0:
                        load_wait("ctxT", "wk0", "wk0r", "consts")
                    o = claim(S, "keys0", p, i)
                    for n, w in enumerate((WK0, WK0R)):
                        last = mm(o[:, 512 * n:512 * n + 256], w[:, i, :],
                                  CTXT[:, :, 0, :], start=True, stop=True)
                    last.then_inc(S.filled, 1)
                elif stage == "values0":
                    if i == 0:
                        load_wait("wv0")
                    o = claim(M, "values0", p, i)
                    mm(o[:, 0:256], WV0[:, i, :], CTXT[:, :, 0, :], start=True, stop=True).then_inc(M.filled, 1)
                elif stage == "fold":
                    if i == 0:
                        load_wait("wo0")
                        pe.wait_ge(*M.read("values0", p, KV0 - 1))
                    o = claim(S, "fold", p, i)
                    for c in range(NPAIR):
                        last = mm(o[:, c * P:c * P + P], VTD0[:, i, c // 2, :], WO0[:, c, :], start=True, stop=True)
                    last.then_inc(S.filled, 1)
                elif stage == "xT":
                    pe.wait_ge(*normed.at(p, i // TPB))
                    o = claim(TR, "xT", p, i)
                    src = XN2 if p == 5 else XN
                    tr(o[:, 0:P], src[:, i, :], IDENT).then_inc(TR.filled, 1)
                elif stage == "query0":
                    if i == 0:
                        load_wait("wq0")
                    o = claim(S, "query0", p, i)
                    pe.wait_ge(*TR.read("xT", p, i))
                    for n in range(2):
                        last = mm(o[:, 512 * n:512 * n + 512], XT[:, i, :], WQ0[:, 512 * n:512 * n + 512],
                                  start=True, stop=True)
                    last.then_inc(S.filled, 1)
                elif stage == "queryT":
                    pe.wait_ge(*rotated.at(p, i))
                    for n in range(2):
                        o = claim(TR, f"queryT{n}", p, i)
                        for c in range(4):
                            last = tr(o[:, c * P:c * P + P], QR[:, i % 2, (4 * n + c) * P:(4 * n + c + 1) * P], IDENT)
                        last.then_inc(TR.filled, 1)
                elif stage == "query":
                    if p == 4 and i == 0:
                        load_wait("mats")
                    o = claim(M, "query", p, i)
                    pe.wait_ge(*TR.read("xT", p, i))
                    mm(o[:, 0:P], mat(f"q{p}"), XT[:, i, :], start=True, stop=True).then_inc(M.filled, 1)
                elif stage == "scores":
                    b = i // TPB
                    o = claim(S, "scores", p, i)
                    if p == 0:
                        if i == 0:
                            pe.wait_ge(*keys0_ready.at(0, KV0 - 1))
                        pe.wait_ge(*TR.read("queryT1", p, i))
                        for c in range(NPAIR):
                            last = mm(o[:, c * P:c * P + P], QT0[:, c, :], KBD0[:, b, c // 2, :],
                                      start=True, stop=True)
                    else:
                        if p == 2:
                            pe.wait_ge(*TR.read("xT", p, i))
                            q = XT[:, i, :]
                        else:
                            pe.wait_ge(*M.read("query", p, i))
                            q = QT[:, i % 2, :]
                        pe.wait_ge(*kbd_ready.at(p, b))
                        for n in range(2):
                            last = mm(o[:, 512 * n:512 * n + 512], q, KBD[:, b % 2, 8 * n:8 * n + 8, :],
                                      start=True, stop=True)
                    last.then_inc(S.filled, 1)
                elif stage == "probsT":
                    pe.wait_ge(*(weighed if p == 0 else exped).at(p, i))
                    a = ATT.index(p) * T + i
                    for n in range(2):
                        o = claim(TR, f"probsT{n}", p, i)
                        for c in range(4):
                            pair = 4 * n + c
                            last = tr(o[:, c * P:c * P + P],
                                      SM[:, a % 3, 2 * pair:2 * pair + 2, :].rearrange("p h k -> p (h k)"), IDENT)
                        last.then_inc(TR.filled, 1)
                elif stage == "values":
                    b = i // TPB
                    a = ATT.index(p) * T + i
                    o = claim(M, "values", p, i)
                    if i % TPB == 0:
                        pe.wait_ge(*(S.read("fold", p, b) if p == 0 else vex_ready.at(p, b) if p == 2 else
                                     M.read("ctxv", p, b)))
                    for c in range(NPAIR):
                        if c % 4 == 0:
                            pe.wait_ge(*TR.read(f"probsT{c // 4}", p, i))
                        if p == 0:
                            last = mm(o[:, 0:D], PT[:, a % 2, c, :], VW[:, b % 2, c, :],
                                      start=(c == 0), stop=(c == NPAIR - 1))
                        else:
                            last = mm(o[:, 0:VX], PT[:, a % 2, c, :], VEX[:, b % 2, c, :],
                                      start=(c == 0), stop=(c == NPAIR - 1))
                    last.then_inc(M.filled, 1)
                elif stage == "outT":
                    pe.wait_ge(*M.read("values", p, i))
                    o = claim(TR, "outT", p, i)
                    tr(o[:, 0:P], AO[:, i % 2, :], IDENT).then_inc(TR.filled, 1)
                elif stage == "project":
                    if p == 2 and i == 0:
                        load_wait("mats")
                    o = claim(M, "project", p, i)
                    pe.wait_ge(*TR.read("outT", p, i))
                    mm(o[:, 0:D], OT[:, i % 2, :], mat(f"w{p}"), start=True, stop=True).then_inc(M.filled, 1)
                elif stage == "keys" and p in (4, 6) and i == 0:
                    o = claim(M, "keys", p, i)
                    mm(o[:, 0:256], mat(f"k{p}"), CTXT[:, :, 0, :], start=True, stop=True).then_inc(M.filled, 1)
                elif stage == "context" and p in (4, 6):
                    if p == 4 and i == 0:
                        load_wait("mats", "rows")
                    o = claim(M, "ctxv", p, i)
                    mm(o[:, 0:D], CTXT[:, i, :, :].rearrange("p h k -> p (h k)"), mat(f"v{p}"),
                       start=True, stop=False)
                    mm(o[:, 0:D], ROW0, row(f"v{p}"), start=False, stop=True).then_inc(M.filled, 1)
                elif stage == "logits":
                    if p == 1 and i == 0:
                        load_wait("mats")
                    o = claim(M, "logits", p, i)
                    pe.wait_ge(*TR.read("xT", p, TPB * i + 1))
                    for j in range(TPB):
                        last = mm(o[:, j * P:j * P + P], XT[:, TPB * i + j, :], mat(f"gate{p}"), start=True, stop=True)
                    last.then_inc(M.filled, 1)
                elif stage == "hidden0":
                    if i == 0:
                        load_wait("wg0", "wu0")
                    o = claim(S, "hidden0", p, i)
                    for n, w in enumerate((WG0, WU0)):
                        last = mm(o[:, 512 * n:512 * n + 512], XT[:, i, :], w, start=True, stop=True)
                    last.then_inc(S.filled, 1)
                elif stage == "gatedT":
                    pe.wait_ge(*gated_ready.at(p, i))
                    o = claim(TR, "gatedT", p, i)
                    for c in range(4):
                        last = tr(o[:, c * P:c * P + P], TH[i % 2][:, c * P:c * P + P], IDENT)
                    last.then_inc(TR.filled, 1)
                elif stage == "down0":
                    if i == 0:
                        load_wait("wd0")
                    o = claim(M, "down0", p, i)
                    pe.wait_ge(*TR.read("gatedT", p, i))
                    for c in range(4):
                        last = mm(o[:, 0:D], AT[:, c * P:c * P + P], WD0[:, c, :], start=(c == 0), stop=(c == 3))
                    last.then_inc(M.filled, 1)
                elif stage == "gateT":
                    pe.wait_ge(*gate_ready.at(p, i))
                    o = claim(TR, "gateT", p, i)
                    for j in range(TPB):
                        last = tr(o[:, j * P:j * P + P], GATE[:, i % 2, j, :], IDENT)
                    last.then_inc(TR.filled, 1)
                elif stage == "bias2":
                    if i == 0:
                        load_wait("bias2")
                    o = claim(M, "bias2", p, i)
                    pe.wait_ge(*TR.read("gateT", p, i))
                    for j in range(TPB):
                        last = mm(o[:, j * D:j * D + D], GT[:, i % 2, j, :], BIAS2[:, (3, 7).index(p), :],
                                  start=True, stop=True)
                    last.then_inc(M.filled, 1)
                elif stage == "hidden":
                    b, e = i
                    if b == 0 and e == 0:
                        load_wait(f"w1_{p}")
                    o = claim(S, "hidden", p, i)
                    if e == 0:
                        pe.wait_ge(*TR.read("xT", p, TPB * b + 1))
                    xt = XT[:, TPB * b:TPB * b + TPB, :]
                    w = W1_3 if p == 3 else W1_7
                    for c in range(HID[p] // P):
                        last = mm(o[:, 256 * c:256 * c + 256], w[:, e, c * P:c * P + P], xt, start=True, stop=True)
                    last.then_inc(S.filled, 1)
                elif stage == "expert":
                    b, e = i
                    if b == 0 and e == 0:
                        load_wait(f"w2_{p}")
                    o = claim(M, "expert", p, i)
                    pe.wait_ge(*S.read("hidden", p, i))
                    w = W2_3 if p == 3 else W2_7
                    nc_ = HID[p] // P
                    for j in range(TPB):
                        for c in range(nc_):
                            last = mm(o[:, j * D:j * D + D], HT[:, (b * E + e) % 3, c, j * P:j * P + P], w[:, e, c, :],
                                      start=(c == 0), stop=(c == nc_ - 1))
                    last.then_inc(M.filled, 1)
                elif stage == "mix":
                    o = claim(M, "mix", p, i)
                    t = TPB * i
                    pe.wait_ge(*TR.read("xT", p, t + 1))
                    mm(o[:, 0:256], mat("attn"), XT[:, t:t + TPB, :], start=True, stop=False)
                    for j in range(TPB):
                        last = mm(o[:, j * P:j * P + P], XN[:, t + j, :], IDENT, start=False, stop=(j == 1))
                    last.then_inc(M.filled, 1)
                elif stage == "hidden5":
                    if i == 0:
                        load_wait("w1_5")
                    if i % 4 == 0:
                        pe.wait_ge(*M.read("mix", p, i // 2 + 1))
                    o = claim(S, "hidden5", p, i)
                    xa = group(XAT, i)
                    for c in range(4):
                        last = mm(o[:, c * P:c * P + P], W1_5[:, i, c * P:c * P + P], xa, start=True, stop=True)
                    last.then_inc(S.filled, 1)
                elif stage == "expert5":
                    if i == 0:
                        load_wait("w2_5")
                    o = claim(M, "expert5", p, i)
                    pe.wait_ge(*S.read("hidden5", p, i))
                    for c in range(4):
                        last = mm(o[:, 0:P], W2_5[:, i, c, :], HT5[:, i % 2, c, :], start=(c == 0), stop=(c == 3))
                    last.then_inc(M.filled, 1)
                elif stage == "next5":
                    o = claim(S, "next5", p, i)
                    pe.wait_ge(*M.read("expert5", p, E // 2 * i + 3))
                    mm(o[:, 0:512], mat("next"), EOT[:, 512 * i:512 * i + 512], start=True, stop=True)\
                        .then_inc(S.filled, 1)
                elif stage == "back":
                    o = claim(TR, "back", p, i)
                    pe.wait_ge(*S.read("next5", p, i // 4))
                    tr(o[:, 0:P], YT[:, i * P:i * P + P], IDENT).then_inc(TR.filled, 1)

        @block.scalar
        def _(act):
            def run(out_, in_, func, bias=0.0, scale=1.0):
                return nc.scalar.activation(out_, in_, func, bias=bias, scale=scale)

            for stage, p, i in SCHEDULE:
                if stage == "values0":
                    act.wait_ge(*M.full("values0", p, i))
                    if i == 0:
                        act.wait_ge(zeroed_tables, 2)
                    ps = M.slot("values0", p, i)
                    for h in range(2):
                        last = run(VTD0[64 * h:64 * h + 64, :, i, 64 * h:64 * h + 64],
                                   ps[64 * h:64 * h + 64, 0:256].rearrange("p (b k) -> p b k", b=B), ACT.Copy)
                        if h == 0:
                            last.then_inc(act_chain, 1)
                    last.then_inc(M.emptied["act"], 1)
                elif stage == "fold":
                    act.wait_ge(*S.full("fold", p, i))
                    if i >= 2:
                        act.wait_ge(*M.full("values", p, TPB * (i - 2) + 1))
                    run(VW[:, i % 2, :, :].rearrange("p c n -> p (c n)"), S.slot("fold", p, i)[:, :], ACT.Copy)\
                        .then_inc(S.emptied["act"], 1)
                elif stage == "xT":
                    act.wait_ge(*TR.full("xT", p, i))
                    ps = TR.slot("xT", p, i)[:, 0:P]
                    if p == 5:
                        if i == 0:
                            act.wait_ge(loaded["cols"], 16)
                        ins = run(XT[:, i, :], ps, ACT.Identity, bias=col("ln_bias"), scale=col("ln_scale"))
                    else:
                        ins = run(XT[:, i, :], ps, ACT.Copy)
                    ins.then_inc(TR.emptied["act"], 1)
                elif stage == "queryT":
                    if i > 0:
                        act.wait_ge(*S.full("scores", p, i - 1))
                    for n in range(2):
                        act.wait_ge(*TR.full(f"queryT{n}", p, i))
                        run(QT0[:, 4 * n:4 * n + 4, :].rearrange("p c q -> p (c q)"), TR.slot(f"queryT{n}", p, i)[:, :],
                            ACT.Copy).then_inc(TR.emptied["act"], 1)
                elif stage == "query":
                    act.wait_ge(*M.full("query", p, i))
                    if p == 4 and i == 0:
                        act.wait_ge(loaded["cols"], 16)
                    if i >= 2:
                        act.wait_ge(*S.full("scores", p, i - 2))
                    elif p == 6:
                        act.wait_ge(*S.full("scores", 4, T - 2 + i))
                    run(QT[:, i % 2, :], M.slot("query", p, i)[:, 0:P], ACT.Identity, bias=col(f"bq{p}"))\
                        .then_inc(M.emptied["act"], 1)
                elif stage == "exp":
                    a = ATT.index(p) * T + i
                    act.wait_ge(*shifted.at(p, i))
                    scale = {0: 1.0, 2: 1.0 / float(np.sqrt(np.float32(D))), 4: 1.0 / float(np.sqrt(np.float32(DH))),
                             6: 1.0 / float(np.sqrt(np.float32(DH)))}[p]
                    run(SM[:, a % 3, :, :], SM[:, a % 3, :, :], ACT.Exp, scale=scale).then_inc(exped.sem, 1)
                elif stage == "probsT":
                    a = ATT.index(p) * T + i
                    if a >= 2:
                        q, t = (p, i - 2) if i >= 2 else (ATT[ATT.index(p) - 1], T - 2 + i)
                        act.wait_ge(*M.full("values", q, t))
                    for n in range(2):
                        act.wait_ge(*TR.full(f"probsT{n}", p, i))
                        run(PT[:, a % 2, 4 * n:4 * n + 4, :].rearrange("p c q -> p (c q)"),
                            TR.slot(f"probsT{n}", p, i)[:, :], ACT.Copy).then_inc(TR.emptied["act"], 1)
                elif stage == "outT":
                    act.wait_ge(*TR.full("outT", p, i))
                    if i >= 2:
                        act.wait_ge(*M.full("project", p, i - 2))
                    run(OT[:, i % 2, :], TR.slot("outT", p, i)[:, 0:P], ACT.Copy).then_inc(TR.emptied["act"], 1)
                elif stage == "keys" and p in (4, 6) and i == 0:
                    if p == 4:
                        act.wait_ge(loaded["cols"], 16)
                    act.wait_ge(*M.full("keys", p, i))
                    if p == 6:
                        act.wait_ge(*kbd_ready.at(4, B - 1))
                    run(KT[:, :, :].rearrange("p b k -> p (b k)"), M.slot("keys", p, i)[:, 0:256],
                        ACT.Identity, bias=col(f"bk{p}")).then_inc(M.emptied["act"], 1)
                elif stage == "context":
                    b = i
                    if p == 2 and b == 0:
                        act.wait_ge(zeroed_values, 5)
                        act.wait_ge(loaded["ctx2"], 16)
                    if b >= 2 or p > 2:
                        q, c = (p, b - 2) if b >= 2 else (p - 2, b + 2)
                        act.wait_ge(*M.full("values", q, TPB * c + 1))
                    if p in (4, 6):
                        act.wait_ge(*M.full("ctxv", p, b))
                    for h in range(2):
                        half = slice(64 * h, 64 * h + 64)
                        src = CTX2[half, b, :] if p == 2 else M.slot("ctxv", p, b)[half, 0:D]
                        ins = run(diagonal(half, b % 2, DH * h, 2 * DH, DH),
                                  src.rearrange("p (c h d) -> p c h d", h=2, d=DH)[:, :, h, :], ACT.Copy)
                        if h == 0:
                            ins.then_inc(act_chain, 1)
                        elif p == 2:
                            ins.then_inc(vex_ready.sem, 1)
                        else:
                            ins.then_inc(M.emptied["act"], 1)
                elif stage == "logits":
                    act.wait_ge(*gate_top.at(p, i))
                    if p == 1:
                        ins = run(GV[:, 1, :], TOP[:, :, 0], ACT.Tanh, scale=0.5)
                    elif p == 3:
                        ins = run(GE[:, :, :], LG[:, :, :], ACT.Tanh, scale=0.5)
                    else:
                        ins = run(GV[:, 1, :], GV[:, 0, :], ACT.Exp)
                    ins.then_inc(gate_exp.sem, 1)
                elif stage == "tanh":
                    b, j = i // TPB, i % TPB
                    act.wait_ge(*S.full("hidden0", p, i))
                    act.wait_ge(*gate_ready.at(p, b))
                    if i >= 2:
                        act.wait_ge(*TR.full("gatedT", p, i - 2))
                    run(TH[i % 2], S.slot("hidden0", p, i)[:, 0:512], ACT.Tanh,
                        scale=GSCALE[:, b % 2, j:j + 1]).then_inc(tanh_ready.sem, 1)
                elif stage == "gatedT":
                    act.wait_ge(*TR.full("gatedT", p, i))
                    if i > 0:
                        act.wait_ge(*M.full("down0", p, i - 1))
                    run(AT, TR.slot("gatedT", p, i)[:, :], ACT.Copy).then_inc(TR.emptied["act"], 1)
                elif stage == "gateT":
                    act.wait_ge(*TR.full("gateT", p, i))
                    if i >= 2:
                        act.wait_ge(*M.full("bias2", p, i - 2))
                    elif p == 7:
                        act.wait_ge(*M.full("bias2", 3, B - 2 + i))
                    run(GT[:, i % 2, :, :].rearrange("p j q -> p (j q)"), TR.slot("gateT", p, i)[:, 0:TPB * P],
                        ACT.Copy).then_inc(TR.emptied["act"], 1)
                elif stage == "hidden":
                    b, e = i
                    if (p, b, e) == (3, 0, 0):
                        act.wait_ge(loaded["cols"], 16)
                    act.wait_ge(*S.full("hidden", p, i))
                    if b > 0 or e >= 3:
                        n = b * E + e - 3
                        act.wait_ge(*M.full("expert", p, (n // E, n % E)))
                    elif p == 3:
                        act.wait_ge(*M.full("values", 0, T - 1))
                    for c in range(HID[p] // P):
                        ins = run(HT[:, (b * E + e) % 3, c, :], S.slot("hidden", p, i)[:, 256 * c:256 * c + 256],
                                  ACT.Silu if p == 3 else ACT.Relu,
                                  bias=col(f"b1_{p}", e * (HID[p] // P) + c))
                        if c < HID[p] // P - 1:
                            ins.then_inc(act_chain, 1)
                    ins.then_inc(S.emptied["act"], 1)
                elif stage == "mix":
                    act.wait_ge(*M.full("mix", p, i))
                    run(XAT[:, 256 * i:256 * i + 256], M.slot("mix", p, i)[:, 0:256], ACT.Identity,
                        bias=col("attn_b")).then_inc(M.emptied["act"], 1)
                elif stage == "hidden5":
                    act.wait_ge(*S.full("hidden5", p, i))
                    if i >= 2:
                        act.wait_ge(*M.full("expert5", p, i - 2))
                    for c in range(4):
                        ins = run(HT5[:, i % 2, c, :], S.slot("hidden5", p, i)[:, c * P:c * P + P], ACT.Gelu,
                                  bias=col("b1_5", 4 * i + c))
                        if c < 3:
                            ins.then_inc(act_chain, 1)
                    ins.then_inc(S.emptied["act"], 1)
                elif stage == "expert5":
                    act.wait_ge(*M.full("expert5", p, i))
                    run(group(EOT, i),
                        M.slot("expert5", p, i)[:, 0:P].rearrange("p (m q) -> p m q", m=2), ACT.Identity,
                        bias=col("b2_5", i)).then_inc(M.emptied["act"], 1)
                elif stage == "next5":
                    act.wait_ge(*S.full("next5", p, i))
                    run(YT[:, 512 * i:512 * i + 512], S.slot("next5", p, i)[:, 0:512], ACT.Gelu,
                        bias=col("next_b")).then_inc(S.emptied["act"], 1)

        @block.vector
        def _(dve):
            v = nc.vector
            steps = [0]

            def mark(ins):
                steps[0] += 1
                ins.then_inc(dve_chain, 1)

            def settle():
                dve.wait_ge(dve_chain, steps[0])

            def step(ins):
                mark(ins)
                settle()

            def sure(ins, sem_, n):
                ins.then_inc(sem_, 1)
                dve.wait_ge(sem_, n)

            def rsqrt(rs, variance):
                step(v.tensor_scalar(VAR[:, :], variance, EPS, None, ALU.add))
                step(v.tensor_scalar(rs.bitcast(I32), VAR[:, :].bitcast(I32), -0.5, RSQRT_SEED, ALU.mult, ALU.add))
                step(v.tensor_tensor(SQ2[:, :], rs, rs, ALU.mult))
                step(v.scalar_tensor_tensor(HV[:, :], SQ2[:, :], -0.5, VAR[:, :], ALU.mult, ALU.mult))
                step(v.scalar_tensor_tensor(rs, HV[:, :], 1.5, rs, ALU.add, ALU.mult))
                step(v.tensor_tensor(SQ2[:, :], rs, rs, ALU.mult))
                step(v.tensor_tensor(HV[:, :], SQ2[:, :], VAR[:, :], ALU.mult))
                step(v.tensor_scalar(SQ2[:, :], HV[:, :], 0.375, -1.25, ALU.mult, ALU.add))
                step(v.tensor_tensor(HV[:, :], SQ2[:, :], HV[:, :], ALU.mult))
                step(v.scalar_tensor_tensor(rs, HV[:, :], 1.875, rs, ALU.add, ALU.mult))

            def gate(p, b):
                dve.wait_ge(*M.full("logits", p, b))
                ps = M.slot("logits", p, b)[:, 0:TPB * P].rearrange("p (j n) -> p j n", j=TPB)[:, :, 0:E]
                if p == 1:
                    sure(v.tensor_copy(LG[:, :, :], ps), *M.read("logits", p, b))
                else:
                    if b == 0:
                        dve.wait_ge(loaded["gbias"], 16)
                    bias = GB[:, (3, 7).index(p), :].unsqueeze(1).broadcast_to([P, TPB, E])
                    sure(v.tensor_tensor(LG[:, :, :], ps, bias, ALU.add), *M.read("logits", p, b))
                for j in range(TPB):
                    mark(v.max(TOP[:, j, :], LG[:, j, :]))
                settle()
                for j in range(TPB):
                    mark(v.max_index(IDX[:, j, :], TOP[:, j, :], LG[:, j, :]))
                settle()
                if p == 3:
                    sure(v.tensor_tensor(LG[:, :, :], LG[:, :, :], TOP[:, :, 0:1].broadcast_to([P, TPB, E]),
                                         ALU.subtract), *gate_top.at(p, b))
                elif p == 7:
                    sure(v.tensor_tensor(GV[:, 0, :], TOP[:, :, 1], TOP[:, :, 0], ALU.subtract), *gate_top.at(p, b))
                if p == 1:
                    sure(v.tensor_copy(IDF[:, :, :], IDX[:, :, :]), *gate_top.at(p, b))
                else:
                    step(v.tensor_copy(IDF[:, :, :], IDX[:, :, :]))
                for n in range(2 if p == 7 else 1):
                    mark(v.tensor_tensor(HOT[:, n, :, :], const("iota").unsqueeze(1).broadcast_to([P, TPB, E]),
                                         IDF[:, :, n:n + 1].broadcast_to([P, TPB, E]), ALU.is_equal))
                settle()
                dve.wait_ge(*gate_exp.at(p, b))
                if b >= 2 and p > 1:
                    dve.wait_ge(*TR.full("gateT", p, b - 2))
                out_ = GATE[:, b % 2, :, 0:E]

                def wide(k):
                    return GV[:, k, :].unsqueeze(2).broadcast_to([P, TPB, E])
                if p == 1:
                    if b >= 2:
                        dve.wait_ge(*tanh_ready.at(p, TPB * (b - 2) + 1))
                    step(v.tensor_scalar(GSCALE[:, b % 2, :], GV[:, 1, :], 1.0, 0.25, ALU.add, ALU.mult))
                    step(v.scalar_tensor_tensor(GV[:, 2, :], GSCALE[:, b % 2, :], 2.0, GSCALE[:, b % 2, :],
                                                ALU.mult, ALU.mult))
                    sure(v.tensor_tensor(out_, HOT[:, 0, :, :], wide(2), ALU.mult), *gate_ready.at(p, b))
                elif p == 3:
                    step(v.tensor_scalar(GE2[:, :, :], GE[:, :, :], -1.0, 1.0, ALU.mult, ALU.add))
                    step(v.reciprocal(GE2[:, :, :], GE2[:, :, :]))
                    step(v.scalar_tensor_tensor(GE[:, :, :], GE[:, :, :], 1.0, GE2[:, :, :], ALU.add, ALU.mult))
                    step(v.tensor_reduce(GV[:, 0, :], GE[:, :, :], X_AXIS, ALU.add))
                    step(v.reciprocal(GV[:, 1, :], GV[:, 0, :]))
                    sure(v.tensor_tensor(out_, HOT[:, 0, :, :], wide(1), ALU.mult), *gate_ready.at(p, b))
                else:
                    step(v.tensor_scalar(GV[:, 2, :], GV[:, 1, :], 1.0, None, ALU.add))
                    step(v.reciprocal(GV[:, 3, :], GV[:, 2, :]))
                    mark(v.tensor_tensor(GE[:, :, :], HOT[:, 0, :, :], wide(3), ALU.mult))
                    step(v.tensor_tensor(GV[:, 4, :], GV[:, 1, :], GV[:, 3, :], ALU.mult))
                    step(v.tensor_tensor(GE2[:, :, :], HOT[:, 1, :, :], wide(4), ALU.mult))
                    sure(v.tensor_tensor(out_, GE2[:, :, :], GE[:, :, :], ALU.add), *gate_ready.at(p, b))

            def add_to_x(ring, job, p, i, t):
                dve.wait_ge(*ring.full(job, p, i))
                sure(v.tensor_tensor(X[:, t, :], ring.slot(job, p, i)[:, 0:D], X[:, t, :], ALU.add),
                     *ring.read(job, p, i))

            step(v.memset(GATE[:, :, :, :], 0.0))

            for stage, p, i in SCHEDULE:
                if stage in ("stats", "stats2"):
                    n = variances.index((stage, p, i))
                    if p == -1:
                        dve.wait_ge(loaded["x01" if i < 2 else "x23"], 16)
                    src = X if stage == "stats" else XN
                    for j in range(TPB):
                        mark(v.bn_stats(ST[:, j, :], src[:, TPB * i + j, :]))
                    settle()
                    for j in range(TPB):
                        mark(v.bn_aggr(MV[:, n % 3, j, :], ST[:, j, :]))
                    settle()
                    rsqrt(RS[:, n % 3, :], MV[:, n % 3, :, 1])
                elif stage in ("norm", "norm2"):
                    stats = "stats" if stage == "norm" else "stats2"
                    n = variances.index((stats, p, i)) % 3
                    src, dst = (X, XN) if stage == "norm" else (XN, XN2)
                    for j in range(TPB):
                        t = TPB * i + j
                        ins = v.tensor_scalar(dst[:, t, :], src[:, t, :], MV[:, n, j, 0:1], RS[:, n, j:j + 1],
                                              ALU.subtract, ALU.mult)
                        if j < TPB - 1 or (p == 4 and stage == "norm"):
                            mark(ins)
                    if p == 4 and stage == "norm":
                        settle()
                    else:
                        sure(ins, *normed.at(p + 1, i))
                elif stage == "keys0":
                    dve.wait_ge(*S.full("keys0", p, i))
                    if i == 0:
                        dve.wait_ge(loaded["consts"], 16)
                        dve.wait_ge(zeroed_tables, 2)
                    ps = S.slot("keys0", p, i)
                    step(v.tensor_tensor(K1.rearrange("p (b k) -> p b k", b=B),
                                         ps[:, 0:256].rearrange("p (b k) -> p b k", b=B), COSK, ALU.mult))
                    sure(v.tensor_tensor(K2.rearrange("p (b k) -> p b k", b=B),
                                         ps[:, 512:768].rearrange("p (b k) -> p b k", b=B), SINK, ALU.mult),
                         *S.read("keys0", p, i))
                    for h in range(2):
                        half = slice(64 * h, 64 * h + 64)
                        ins = v.tensor_tensor(KBD0[half, :, i, 64 * h:64 * h + 64],
                                              K1[half, :].rearrange("p (b k) -> p b k", b=B),
                                              K2[half, :].rearrange("p (b k) -> p b k", b=B), ALU.add)
                        if h == 0:
                            step(ins)
                    sure(ins, *keys0_ready.at(p, i))
                    if i == KV0 - 1:
                        dve.wait_ge(loaded["mask0"], 16)
                        sure(v.tensor_scalar(FILL0[:, :, :], M0[:, :, :], 0.0, FILL, ALU.is_equal, ALU.mult), fills, 1)
                elif stage == "query0":
                    j = i % TPB
                    dve.wait_ge(*S.full("query0", p, i))
                    if i > 0:
                        dve.wait_ge(*rotated.at(p, i - 1))
                    ps = S.slot("query0", p, i)[:, :].rearrange("p (h d) -> p h d", h=H)
                    t1, t2 = (t.rearrange("p (h d) -> p h d", h=H) for t in (T1, T2))

                    def table(t, lo, hi):
                        return t[:, j, lo:hi].unsqueeze(1).broadcast_to([P, H, hi - lo])
                    step(v.tensor_tensor(t1, ps, table(COSQ, 0, D0), ALU.mult))
                    step(v.tensor_tensor(t2[:, :, 0:32], ps[:, :, 32:64], table(SINQ, 0, 32), ALU.mult))
                    sure(v.tensor_tensor(t2[:, :, 32:64], ps[:, :, 0:32], table(SINQ, 32, 64), ALU.mult),
                         *S.read("query0", p, i))
                elif stage == "scores":
                    a = ATT.index(p) * T + i
                    b = i // TPB
                    dve.wait_ge(*S.full("scores", p, i))
                    if a >= 3:
                        q, t = (p, i - 3) if i >= 3 else (ATT[ATT.index(p) - 1], T - 3 + i)
                        dve.wait_ge(*TR.full("probsT1", q, t))
                    ps = S.slot("scores", p, i)[:, :].rearrange("p (h k) -> p h k", h=H)
                    sm = SM[:, a % 3, :, :]
                    if p == 0:
                        dve.wait_ge(*relmasked.at(p, i))
                        sure(v.scalar_tensor_tensor(sm, ps, float(D0) ** -0.5, RELM[:, i % 2, :, :],
                                                    ALU.mult, ALU.add), *S.read("scores", p, i))
                    else:
                        fill = FILL2[:, b, :] if p == 4 else FILL1[:, i, :]
                        sure(v.tensor_tensor(sm, ps, fill.unsqueeze(1).broadcast_to([P, H, SK]), ALU.add),
                             *S.read("scores", p, i))
                    sure(v.tensor_reduce(MX[:, a % 3, :], sm, X_AXIS, ALU.max), *masked.at(p, i))
                elif stage == "sum":
                    a = ATT.index(p) * T + i
                    dve.wait_ge(*exped.at(p, i))
                    if i >= 2:
                        dve.wait_ge(*weighed.at(p, i - 2))
                    step(v.tensor_reduce(SUM[:, i % 2, :], SM[:, a % 3, :, :], X_AXIS, ALU.add))
                    sure(v.reciprocal(RCP[:, i % 2, :], SUM[:, i % 2, :]), *summed.at(p, i))
                elif stage == "values" and p == 0:
                    add_to_x(M, "values", p, i, i)
                    if i == 0:
                        dve.wait_ge(loaded["mask1"], 16)
                        dve.wait_ge(loaded["mask2"], 16)
                        step(v.tensor_scalar(FILL1, M1[:, :, :], 0.0, FILL, ALU.is_equal, ALU.mult))
                        step(v.tensor_scalar(FILL2, M2[:, :, :], 0.0, FILL, ALU.is_equal, ALU.mult))
                elif stage == "values":
                    k = i % 2
                    if p == 2 and i < 2:
                        dve.wait_ge(*weighed.at(0, T - 2 + i))
                    dve.wait_ge(*M.full("values", p, i))
                    ps = M.slot("values", p, i)
                    step(v.reciprocal(RCP[:, k, :], ps[:, D:VX]))
                    if i >= 2:
                        dve.wait_ge(*TR.full("outT", p, i - 2))
                    sure(v.tensor_tensor(AO[:, k, :].rearrange("p (h d) -> p h d", h=H),
                                         ps[:, 0:D].rearrange("p (h d) -> p h d", h=H),
                                         RCP[:, k, :].unsqueeze(2).broadcast_to([P, H, DH]), ALU.mult),
                         *M.read("values", p, i))
                elif stage == "project":
                    if i % TPB == 0:
                        dve.wait_ge(*biased.at(p, i // TPB))
                    add_to_x(M, "project", p, i, i)
                elif stage == "logits":
                    gate(p, i)
                elif stage == "tanh":
                    b, j = i // TPB, i % TPB
                    dve.wait_ge(*S.full("hidden0", p, i))
                    if i >= 2:
                        dve.wait_ge(*gated_ready.at(p, i - 2))
                    step(v.tensor_tensor(UP[i % 2].rearrange("p (e f) -> p e f", e=E),
                                         S.slot("hidden0", p, i)[:, 512:1024].rearrange("p (e f) -> p e f", e=E),
                                         GATE[:, b % 2, j, 0:E].unsqueeze(2).broadcast_to([P, E, I0]), ALU.mult))
                elif stage == "gated":
                    dve.wait_ge(*tanh_ready.at(p, i))
                    sure(v.scalar_tensor_tensor(GP[i % 2], TH[i % 2], 1.0, S.slot("hidden0", p, i)[:, 0:512],
                                                ALU.add, ALU.mult), *S.read("hidden0", p, i))
                elif stage == "down0":
                    add_to_x(M, "down0", p, i, i)
                elif stage == "bias2":
                    dve.wait_ge(*M.full("bias2", p, i))
                    both = X[:, TPB * i:TPB * i + TPB, :]
                    sure(v.tensor_tensor(both, M.slot("bias2", p, i)[:, 0:TPB * D].rearrange("p (j d) -> p j d", j=TPB),
                                         both, ALU.add), *M.read("bias2", p, i))
                elif stage == "expert":
                    b, e = i
                    dve.wait_ge(*M.full("expert", p, i))
                    for j in range(TPB):
                        t = TPB * b + j
                        ins = v.scalar_tensor_tensor(X[:, t, :], M.slot("expert", p, i)[:, j * D:j * D + D],
                                                     GATE[:, b % 2, j, e:e + 1], X[:, t, :], ALU.mult, ALU.add)
                        if j < TPB - 1:
                            mark(ins)
                    sure(ins, *M.read("expert", p, i))
                elif stage == "back":
                    add_to_x(TR, "back", p, i, i)

        @block.gpsimd
        def _(pool):
            g = nc.gpsimd
            def sure(ins, sem_, n):
                ins.then_inc(sem_, 1)
                pool.wait_ge(sem_, n)

            sure(g.memset(KBD0, 0.0), zeroed_tables, 1)
            sure(g.memset(VTD0, 0.0), zeroed_tables, 2)
            sure(g.memset(ROW[:, :, :], 0.0), zeroed_rows, 1)
            sure(g.memset(BIAS2[:, :, :], 0.0), zeroed_rows, 2)
            sure(g.memset(VEX[:, :, :, :], 0.0), zeroed_values, 1)
            for r in range(2):
                for h in range(2):
                    sure(g.memset(diagonal(slice(64 * h, 64 * h + 64), r, D + h, 2, 1), 1.0),
                         zeroed_values, 2 + 2 * r + h)

            for stage, p, i in SCHEDULE:
                if stage == "query0":
                    b, j = i // TPB, i % TPB
                    if i == 0:
                        pool.wait_ge(loaded["rel"], 16)
                        pool.wait_ge(fills, 1)
                    if i >= 2:
                        pool.wait_ge(*masked.at(p, i - 2))
                    sure(g.tensor_tensor(RELM[:, i % 2, :, :], REL[:, j, :, :],
                                         FILL0[:, b, :].unsqueeze(1).broadcast_to([P, H, SK]), ALU.add),
                         *relmasked.at(p, i))
                    pool.wait_ge(*S.read("query0", p, i))
                    if i >= 2:
                        pool.wait_ge(*TR.full("queryT1", p, i - 2))
                    sure(g.tensor_tensor(QR[:, i % 2, :], T1, T2, ALU.add), *rotated.at(p, i))
                elif stage == "keys":
                    b = i
                    if (p, b) == (2, 0):
                        pool.wait_ge(loaded["consts"], 16)
                        pool.wait_ge(loaded["ctxT"], 16)
                    if p > 2 and b == 0:
                        pool.wait_ge(*M.read("keys", p, 0))
                    if b >= 2 or p > 2:
                        q, c = (p, b - 2) if b >= 2 else (p - 2, b + 2)
                        pool.wait_ge(*S.full("scores", q, TPB * c + 1))
                    src = CTXT[:, b, 0, :] if p == 2 else KT[:, b, :]
                    sure(g.tensor_tensor(KBD[:, b % 2, :, :], src.unsqueeze(1).broadcast_to([P, H, SK]), HEADS,
                                         ALU.mult), *kbd_ready.at(p, b))
                elif stage == "scores":
                    a = ATT.index(p) * T + i
                    pool.wait_ge(*masked.at(p, i))
                    sure(g.tensor_tensor(SM[:, a % 3, :, :], SM[:, a % 3, :, :],
                                         MX[:, a % 3, :].unsqueeze(2).broadcast_to([P, H, SK]), ALU.subtract),
                         *shifted.at(p, i))
                elif stage == "sum":
                    a = ATT.index(p) * T + i
                    pool.wait_ge(*summed.at(p, i))
                    sure(g.tensor_tensor(SM[:, a % 3, :, :], SM[:, a % 3, :, :],
                                         RCP[:, i % 2, :].unsqueeze(2).broadcast_to([P, H, SK]), ALU.mult),
                         *weighed.at(p, i))
                elif stage == "bias":
                    if (p, i) == (2, 0):
                        pool.wait_ge(loaded["xbias"], 16)
                    pool.wait_ge(*normed.at(p, i))
                    both = X[:, TPB * i:TPB * i + TPB, :]
                    sure(g.tensor_tensor(both, both, XBIAS[:, (2, 4, 6).index(p), :].unsqueeze(1)
                                         .broadcast_to([P, TPB, D]), ALU.add), *biased.at(p, i))
                elif stage == "gated":
                    pool.wait_ge(*S.read("hidden0", p, i))
                    sure(g.tensor_tensor(TH[i % 2], GP[i % 2], UP[i % 2], ALU.mult), *gated_ready.at(p, i))


def _constants():
    c = np.zeros((P, NCONST), np.float32)

    def put(name, a):
        o, n = CONSTS[name]
        c[:, o:o + n] = np.asarray(a, np.float32).reshape(P, n)

    put("ident", np.eye(P))
    row0 = np.zeros((P, P))
    row0[0] = 1
    put("row0", row0)
    put("heads", np.arange(P)[:, None] // DH == np.arange(H)[None, :])
    put("iota", np.tile(np.arange(E), (P, 1)))
    inv = (1.0 / np.float32(10000.0) ** (np.arange(0, D0, 2, dtype=np.float32) / np.float32(D0))).astype(np.float32)
    angle = np.repeat(np.outer(np.arange(SQ, dtype=np.float32), inv).astype(np.float32), 2, axis=-1)
    cos, sin = np.cos(angle), np.sin(angle)
    sin[:, :D0 // 2] *= -1
    put("cosq", cos.reshape(TPB, P, D0).transpose(1, 0, 2))
    put("sinq", sin.reshape(TPB, P, D0).transpose(1, 0, 2))
    put("cosk", np.tile(cos[:SK].T, (2, 1)))
    put("sink", np.tile(sin[:SK].T, (2, 1)))
    return c


def _layout(a):
    f = {}
    f["x"] = a["x"][ORDER].reshape(T, P, D).transpose(1, 0, 2)
    ctx = a["ctx_1024"][ORDER]
    f["ctxT"] = np.tile(ctx.transpose(2, 0, 1)[:, :, None], (1, 1, 2, 1))
    f["ctx2"] = np.tile(ctx.transpose(1, 0, 2), (2, 1, 1))
    f["consts"] = _constants()
    zero = np.zeros((P, NCOLS), np.float32)

    def cols(v):
        return v.reshape(-1, P).T

    for name, v in (("bq4", a["L2_xattn_bq"]), ("bk4", a["L2_xattn_bk"]), ("bq6", a["L3_xattn_bq"]),
                    ("bk6", a["L3_xattn_bk"]), ("ln_scale", a["L2_ffn_ln_scale"]), ("ln_bias", a["L2_ffn_ln_bias"]),
                    ("attn_b", a["L2_ffn_attn_b"]), ("next_b", a["L2_ffn_next_b"]), ("b1_3", a["L1_ffn_b1"]),
                    ("b1_5", a["L2_ffn_b1"]), ("b2_5", a["L2_ffn_b2"]), ("b1_7", a["L3_ffn_b1"])):
        v = cols(v)
        zero[:, COLS[name]:COLS[name] + v.shape[1]] = v
    f["cols"] = zero
    m = {"w2": a["L1_xattn_W_fc"].T, "q4": a["L2_xattn_Wq"].T, "k4": a["L2_xattn_Wk"].T, "v4": a["L2_xattn_Wv"].T,
         "w4": a["L2_xattn_Wo"].T, "attn": a["L2_ffn_attn_w"].T, "next": a["L2_ffn_next_w"].T,
         "q6": a["L3_xattn_Wq"], "k6": a["L3_xattn_Wk"], "v6": a["L3_xattn_Wv"], "w6": a["L3_xattn_Wo"],
         "gate1": a["L0_ffn_gate_w"].T, "gate3": a["L1_ffn_Wg"], "gate7": a["L3_ffn_Wr"]}
    mats = np.zeros((P, len(MATS), P), np.float32)
    for n, name in enumerate(MATS):
        mats[:, n, :m[name].shape[1]] = m[name]
    f["mats"] = mats
    r = {"b2": "L1_xattn_b_fc", "v4": "L2_xattn_bv", "b4": "L2_xattn_bo", "v6": "L3_xattn_bv", "b6": "L3_xattn_bo"}
    f["rows"] = np.stack([a[r[n]] for n in ROWS])[None]
    f["xbias"] = np.tile(np.stack([a[r[n]] for n in XBIASES])[None], (P, 1, 1))
    f["bias2"] = np.stack([a["L1_ffn_b2"], a["L3_ffn_b2"]], axis=1)
    f["gbias"] = np.tile(np.stack([a["L1_ffn_bg"], a["L3_ffn_br"]])[None], (P, 1, 1))
    away = np.abs(np.arange(SQ)[:, None] - np.arange(SK)[None, :])
    rel = a["L0_xattn_rel_pos_bias"][:, away]
    f["relpos"] = rel.reshape(H, TPB, P, SK).transpose(2, 1, 0, 3)
    f["mask0"] = np.tile(a["mask_BxS2_bf1"][ORDER].view(np.uint8)[None], (P, 1, 1))
    f["mask1"] = a["mask_Bx1xSxS2_ik1"][ORDER].reshape(T, P, SK).transpose(1, 0, 2)
    f["mask2"] = np.tile(a["mask_Bx1x1xS2_ik0"][ORDER].reshape(1, B, SK), (P, 1, 1))
    f["wq0"] = a["L0_xattn_Wq"]
    wk = a["L0_xattn_Wk"].reshape(D, KV0, D0)
    f["wk0"] = np.tile(wk, (1, 1, 2))
    f["wk0r"] = np.tile(np.roll(wk, D0 // 2, axis=-1), (1, 1, 2))
    f["wv0"] = np.tile(a["L0_xattn_Wv"].reshape(D, KV0, D0), (1, 1, 2))
    f["wo0"] = a["L0_xattn_Wo"].reshape(NPAIR, P, D).transpose(1, 0, 2)
    f["wg0"] = a["L0_ffn_w_gate"].transpose(2, 0, 1).reshape(D, E * I0)
    f["wu0"] = a["L0_ffn_w_up"].transpose(2, 0, 1).reshape(D, E * I0)
    f["wd0"] = a["L0_ffn_w_down"].transpose(0, 2, 1).reshape(4, P, D).transpose(1, 0, 2)
    for p, n in ((3, "L1_ffn_W1"), (5, "L2_ffn_w1"), (7, "L3_ffn_W1")):
        f[f"w1_{p}"] = a[n].transpose(1, 0, 2)
    for p, n in ((3, "L1_ffn_W2"), (5, "L2_ffn_w2"), (7, "L3_ffn_W2")):
        f[f"w2_{p}"] = a[n].reshape(E, HID[p] // P, P, D).transpose(2, 0, 1, 3)
    return {k: np.ascontiguousarray(v) for k, v in f.items()}


NAMES = ["x", "ctxT", "ctx2", "consts", "cols", "mats", "rows", "xbias", "bias2", "gbias", "relpos", "mask0", "mask1", "mask2",
         "wq0", "wk0", "wk0r", "wv0", "wo0", "wg0", "wu0", "wd0", "w1_3", "w2_3", "w1_5", "w2_5", "w1_7", "w2_7"]


def kernel(**inputs):
    import concourse.bacc as bacc
    from concourse.bass_utils import run_bass_kernel_spmd

    laid = _layout({k: np.asarray(v) for k, v in inputs.items()})
    nc = bacc.Bacc("TRN2", target_bir_lowering=False, num_devices=1)
    arrays, args = {}, []
    for name in NAMES:
        v = laid[name]
        arrays[f"in_{name}"] = v
        args.append(nc.dram_tensor(f"in_{name}", v.shape, mybir.dt.from_np(v.dtype), kind="ExternalInput").ap())
    args.append(nc.dram_tensor("out_x", (P, T, D), F32, kind="ExternalOutput").ap())
    build(nc, *args)
    r = run_bass_kernel_spmd(nc, [arrays], core_ids=[0])
    return np.ascontiguousarray(r.results[0]["out_x"].transpose(1, 0, 2).reshape(B, SQ, D)[ORDER])
```

```python
from contextlib import ExitStack

import numpy as np
import concourse.bass as bass
from concourse import mybir

F32 = mybir.dt.float32
F32R = mybir.dt.float32r
I32 = mybir.dt.int32
U32 = mybir.dt.uint32
U8 = mybir.dt.uint8
ALU = mybir.AluOpType
ACT = mybir.ActivationFunctionType
X_AXIS = mybir.AxisListType.X

P = 128
B, SQ, D = 4, 256, 128
ORDER = [0, 2, 1, 3]
SK = 64
T = B * SQ // P
TPB = SQ // P
H = 16
D0, KV0 = 64, 4
DH = D // H
NPAIR = H // 2
E = 8
I0 = 64
HID = {3: 512, 5: 512, 7: 256}
CHUNK = 1024
EPS = 1e-5
FILL = -float(2.0 ** 100)
RSQRT_SEED = float(0x5F3759DF)
VX = D + H

ATT, FFN = (0, 2, 4, 6), (1, 3, 5, 7)
START = {0: 0, 1: 7.4, 2: 15.05, 3: 20.75, 4: 29.2, 5: 36.3, 6: 47.85, 7: 54.25}
PL = {
    ("exp", 0): -0.27, ("exp", 0, "odd"): -0.08, ("finish", 0): 2.27, ("first", 0): -4.29, ("fold", 0): -0.68,
    ("fold0", 0): -0.46, ("keys0", 0): -3.09, ("nextnorm", 0): 1.07, ("norm", 0): 0.16, ("probsT", 0): 1.14,
    ("probsT", 0, "odd"): 0.25, ("query0", 0): -3.08, ("query0", 0, "odd"): 0.31, ("queryT", 0): -1.63,
    ("queryT", 0, "odd"): -0.03, ("scores", 0): -1.3, ("scores", 0, "odd"): 0.12, ("sum", 0): -0.56,
    ("sum", 0, "odd"): 0.4, ("values", 0): 1.88, ("values", 0, "odd"): 0.02, ("values0", 0): -1.69, ("xT", 0): -4.58,
    ("xT", 0, "odd"): 0.59,
    ("down0", 1): 1.67, ("down0", 1, "odd"): 0.03, ("finish", 1): 2.37, ("gated", 1): -0.71,
    ("gated", 1, "odd"): 0.25, ("gatedT", 1): 0.61, ("gatedT", 1, "odd"): 0.32, ("hidden0", 1): -0.94,
    ("hidden0", 1, "odd"): -0.12, ("logits", 1): -2, ("norm", 1): 0.03, ("tanh", 1): -0.84, ("tanh", 1, "odd"): 0.27,
    ("xT", 1): -2.56, ("xT", 1, "odd"): -0.01,
    ("bias", 2): -2.47, ("context", 2): 0.03, ("exp", 2): -0.87, ("exp", 2, "odd"): 0.21, ("finish", 2): 1.89,
    ("keys", 2): -3.49, ("norm", 2): 0.12, ("outT", 2): 1.58, ("outT", 2, "odd"): -0.35, ("probsT", 2): 0.06,
    ("probsT", 2, "odd"): -0.06, ("project", 2): 1.89, ("project", 2, "odd"): -0.13, ("scores", 2): -1.91,
    ("scores", 2, "odd"): 0.05, ("values", 2): 0.6, ("values", 2, "odd"): 0.09, ("xT", 2): -2.71,
    ("xT", 2, "odd"): 0.2,
    ("bias2", 3): 1.36, ("gateT", 3): 0.71, ("hidden", 3): -0.12, ("logits", 3): -0.17, ("norm", 3): 0.67,
    ("step", 3): 0.25, ("wsplit", 3): -13.65, ("wstep", 3): 1.26, ("xT", 3): -1.95, ("xsplit", 3): -2.26,
    ("bias", 4): 0.79, ("context", 4): -0.86, ("exp", 4): -0.33, ("exp", 4, "odd"): -0.49, ("finish", 4): 1.69,
    ("keys", 4): -4.36, ("norm", 4): 0.38, ("norm2", 4): 0.41, ("outT", 4): 1.2, ("outT", 4, "odd"): -0.01,
    ("probsT", 4): 0.05, ("probsT", 4, "odd"): -0.34, ("project", 4): 1.87, ("project", 4, "odd"): -0.53,
    ("query", 4): -2.64, ("query", 4, "odd"): 0.51, ("scores", 4): -1.91, ("scores", 4, "odd"): 0.08,
    ("values", 4): 0.2, ("values", 4, "odd"): 0.19, ("xT", 4): -3.61, ("xT", 4, "odd"): 0.93,
    ("back", 5): 6.22, ("expert5", 5): 0.54, ("hidden5", 5): -0.53, ("mix", 5): -1.72, ("next5", 5): 2.98,
    ("norm", 5): 0.17, ("step", 5): 0.56, ("xT", 5): -2.06,
    ("bias", 6): -2.76, ("context", 6): -0.68, ("exp", 6): -0.41, ("exp", 6, "odd"): -0.75, ("finish", 6): 2.2,
    ("keys", 6): -4.95, ("norm", 6): 0.66, ("outT", 6): 1.37, ("outT", 6, "odd"): -0.02, ("probsT", 6): -0.27,
    ("probsT", 6, "odd"): -0.25, ("project", 6): 2.1, ("project", 6, "odd"): 0.1, ("query", 6): -2.32,
    ("query", 6, "odd"): -0.24, ("scores", 6): -1.85, ("scores", 6, "odd"): 0.13, ("values", 6): 0.36,
    ("values", 6, "odd"): 0.16, ("xT", 6): -2.53, ("xT", 6, "odd"): -0.18,
    ("bias2", 7): 1.52, ("gateT", 7): 0.37, ("hidden", 7): -0.04, ("logits", 7): -1.07, ("step", 7): 0.25,
    ("wsplit", 7): -20.33, ("wstep", 7): 2.54, ("xT", 7): -1.98, ("xsplit", 7): -0.9,
}
LAG = 2


def make_schedule():
    out = []

    def put(p, time, stage, index, named=None):
        out.append((START[p] + time, len(out), stage, p if named is None else named, index))

    def finish(p, b, time):
        put(p, time, "stats", b)
        put(p, time + PL["norm", p], "norm", b)
        if p + 1 == 5:
            put(p, time + PL["norm", p] + 0.01, "stats2", b)
            put(p, time + PL["norm", p] + PL["norm2", p], "norm2", b)

    for p in range(8):
        for t in range(T):
            odd = t % TPB == TPB - 1
            b = t // TPB
            if p in ATT:
                for stage in ("probsT", "query0", "queryT", "values", "exp", "sum", "outT", "scores", "xT", "project",
                              "query"):
                    if (stage, p) in PL:
                        put(p, t + PL[stage, p] + odd * PL.get((stage, p, "odd"), 0), stage, t)
                if not odd and p > 0:
                    for stage in ("keys", "context", "bias"):
                        put(p, t + PL[stage, p], stage, b)
                if not odd and p == 0 and b > 0:
                    put(p, t + PL["fold", 0], "fold", b)
                if odd:
                    finish(p, b, t + PL["finish", p])
            elif p == 1:
                for stage in ("xT", "hidden0", "tanh", "gated", "gatedT", "down0"):
                    put(p, t + PL[stage, p] + odd * PL.get((stage, p, "odd"), 0), stage, t)
                if odd:
                    put(p, t + PL["logits", p], "logits", b)
                    finish(p, b, t + PL["finish", p])
            elif p in (3, 7):
                put(p, t + PL["xT", p], "xT", t)
                if odd:
                    put(p, t + PL["xsplit", p], "xsplit", b)
                    put(p, t + PL["logits", p], "logits", b)
                    for e in range(E):
                        put(p, t + PL["hidden", p] + e * PL["step", p], "hidden", (b, e))
                        put(p, t + PL["hidden", p] + (e + LAG) * PL["step", p] + 0.01, "expert", (b, e))
                    put(p, t + PL["gateT", p], "gateT", b)
                    put(p, t + PL["bias2", p], "bias2", b)
                    if p == 3:
                        finish(p, b, t + PL["hidden", p] + (E - 1 + LAG) * PL["step", p] + 0.02)
                if t < E * HID[p] // CHUNK:
                    put(p, PL["wsplit", p] + t * PL["wstep", p], "wsplit", t)
            else:
                put(p, t + PL["xT", p], "xT", t)
                if odd:
                    put(p, t + PL["mix", p], "mix", b)
                put(p, t + PL["back", p], "back", t)
                if odd:
                    finish(p, b, t + PL["back", p] + 0.01)
                if t % 4 == 3:
                    half = t // 4
                    for e in range(E // 2):
                        put(p, t + PL["hidden5", p] + e * PL["step", p], "hidden5", E // 2 * half + e)
                        put(p, t + PL["expert5", p] + e * PL["step", p], "expert5", E // 2 * half + e)
                    put(p, t + PL["next5", p], "next5", half)
    for b in range(B):
        put(0, PL["first", 0] + b * PL["nextnorm", 0], "stats", b, -1)
        put(0, PL["first", 0] + b * PL["nextnorm", 0] + 0.05, "norm", b, -1)
    for g in range(KV0):
        put(0, PL["keys0", 0] + 0.01 * g, "keys0", g)
        put(0, PL["values0", 0] + 0.01 * g, "values0", g)
    put(0, PL["fold0", 0], "fold", 0)
    return [x[2:] for x in sorted(out)]


SCHEDULE = make_schedule()

JOBS = {
    "keys0": [("S", "keys0", "dve")], "values0": [("M", "values0", "act")],
    "xT": [("T", "xT", "act")], "query0": [("S", "query0", "dve")],
    "queryT": [("T", "queryT0", "act"), ("T", "queryT1", "act")], "query": [("M", "query", "act")],
    "probsT": [("T", "probsT0", "act"), ("T", "probsT1", "act")],
    "fold": [("S", "fold", "act")], "values": [("M", "values", "dve")], "outT": [("T", "outT", "act")],
    "project": [("M", "project", "dve")], "logits": [("M", "logits", "dve")],
    "hidden0": [("S", "hidden0", "late")], "gatedT": [("T", "gatedT", "act")], "down0": [("M", "down0", "dve")],
    "gateT": [("T", "gateT", "act")], "bias2": [("M", "bias2", "dve")],
    "hidden": [("S", "hidden", "act")], "expert": [("M", "expert", "dve")],
    "mix": [("M", "mix", "act")], "hidden5": [("S", "hidden5", "act")], "expert5": [("M", "expert5", "act")],
    "next5": [("S", "next5", "act")], "back": [("T", "back", "dve")],
}


def jobs_of(stage, p, i):
    if stage == "scores":
        return [("S", "scores", "dve" if p == 0 else "act")]
    if stage == "keys":
        return [("M", "keys", "act")] if p in (4, 6) and i == 0 else []
    if stage == "context":
        return [("M", "ctxv", "act")] if p in (4, 6) else []
    return JOBS.get(stage, [])


class Ring:

    def __init__(self, name, slots, filled, emptied):
        self.slots, self.filled, self.emptied = slots, filled, emptied
        self.number, self.turn = {}, []
        for stage, p, i in SCHEDULE:
            for ring, job, reader in jobs_of(stage, p, i):
                if ring == name:
                    self.number[job, p, i] = len(self.turn)
                    self.turn.append((reader, 1 + sum(r == reader for r, _ in self.turn)))

    def slot(self, *job):
        return self.slots[self.number[job] % len(self.slots)]

    def full(self, *job):
        return self.filled, self.number[job] + 1

    def read(self, *job):
        reader, n = self.turn[self.number[job]]
        return self.emptied[reader], n

    def reused(self, *job):
        return self.number[job] >= len(self.slots)

    def vacated(self, *job):
        reader, n = self.turn[self.number[job] - len(self.slots)]
        return self.emptied[reader], n


class Mark:

    def __init__(self, sem, keys):
        self.sem, self.nth = sem, {k: n + 1 for n, k in enumerate(keys)}

    def at(self, *key):
        return self.sem, self.nth[key]


COLS = {"bq4": 0, "bk4": 1, "bq6": 2, "bk6": 3, "ln_scale": 4, "ln_bias": 5, "attn_b": 6, "next_b": 7,
        "b1_3": 8, "b1_5": 40, "b2_5": 72, "b1_7": 80}
NCOLS = 96
MATS = ["w2", "q4", "k4", "v4", "w4", "attn", "next", "q6", "k6", "v6", "w6", "gate1", "gate3", "gate7"]
ROWS = ["v4", "v6"]
XBIASES = ["b2", "b4", "b6"]
CONSTS = {"ident": (0, 128), "row0": (128, 128), "heads": (256, 16), "iota": (272, 8), "cosq": (280, 128),
          "sinq": (408, 128), "cosk": (536, 64), "sink": (600, 64), "one": (664, 1)}
NCONST = 665


def build(nc, x, ctxT, ctx2, consts, cols, mats, rows, xbias, bias2, gbias, relpos, mask0, mask1, mask2,
          wq0, wk0, wk0r, wv0, wo0, wg0, wu0, wd0, w1_3, w2_3, w1_5, w2_5, w1_7, w2_7, out):
    with ExitStack() as ctx:
        def sb(name, shape, dt=F32):
            return ctx.enter_context(nc.sbuf_tensor(name, [P] + shape, dt))

        def sb_twice(name, shape, alias, columns, dt=F32):
            with nc.sbuf_tensor(alias, [P, columns], F32R) as second:
                pass
            return sb(name, shape, dt), second

        def sem(name):
            return ctx.enter_context(nc.semaphore(name))

        X = sb("X", [T, D])
        CST = sb("CST", [NCONST])
        COL = sb("COL", [NCOLS])
        MAT = sb("MAT", [len(MATS), P])
        ROW = sb("ROW", [len(ROWS), P])
        XBIAS = sb("XBIAS", [len(XBIASES), D])
        BIAS2 = sb("BIAS2", [2, P])
        GB = sb("GB", [2, E])
        CTXT = sb("CTXT", [B, 2, SK])
        CTX2 = sb("CTX2", [B, D])
        M0 = sb("M0", [B, SK], U8)
        M1, FILL1 = sb_twice("M1", [T, SK], "FILL1", T * SK, I32)
        M2, FILL2 = sb_twice("M2", [B, SK], "FILL2", B * SK, I32)
        FILL0 = sb("FILL0", [B, SK])
        IDENT_R = sb("IDENT_R", [P], F32R)
        W1_3, W1_3R = sb_twice("W1_3", [E, HID[3]], "W1_3R", E * HID[3])
        W2_3 = sb("W2_3", [E, HID[3] // P, D])
        W0, W0R = sb_twice("W0", [4608], "W0R", E * HID[7])
        TAB0, TAB0R = sb_twice("TAB0", [8192], "TAB0R", E * HID[3])
        XN = sb("XN", [T, D])
        XT = sb("XT", [T, P])
        QT = sb("QT", [2, P])
        SM = sb("SM", [4, H, SK])
        PT = sb("PT", [2, NPAIR, P])
        KBD = sb("KBD", [2, H, SK])
        VEX = sb("VEX", [2, NPAIR, VX])
        KT = sb("KT", [B, SK])
        WORK = sb("WORK", [8192])
        HALF, HALFR = sb_twice("HALF", [4, 512], "HALFR", 2 * 2 * TPB * P)
        AO = sb("AO", [2, D])
        OT = sb("OT", [2, P])
        GATE = sb("GATE", [2, TPB, P])
        GSCALE = sb("GSCALE", [2, TPB])
        GT = sb("GT", [2, TPB, P])
        ST = sb("ST", [TPB, 6])
        MV = sb("MV", [3, TPB, 2])
        VAR = sb("VAR", [TPB])
        RS = sb("RS", [3, TPB])
        SQ2 = sb("SQ2", [TPB])
        HV = sb("HV", [TPB])
        MX = sb("MX", [3, H])
        SUM = sb("SUM", [2, H])
        RCP = sb("RCP", [2, H])
        LG = sb("LG", [TPB, E])
        TOP = sb("TOP", [TPB, E])
        IDX = sb("IDX", [TPB, E], U32)
        IDF = sb("IDF", [TPB, E])
        HOT = sb("HOT", [2, TPB, E])
        GV = sb("GV", [8, TPB])
        GE = sb("GE", [TPB, E])
        GE2 = sb("GE2", [TPB, E])

        def const(name):
            o, n = CONSTS[name]
            return CST[:, o:o + n]

        def col(name, k=0):
            o = COLS[name] + k
            return COL[:, o:o + 1]

        def mat(name):
            return MAT[:, MATS.index(name), :]

        def row(name):
            return ROW[:, ROWS.index(name), :]

        def diagonal(half, r, first, step, n):
            flat = VEX[half, r, :, :].rearrange("p c v -> p (c v)")
            return bass.AP(flat.tensor, flat.offset + first, [list(flat.ap[0]), [VX + step, NPAIR], [1, n]])

        IDENT, ROW0 = const("ident"), const("row0")
        HEADS = const("heads").unsqueeze(2).broadcast_to([P, H, SK])
        COSQ = const("cosq").rearrange("p (j d) -> p j d", j=TPB)
        SINQ = const("sinq").rearrange("p (j d) -> p j d", j=TPB)
        COSK = const("cosk").unsqueeze(1).broadcast_to([P, B, SK])
        SINK = const("sink").unsqueeze(1).broadcast_to([P, B, SK])

        WQ0, WO0 = W0[:, 0:1024], W0[:, 1024:2048].rearrange("p (c n) -> p c n", c=NPAIR)
        WK0 = W0[:, 2048:2560].rearrange("p (g d) -> p g d", g=KV0)
        WK0R = W0[:, 2560:3072].rearrange("p (g d) -> p g d", g=KV0)
        WG0, WU0 = W0[:, 3072:3584], W0[:, 3584:4096]
        WD0 = W0[:, 4096:4608].rearrange("p (c n) -> p c n", c=4)
        W1_7 = W0[:, 0:2048].rearrange("p (e f) -> p e f", e=E)
        W2_7 = W0[:, 2048:4096].rearrange("p (e c n) -> p e c n", e=E, c=2)
        W1_ALL = {3: W1_3[:, :, :].rearrange("p e f -> p (e f)"), 7: W0[:, 0:2048]}
        W1_HI, W1_LO = {3: TAB0R, 7: W1_3R}, {3: W1_3R, 7: W0R}
        XS = HALFR[:, :].rearrange("p (b n) -> p b n", b=2)
        X_HI, X_LO = XS[:, :, 0:TPB * P], XS[:, :, TPB * P:2 * TPB * P]
        REL = TAB0[:, 0:2048].rearrange("p (j h k) -> p j h k", j=TPB, h=H)
        RELM = TAB0[:, 2048:4096].rearrange("p (j h k) -> p j h k", j=2, h=H)
        KBD0 = TAB0[:, 4096:6144].rearrange("p (b g k) -> p b g k", b=B, g=KV0)
        VTD0 = TAB0[:, 6144:8192].rearrange("p (b g k) -> p b g k", b=B, g=KV0)
        W1_5 = TAB0[:, 0:4096].rearrange("p (e f) -> p e f", e=E)
        W2_5 = TAB0[:, 4096:8192].rearrange("p (e c n) -> p e c n", e=E, c=4)
        T1, T2 = WORK[:, 0:1024], WORK[:, 1024:2048]
        QR = WORK[:, 2048:4096].rearrange("p (r n) -> p r n", r=2)
        QT0 = WORK[:, 4096:5120].rearrange("p (c q) -> p c q", c=NPAIR)
        VW = WORK[:, 5120:7168].rearrange("p (r c n) -> p r c n", r=2, c=NPAIR)
        WV0 = WORK[:, 7168:7680].rearrange("p (g d) -> p g d", g=KV0)
        K1, K2 = WORK[:, 7680:7936], WORK[:, 7936:8192]
        HT = WORK[:, 0:3072].rearrange("p (r c q) -> p r c q", r=3, c=4)
        XAT = WORK[:, 2048:3072]
        EOT = WORK[:, 3072:4096]
        YT = WORK[:, 4096:5120]
        HT5 = WORK[:, 5120:6144].rearrange("p (r c q) -> p r c q", r=2, c=4)
        XN2 = WORK[:, 6144:7168].rearrange("p (t n) -> p t n", t=T)
        GP, UP = (WORK[:, 7680:8192], W0[:, 2048:2560]), (HALF[:, 0, :], W0[:, 2560:3072])
        TH, AT = (HALF[:, 1, :], HALF[:, 2, :]), HALF[:, 3, :]

        psS = [ctx.enter_context(nc.psum_tensor(f"psS{k}", [P, 1024], F32)) for k in range(2)]
        psT = [ctx.enter_context(nc.psum_tensor(f"psT{k}", [P, 512], F32)) for k in range(2)]
        psM = [ctx.enter_context(nc.psum_tensor(f"psM{k}", [P, 512], F32)) for k in range(2)]
        rings = {}
        for name, slots in (("S", psS), ("T", psT), ("M", psM)):
            rings[name] = Ring(name, slots, sem(f"filled_{name}"),
                               {who: sem(f"emptied_{name}_by_{who}") for who in ("act", "dve", "late")})
        S, TR, M = rings["S"], rings["T"], rings["M"]

        def staged(*names):
            return [(p, i) for s, p, i in SCHEDULE if s in names]

        normed = Mark(sem("normed"), [(p + 1, b) for s, p, b in SCHEDULE if s == ("norm2" if p == 4 else "norm")])
        variances = [(s, p, b) for s, p, b in SCHEDULE if s in ("stats", "stats2")]
        masked = Mark(sem("masked"), staged("scores"))
        shifted = Mark(sem("shifted"), staged("scores"))
        exped = Mark(sem("exped"), staged("exp"))
        summed = Mark(sem("summed"), staged("sum"))
        weighed = Mark(sem("weighed"), staged("sum"))
        biased = Mark(sem("biased"), staged("bias"))
        x_rounded = Mark(sem("x_rounded"), staged("xsplit"))
        w_rounded = Mark(sem("w_rounded"), staged("wsplit"))
        x_split = Mark(sem("x_split"), staged("xsplit"))
        w_split = Mark(sem("w_split"), staged("wsplit"))
        rotated = Mark(sem("rotated"), staged("query0"))
        relmasked = Mark(sem("relmasked"), staged("query0"))
        kbd_ready = Mark(sem("kbd_ready"), staged("keys"))
        vex_ready = Mark(sem("vex_ready"), [(p, b) for p, b in staged("context") if p == 2])
        keys0_ready = Mark(sem("keys0_ready"), staged("keys0"))
        gate_top = Mark(sem("gate_top"), staged("logits"))
        gate_exp = Mark(sem("gate_exp"), staged("logits"))
        gate_ready = Mark(sem("gate_ready"), staged("logits"))
        tanh_ready = Mark(sem("tanh_ready"), staged("tanh"))
        gated_ready = Mark(sem("gated_ready"), staged("gated"))
        zeroed_tables = sem("zeroed_tables")
        zeroed_rows = sem("zeroed_rows")
        zeroed_values = sem("zeroed_values")
        fills = sem("fills")
        masks_ready = sem("masks_ready")
        stored = sem("stored")
        act_chain = sem("act_chain")
        dve_chain = sem("dve_chain")

        def pv(t):
            return t.rearrange("(a n) -> a n", a=1)

        loads = [
            ("x01", X[:, 0:4, :], x[:, 0:4, :]), ("consts", CST[:, :], consts), ("wq0", WQ0, wq0),
            ("ctxT", CTXT[:, :, :, :], ctxT), ("wk0", WK0, wk0), ("wk0r", WK0R, wk0r), ("mask0", M0[:, :, :], mask0),
            ("rel", REL, relpos), ("wv0", WV0, wv0), ("wo0", WO0, wo0), ("x23", X[:, 4:8, :], x[:, 4:8, :]),
            ("cols", COL[:, :], cols), ("mats", MAT[:, :, :], mats),
            ("wg0", WG0, wg0), ("wu0", WU0, wu0), ("wd0", WD0, wd0),
            ("ctx2", CTX2[:, :, :], ctx2), ("mask1", M1[:, :, :], mask1), ("mask2", M2[:, :, :], mask2),
            ("gbias", GB[:, :, :], gbias), ("xbias", XBIAS[:, :, :], xbias),
            ("rows", ROW[0:1, :, :], rows), ("bias2", BIAS2[0:E, :, :], bias2),
            ("w1_3", W1_3[:, :, :], w1_3), ("w2_3", W2_3[:, :, :, :], w2_3),
            ("w1_7", W1_7, w1_7), ("w2_7", W2_7, w2_7), ("w1_5", W1_5, w1_5), ("w2_5", W2_5, w2_5)]
        loaded = {name: sem(f"loaded_{name}") for name, _, _ in loads}

        block = ctx.enter_context(nc.Block())

        def group(t, e):
            return t.rearrange("p (f m g q) -> p f m g q", f=2, m=2, g=4)[:, e // 4, :, e % 4, :]

        @block.sync
        def _(sp):
            for name, dst, src in loads:
                if name == "rows":
                    sp.wait_ge(zeroed_rows, 2)
                if name == "w1_5":
                    sp.wait_ge(*S.full("hidden", 3, (B - 1, E - 1)))
                if name == "w1_7":
                    sp.wait_ge(*M.full("down0", 1, T - 1))
                sp.dma_start(dst, src).then_inc(loaded[name], 16)
            for b in range(B):
                sp.wait_ge(*M.read("expert", 7, (b, E - 1)))
                sp.dma_start(out[:, TPB * b:TPB * (b + 1), :], X[:, TPB * b:TPB * (b + 1), :]).then_inc(stored, 16)
            sp.wait_ge(stored, 16 * B)

        @block.tensor
        def _(pe):
            mm, tr = nc.tensor.matmul, nc.tensor.transpose

            def claim(ring, *job):
                if ring.reused(*job):
                    pe.wait_ge(*ring.vacated(*job))
                return ring.slot(*job)

            def load_wait(*names):
                for n in names:
                    pe.wait_ge(loaded[n], 16)

            for stage, p, i in SCHEDULE:
                if stage == "keys0":
                    if i == 0:
                        load_wait("ctxT", "wk0", "wk0r")
                    o = claim(S, "keys0", p, i)
                    for n, w in enumerate((WK0, WK0R)):
                        last = mm(o[:, 512 * n:512 * n + 256], w[:, i, :],
                                  CTXT[:, :, 0, :], start=True, stop=True)
                    last.then_inc(S.filled, 1)
                elif stage == "values0":
                    if i == 0:
                        load_wait("wv0")
                    o = claim(M, "values0", p, i)
                    mm(o[:, 0:256], WV0[:, i, :], CTXT[:, :, 0, :], start=True, stop=True).then_inc(M.filled, 1)
                elif stage == "fold":
                    if i == 0:
                        load_wait("wo0")
                        pe.wait_ge(*M.read("values0", p, KV0 - 1))
                    o = claim(S, "fold", p, i)
                    for c in range(NPAIR):
                        last = mm(o[:, c * P:c * P + P], VTD0[:, i, c // 2, :], WO0[:, c, :], start=True, stop=True)
                    last.then_inc(S.filled, 1)
                elif stage == "xT":
                    if p == 0 and i == 0:
                        load_wait("consts")
                    pe.wait_ge(*normed.at(p, i // TPB))
                    o = claim(TR, "xT", p, i)
                    src = XN2 if p == 5 else XN
                    tr(o[:, 0:P], src[:, i, :], IDENT).then_inc(TR.filled, 1)
                elif stage == "query0":
                    if i == 0:
                        load_wait("wq0")
                    o = claim(S, "query0", p, i)
                    pe.wait_ge(*TR.read("xT", p, i))
                    for n in range(2):
                        last = mm(o[:, 512 * n:512 * n + 512], XT[:, i, :], WQ0[:, 512 * n:512 * n + 512],
                                  start=True, stop=True)
                    last.then_inc(S.filled, 1)
                elif stage == "queryT":
                    pe.wait_ge(*rotated.at(p, i))
                    for n in range(2):
                        o = claim(TR, f"queryT{n}", p, i)
                        for c in range(4):
                            last = tr(o[:, c * P:c * P + P], QR[:, i % 2, (4 * n + c) * P:(4 * n + c + 1) * P], IDENT)
                        last.then_inc(TR.filled, 1)
                elif stage == "query":
                    if p == 4 and i == 0:
                        load_wait("mats")
                    o = claim(M, "query", p, i)
                    pe.wait_ge(*TR.read("xT", p, i))
                    mm(o[:, 0:P], mat(f"q{p}"), XT[:, i, :], start=True, stop=True).then_inc(M.filled, 1)
                elif stage == "scores":
                    b = i // TPB
                    o = claim(S, "scores", p, i)
                    if p == 0:
                        if i == 0:
                            pe.wait_ge(*keys0_ready.at(0, KV0 - 1))
                        pe.wait_ge(*TR.read("queryT1", p, i))
                        for c in range(NPAIR):
                            last = mm(o[:, c * P:c * P + P], QT0[:, c, :], KBD0[:, b, c // 2, :],
                                      start=True, stop=True)
                    else:
                        if (p, i) == (2, 0):
                            pe.wait_ge(masks_ready, 3)
                        k = i if p != 4 else b
                        fill = (FILL2 if p == 4 else FILL1)[:, k * SK:k * SK + SK]
                        for n in range(2):
                            mm(o[:, 512 * n:512 * n + 512], IDENT_R[:, :],
                               fill.unsqueeze(1).broadcast_to([P, H // 2, SK]), start=True, stop=False)
                        if p == 2:
                            pe.wait_ge(*TR.read("xT", p, i))
                            q = XT[:, i, :]
                        else:
                            pe.wait_ge(*M.read("query", p, i))
                            q = QT[:, i % 2, :]
                        pe.wait_ge(*kbd_ready.at(p, b))
                        for n in range(2):
                            last = mm(o[:, 512 * n:512 * n + 512], q, KBD[:, b % 2, 8 * n:8 * n + 8, :],
                                      start=False, stop=True)
                    last.then_inc(S.filled, 1)
                elif stage == "probsT":
                    pe.wait_ge(*(weighed if p == 0 else exped).at(p, i))
                    a = ATT.index(p) * T + i
                    for n in range(2):
                        o = claim(TR, f"probsT{n}", p, i)
                        for c in range(4):
                            pair = 4 * n + c
                            last = tr(o[:, c * P:c * P + P],
                                      SM[:, a % 4, 2 * pair:2 * pair + 2, :].rearrange("p h k -> p (h k)"), IDENT)
                        last.then_inc(TR.filled, 1)
                elif stage == "values":
                    b = i // TPB
                    a = ATT.index(p) * T + i
                    o = claim(M, "values", p, i)
                    if i % TPB == 0:
                        pe.wait_ge(*(S.read("fold", p, b) if p == 0 else vex_ready.at(p, b) if p == 2 else
                                     M.read("ctxv", p, b)))
                    for c in range(NPAIR):
                        if c % 4 == 0:
                            pe.wait_ge(*TR.read(f"probsT{c // 4}", p, i))
                        if p == 0:
                            last = mm(o[:, 0:D], PT[:, a % 2, c, :], VW[:, b % 2, c, :],
                                      start=(c == 0), stop=(c == NPAIR - 1))
                        else:
                            last = mm(o[:, 0:VX], PT[:, a % 2, c, :], VEX[:, b % 2, c, :],
                                      start=(c == 0), stop=(c == NPAIR - 1))
                    last.then_inc(M.filled, 1)
                elif stage == "outT":
                    pe.wait_ge(*M.read("values", p, i))
                    o = claim(TR, "outT", p, i)
                    tr(o[:, 0:P], AO[:, i % 2, :], IDENT).then_inc(TR.filled, 1)
                elif stage == "project":
                    if p == 2 and i == 0:
                        load_wait("mats")
                    o = claim(M, "project", p, i)
                    pe.wait_ge(*TR.read("outT", p, i))
                    mm(o[:, 0:D], OT[:, i % 2, :], mat(f"w{p}"), start=True, stop=True).then_inc(M.filled, 1)
                elif stage == "keys" and p in (4, 6) and i == 0:
                    o = claim(M, "keys", p, i)
                    mm(o[:, 0:256], mat(f"k{p}"), CTXT[:, :, 0, :], start=True, stop=True).then_inc(M.filled, 1)
                elif stage == "context" and p in (4, 6):
                    if p == 4 and i == 0:
                        load_wait("mats", "rows")
                    o = claim(M, "ctxv", p, i)
                    mm(o[:, 0:D], CTXT[:, i, :, :].rearrange("p h k -> p (h k)"), mat(f"v{p}"),
                       start=True, stop=False)
                    mm(o[:, 0:D], ROW0, row(f"v{p}"), start=False, stop=True).then_inc(M.filled, 1)
                elif stage == "logits":
                    if p == 1 and i == 0:
                        load_wait("mats")
                    o = claim(M, "logits", p, i)
                    pe.wait_ge(*TR.read("xT", p, TPB * i + 1))
                    for j in range(TPB):
                        last = mm(o[:, j * P:j * P + P], XT[:, TPB * i + j, :], mat(f"gate{p}"), start=True, stop=True)
                    last.then_inc(M.filled, 1)
                elif stage == "hidden0":
                    if i == 0:
                        load_wait("wg0", "wu0")
                    o = claim(S, "hidden0", p, i)
                    for n, w in enumerate((WG0, WU0)):
                        last = mm(o[:, 512 * n:512 * n + 512], XT[:, i, :], w, start=True, stop=True)
                    last.then_inc(S.filled, 1)
                elif stage == "gatedT":
                    pe.wait_ge(*gated_ready.at(p, i))
                    o = claim(TR, "gatedT", p, i)
                    for c in range(4):
                        last = tr(o[:, c * P:c * P + P], TH[i % 2][:, c * P:c * P + P], IDENT)
                    last.then_inc(TR.filled, 1)
                elif stage == "down0":
                    if i == 0:
                        load_wait("wd0")
                    o = claim(M, "down0", p, i)
                    pe.wait_ge(*TR.read("gatedT", p, i))
                    for c in range(4):
                        last = mm(o[:, 0:D], AT[:, c * P:c * P + P], WD0[:, c, :], start=(c == 0), stop=(c == 3))
                    last.then_inc(M.filled, 1)
                elif stage == "gateT":
                    pe.wait_ge(*gate_ready.at(p, i))
                    o = claim(TR, "gateT", p, i)
                    for j in range(TPB):
                        last = tr(o[:, j * P:j * P + P], GATE[:, i % 2, j, :], IDENT)
                    last.then_inc(TR.filled, 1)
                elif stage == "bias2":
                    if i == 0:
                        load_wait("bias2")
                    o = claim(M, "bias2", p, i)
                    pe.wait_ge(*TR.read("gateT", p, i))
                    for j in range(TPB):
                        last = mm(o[:, j * D:j * D + D], GT[:, i % 2, j, :], BIAS2[:, (3, 7).index(p), :],
                                  start=True, stop=True)
                    last.then_inc(M.filled, 1)
                elif stage == "hidden":
                    b, e = i
                    if b == 0 and e * HID[p] % CHUNK == 0:
                        pe.wait_ge(*w_split.at(p, e * HID[p] // CHUNK))
                    o = claim(S, "hidden", p, i)
                    if e == 0:
                        pe.wait_ge(*x_split.at(p, b))
                    for c in range(HID[p] // P):
                        cols_ = slice(e * HID[p] + c * P, e * HID[p] + c * P + P)
                        oc = o[:, 256 * c:256 * c + 256]
                        mm(oc, W1_HI[p][:, cols_], X_HI[:, b % 2, :], start=True, stop=False)
                        mm(oc, W1_HI[p][:, cols_], X_LO[:, b % 2, :], start=False, stop=False)
                        last = mm(oc, W1_LO[p][:, cols_], X_HI[:, b % 2, :], start=False, stop=True)
                    last.then_inc(S.filled, 1)
                elif stage == "expert":
                    b, e = i
                    if b == 0 and e == 0:
                        load_wait(f"w2_{p}")
                    o = claim(M, "expert", p, i)
                    pe.wait_ge(*S.read("hidden", p, i))
                    w = W2_3 if p == 3 else W2_7
                    nc_ = HID[p] // P
                    for j in range(TPB):
                        for c in range(nc_):
                            last = mm(o[:, j * D:j * D + D], HT[:, (b * E + e) % 3, c, j * P:j * P + P], w[:, e, c, :],
                                      start=(c == 0), stop=(c == nc_ - 1))
                    last.then_inc(M.filled, 1)
                elif stage == "mix":
                    o = claim(M, "mix", p, i)
                    t = TPB * i
                    pe.wait_ge(*TR.read("xT", p, t + 1))
                    mm(o[:, 0:256], mat("attn"), XT[:, t:t + TPB, :], start=True, stop=False)
                    for j in range(TPB):
                        last = mm(o[:, j * P:j * P + P], XN[:, t + j, :], IDENT, start=False, stop=(j == 1))
                    last.then_inc(M.filled, 1)
                elif stage == "hidden5":
                    if i == 0:
                        load_wait("w1_5")
                    if i % 4 == 0:
                        pe.wait_ge(*M.read("mix", p, i // 2 + 1))
                    o = claim(S, "hidden5", p, i)
                    xa = group(XAT, i)
                    for c in range(4):
                        last = mm(o[:, c * P:c * P + P], W1_5[:, i, c * P:c * P + P], xa, start=True, stop=True)
                    last.then_inc(S.filled, 1)
                elif stage == "expert5":
                    if i == 0:
                        load_wait("w2_5")
                    o = claim(M, "expert5", p, i)
                    pe.wait_ge(*S.read("hidden5", p, i))
                    for c in range(4):
                        last = mm(o[:, 0:P], W2_5[:, i, c, :], HT5[:, i % 2, c, :], start=(c == 0), stop=(c == 3))
                    last.then_inc(M.filled, 1)
                elif stage == "next5":
                    o = claim(S, "next5", p, i)
                    pe.wait_ge(*M.read("expert5", p, E // 2 * i + 3))
                    mm(o[:, 0:512], mat("next"), EOT[:, 512 * i:512 * i + 512], start=True, stop=True)\
                        .then_inc(S.filled, 1)
                elif stage == "back":
                    o = claim(TR, "back", p, i)
                    pe.wait_ge(*S.read("next5", p, i // 4))
                    tr(o[:, 0:P], YT[:, i * P:i * P + P], IDENT).then_inc(TR.filled, 1)

        @block.scalar
        def _(act):
            def run(out_, in_, func, bias=0.0, scale=1.0):
                return nc.scalar.activation(out_, in_, func, bias=bias, scale=scale)

            for stage, p, i in SCHEDULE:
                if stage == "values0":
                    act.wait_ge(*M.full("values0", p, i))
                    if i == 0:
                        act.wait_ge(zeroed_tables, 2)
                    ps = M.slot("values0", p, i)
                    for h in range(2):
                        last = run(VTD0[64 * h:64 * h + 64, :, i, 64 * h:64 * h + 64],
                                   ps[64 * h:64 * h + 64, 0:256].rearrange("p (b k) -> p b k", b=B), ACT.Copy)
                        if h == 0:
                            last.then_inc(act_chain, 1)
                    last.then_inc(M.emptied["act"], 1)
                elif stage == "fold":
                    act.wait_ge(*S.full("fold", p, i))
                    if i >= 2:
                        act.wait_ge(*M.full("values", p, TPB * (i - 2) + 1))
                    run(VW[:, i % 2, :, :].rearrange("p c n -> p (c n)"), S.slot("fold", p, i)[:, :], ACT.Copy)\
                        .then_inc(S.emptied["act"], 1)
                elif stage == "xT":
                    act.wait_ge(*TR.full("xT", p, i))
                    ps = TR.slot("xT", p, i)[:, 0:P]
                    if p == 5:
                        if i == 0:
                            act.wait_ge(loaded["cols"], 16)
                        ins = run(XT[:, i, :], ps, ACT.Identity, bias=col("ln_bias"), scale=col("ln_scale"))
                    else:
                        ins = run(XT[:, i, :], ps, ACT.Copy)
                    ins.then_inc(TR.emptied["act"], 1)
                elif stage == "queryT":
                    if i > 0:
                        act.wait_ge(*S.full("scores", p, i - 1))
                    for n in range(2):
                        act.wait_ge(*TR.full(f"queryT{n}", p, i))
                        run(QT0[:, 4 * n:4 * n + 4, :].rearrange("p c q -> p (c q)"), TR.slot(f"queryT{n}", p, i)[:, :],
                            ACT.Copy).then_inc(TR.emptied["act"], 1)
                elif stage == "query":
                    act.wait_ge(*M.full("query", p, i))
                    if p == 4 and i == 0:
                        act.wait_ge(loaded["cols"], 16)
                    if i >= 2:
                        act.wait_ge(*S.full("scores", p, i - 2))
                    elif p == 6:
                        act.wait_ge(*S.full("scores", 4, T - 2 + i))
                    run(QT[:, i % 2, :], M.slot("query", p, i)[:, 0:P], ACT.Identity, bias=col(f"bq{p}"))\
                        .then_inc(M.emptied["act"], 1)
                elif stage == "scores" and p > 0:
                    a = ATT.index(p) * T + i
                    q, t = (p, i - 4) if i >= 4 else (ATT[ATT.index(p) - 1], T - 4 + i)
                    act.wait_ge(*TR.full("probsT1", q, t))
                    act.wait_ge(*S.full("scores", p, i))
                    run(SM[:, a % 4, :, :].rearrange("p h k -> p (h k)"), S.slot("scores", p, i)[:, :], ACT.Copy)\
                        .then_inc(S.emptied["act"], 1)
                elif stage == "exp":
                    a = ATT.index(p) * T + i
                    act.wait_ge(*shifted.at(p, i))
                    scale = {0: 1.0, 2: 1.0 / float(np.sqrt(np.float32(D))), 4: 1.0 / float(np.sqrt(np.float32(DH))),
                             6: 1.0 / float(np.sqrt(np.float32(DH)))}[p]
                    run(SM[:, a % 4, :, :], SM[:, a % 4, :, :], ACT.Exp, scale=scale).then_inc(exped.sem, 1)
                elif stage == "probsT":
                    a = ATT.index(p) * T + i
                    if a >= 2:
                        q, t = (p, i - 2) if i >= 2 else (ATT[ATT.index(p) - 1], T - 2 + i)
                        act.wait_ge(*M.full("values", q, t))
                    for n in range(2):
                        act.wait_ge(*TR.full(f"probsT{n}", p, i))
                        run(PT[:, a % 2, 4 * n:4 * n + 4, :].rearrange("p c q -> p (c q)"),
                            TR.slot(f"probsT{n}", p, i)[:, :], ACT.Copy).then_inc(TR.emptied["act"], 1)
                elif stage == "outT":
                    act.wait_ge(*TR.full("outT", p, i))
                    if i >= 2:
                        act.wait_ge(*M.full("project", p, i - 2))
                    run(OT[:, i % 2, :], TR.slot("outT", p, i)[:, 0:P], ACT.Copy).then_inc(TR.emptied["act"], 1)
                elif stage == "keys" and p in (4, 6) and i == 0:
                    if p == 4:
                        act.wait_ge(loaded["cols"], 16)
                    act.wait_ge(*M.full("keys", p, i))
                    if p == 6:
                        act.wait_ge(*kbd_ready.at(4, B - 1))
                    run(KT[:, :, :].rearrange("p b k -> p (b k)"), M.slot("keys", p, i)[:, 0:256],
                        ACT.Identity, bias=col(f"bk{p}")).then_inc(M.emptied["act"], 1)
                elif stage == "context":
                    b = i
                    if p == 2 and b == 0:
                        act.wait_ge(zeroed_values, 5)
                        act.wait_ge(loaded["ctx2"], 16)
                    if b >= 2 or p > 2:
                        q, c = (p, b - 2) if b >= 2 else (p - 2, b + 2)
                        act.wait_ge(*M.full("values", q, TPB * c + 1))
                    if p in (4, 6):
                        act.wait_ge(*M.full("ctxv", p, b))
                    for h in range(2):
                        half = slice(64 * h, 64 * h + 64)
                        src = CTX2[half, b, :] if p == 2 else M.slot("ctxv", p, b)[half, 0:D]
                        ins = run(diagonal(half, b % 2, DH * h, 2 * DH, DH),
                                  src.rearrange("p (c h d) -> p c h d", h=2, d=DH)[:, :, h, :], ACT.Copy)
                        if h == 0:
                            ins.then_inc(act_chain, 1)
                        elif p == 2:
                            ins.then_inc(vex_ready.sem, 1)
                        else:
                            ins.then_inc(M.emptied["act"], 1)
                elif stage == "logits":
                    act.wait_ge(*gate_top.at(p, i))
                    if p == 1:
                        ins = run(GV[:, 1, :], TOP[:, :, 0], ACT.Tanh, scale=0.5)
                    elif p == 3:
                        ins = run(GE[:, :, :], LG[:, :, :], ACT.Tanh, scale=0.5)
                    else:
                        ins = run(GV[:, 1, :], GV[:, 0, :], ACT.Exp)
                    ins.then_inc(gate_exp.sem, 1)
                elif stage == "tanh":
                    b, j = i // TPB, i % TPB
                    act.wait_ge(*S.full("hidden0", p, i))
                    act.wait_ge(*gate_ready.at(p, b))
                    if i >= 2:
                        act.wait_ge(*TR.full("gatedT", p, i - 2))
                    run(TH[i % 2], S.slot("hidden0", p, i)[:, 0:512], ACT.Tanh,
                        scale=GSCALE[:, b % 2, j:j + 1]).then_inc(tanh_ready.sem, 1)
                elif stage == "gatedT":
                    act.wait_ge(*TR.full("gatedT", p, i))
                    if i > 0:
                        act.wait_ge(*M.full("down0", p, i - 1))
                    run(AT, TR.slot("gatedT", p, i)[:, :], ACT.Copy).then_inc(TR.emptied["act"], 1)
                elif stage == "gateT":
                    act.wait_ge(*TR.full("gateT", p, i))
                    if i >= 2:
                        act.wait_ge(*M.full("bias2", p, i - 2))
                    elif p == 7:
                        act.wait_ge(*M.full("bias2", 3, B - 2 + i))
                    run(GT[:, i % 2, :, :].rearrange("p j q -> p (j q)"), TR.slot("gateT", p, i)[:, 0:TPB * P],
                        ACT.Copy).then_inc(TR.emptied["act"], 1)
                elif stage == "hidden":
                    b, e = i
                    if (p, b, e) == (3, 0, 0):
                        act.wait_ge(loaded["cols"], 16)
                    act.wait_ge(*S.full("hidden", p, i))
                    if b > 0 or e >= 3:
                        n = b * E + e - 3
                        act.wait_ge(*M.full("expert", p, (n // E, n % E)))
                    elif p == 3:
                        act.wait_ge(*M.full("values", 0, T - 1))
                    for c in range(HID[p] // P):
                        ins = run(HT[:, (b * E + e) % 3, c, :], S.slot("hidden", p, i)[:, 256 * c:256 * c + 256],
                                  ACT.Silu if p == 3 else ACT.Relu,
                                  bias=col(f"b1_{p}", e * (HID[p] // P) + c))
                        if c < HID[p] // P - 1:
                            ins.then_inc(act_chain, 1)
                    ins.then_inc(S.emptied["act"], 1)
                elif stage == "mix":
                    act.wait_ge(*M.full("mix", p, i))
                    run(XAT[:, 256 * i:256 * i + 256], M.slot("mix", p, i)[:, 0:256], ACT.Identity,
                        bias=col("attn_b")).then_inc(M.emptied["act"], 1)
                elif stage == "hidden5":
                    act.wait_ge(*S.full("hidden5", p, i))
                    if i >= 2:
                        act.wait_ge(*M.full("expert5", p, i - 2))
                    for c in range(4):
                        ins = run(HT5[:, i % 2, c, :], S.slot("hidden5", p, i)[:, c * P:c * P + P], ACT.Gelu,
                                  bias=col("b1_5", 4 * i + c))
                        if c < 3:
                            ins.then_inc(act_chain, 1)
                    ins.then_inc(S.emptied["act"], 1)
                elif stage == "expert5":
                    act.wait_ge(*M.full("expert5", p, i))
                    run(group(EOT, i),
                        M.slot("expert5", p, i)[:, 0:P].rearrange("p (m q) -> p m q", m=2), ACT.Identity,
                        bias=col("b2_5", i)).then_inc(M.emptied["act"], 1)
                elif stage == "next5":
                    act.wait_ge(*S.full("next5", p, i))
                    run(YT[:, 512 * i:512 * i + 512], S.slot("next5", p, i)[:, 0:512], ACT.Gelu,
                        bias=col("next_b")).then_inc(S.emptied["act"], 1)

        @block.vector
        def _(dve):
            v = nc.vector
            steps = [0]

            def mark(ins):
                steps[0] += 1
                ins.then_inc(dve_chain, 1)

            def settle():
                dve.wait_ge(dve_chain, steps[0])

            def step(ins):
                mark(ins)
                settle()

            def sure(ins, sem_, n):
                ins.then_inc(sem_, 1)
                dve.wait_ge(sem_, n)

            def rsqrt(rs, variance):
                step(v.tensor_scalar(VAR[:, :], variance, EPS, None, ALU.add))
                step(v.tensor_scalar(rs.bitcast(I32), VAR[:, :].bitcast(I32), -0.5, RSQRT_SEED, ALU.mult, ALU.add))
                step(v.tensor_tensor(SQ2[:, :], rs, rs, ALU.mult))
                step(v.scalar_tensor_tensor(HV[:, :], SQ2[:, :], -0.5, VAR[:, :], ALU.mult, ALU.mult))
                step(v.scalar_tensor_tensor(rs, HV[:, :], 1.5, rs, ALU.add, ALU.mult))
                step(v.tensor_tensor(SQ2[:, :], rs, rs, ALU.mult))
                step(v.tensor_tensor(HV[:, :], SQ2[:, :], VAR[:, :], ALU.mult))
                step(v.tensor_scalar(SQ2[:, :], HV[:, :], 0.375, -1.25, ALU.mult, ALU.add))
                step(v.tensor_tensor(HV[:, :], SQ2[:, :], HV[:, :], ALU.mult))
                step(v.scalar_tensor_tensor(rs, HV[:, :], 1.875, rs, ALU.add, ALU.mult))

            def gate(p, b):
                dve.wait_ge(*M.full("logits", p, b))
                ps = M.slot("logits", p, b)[:, 0:TPB * P].rearrange("p (j n) -> p j n", j=TPB)[:, :, 0:E]
                if p == 1:
                    sure(v.tensor_copy(LG[:, :, :], ps), *M.read("logits", p, b))
                else:
                    if b == 0:
                        dve.wait_ge(loaded["gbias"], 16)
                    bias = GB[:, (3, 7).index(p), :].unsqueeze(1).broadcast_to([P, TPB, E])
                    sure(v.tensor_tensor(LG[:, :, :], ps, bias, ALU.add), *M.read("logits", p, b))
                for j in range(TPB):
                    mark(v.max(TOP[:, j, :], LG[:, j, :]))
                settle()
                for j in range(TPB):
                    mark(v.max_index(IDX[:, j, :], TOP[:, j, :], LG[:, j, :]))
                settle()
                if p == 3:
                    sure(v.tensor_tensor(LG[:, :, :], LG[:, :, :], TOP[:, :, 0:1].broadcast_to([P, TPB, E]),
                                         ALU.subtract), *gate_top.at(p, b))
                elif p == 7:
                    sure(v.tensor_tensor(GV[:, 0, :], TOP[:, :, 1], TOP[:, :, 0], ALU.subtract), *gate_top.at(p, b))
                if p == 1:
                    sure(v.tensor_copy(IDF[:, :, :], IDX[:, :, :]), *gate_top.at(p, b))
                else:
                    step(v.tensor_copy(IDF[:, :, :], IDX[:, :, :]))
                for n in range(2 if p == 7 else 1):
                    mark(v.tensor_tensor(HOT[:, n, :, :], const("iota").unsqueeze(1).broadcast_to([P, TPB, E]),
                                         IDF[:, :, n:n + 1].broadcast_to([P, TPB, E]), ALU.is_equal))
                settle()
                dve.wait_ge(*gate_exp.at(p, b))
                if b >= 2 and p > 1:
                    dve.wait_ge(*TR.full("gateT", p, b - 2))
                out_ = GATE[:, b % 2, :, 0:E]

                def wide(k):
                    return GV[:, k, :].unsqueeze(2).broadcast_to([P, TPB, E])
                if p == 1:
                    if b >= 2:
                        dve.wait_ge(*tanh_ready.at(p, TPB * (b - 2) + 1))
                    step(v.tensor_scalar(GSCALE[:, b % 2, :], GV[:, 1, :], 1.0, 0.25, ALU.add, ALU.mult))
                    step(v.scalar_tensor_tensor(GV[:, 2, :], GSCALE[:, b % 2, :], 2.0, GSCALE[:, b % 2, :],
                                                ALU.mult, ALU.mult))
                    sure(v.tensor_tensor(out_, HOT[:, 0, :, :], wide(2), ALU.mult), *gate_ready.at(p, b))
                elif p == 3:
                    step(v.tensor_scalar(GE2[:, :, :], GE[:, :, :], -1.0, 1.0, ALU.mult, ALU.add))
                    step(v.reciprocal(GE2[:, :, :], GE2[:, :, :]))
                    step(v.scalar_tensor_tensor(GE[:, :, :], GE[:, :, :], 1.0, GE2[:, :, :], ALU.add, ALU.mult))
                    step(v.tensor_reduce(GV[:, 0, :], GE[:, :, :], X_AXIS, ALU.add))
                    step(v.reciprocal(GV[:, 1, :], GV[:, 0, :]))
                    sure(v.tensor_tensor(out_, HOT[:, 0, :, :], wide(1), ALU.mult), *gate_ready.at(p, b))
                else:
                    step(v.tensor_scalar(GV[:, 2, :], GV[:, 1, :], 1.0, None, ALU.add))
                    step(v.reciprocal(GV[:, 3, :], GV[:, 2, :]))
                    mark(v.tensor_tensor(GE[:, :, :], HOT[:, 0, :, :], wide(3), ALU.mult))
                    step(v.tensor_tensor(GV[:, 4, :], GV[:, 1, :], GV[:, 3, :], ALU.mult))
                    step(v.tensor_tensor(GE2[:, :, :], HOT[:, 1, :, :], wide(4), ALU.mult))
                    sure(v.tensor_tensor(out_, GE2[:, :, :], GE[:, :, :], ALU.add), *gate_ready.at(p, b))

            def add_to_x(ring, job, p, i, t):
                dve.wait_ge(*ring.full(job, p, i))
                sure(v.tensor_tensor(X[:, t, :], ring.slot(job, p, i)[:, 0:D], X[:, t, :], ALU.add),
                     *ring.read(job, p, i))

            step(v.memset(GATE[:, :, :, :], 0.0))

            for stage, p, i in SCHEDULE:
                if stage in ("stats", "stats2"):
                    n = variances.index((stage, p, i))
                    if p == -1:
                        dve.wait_ge(loaded["x01" if i < 2 else "x23"], 16)
                    src = X if stage == "stats" else XN
                    for j in range(TPB):
                        mark(v.bn_stats(ST[:, j, :], src[:, TPB * i + j, :]))
                    settle()
                    for j in range(TPB):
                        mark(v.bn_aggr(MV[:, n % 3, j, :], ST[:, j, :]))
                    settle()
                    rsqrt(RS[:, n % 3, :], MV[:, n % 3, :, 1])
                elif stage in ("norm", "norm2"):
                    stats = "stats" if stage == "norm" else "stats2"
                    n = variances.index((stats, p, i)) % 3
                    src, dst = (X, XN) if stage == "norm" else (XN, XN2)
                    for j in range(TPB):
                        t = TPB * i + j
                        ins = v.tensor_scalar(dst[:, t, :], src[:, t, :], MV[:, n, j, 0:1], RS[:, n, j:j + 1],
                                              ALU.subtract, ALU.mult)
                        if j < TPB - 1 or (p == 4 and stage == "norm"):
                            mark(ins)
                    if p == 4 and stage == "norm":
                        settle()
                    else:
                        sure(ins, *normed.at(p + 1, i))
                elif stage == "keys0":
                    dve.wait_ge(*S.full("keys0", p, i))
                    if i == 0:
                        dve.wait_ge(zeroed_tables, 2)
                    ps = S.slot("keys0", p, i)
                    step(v.tensor_tensor(K1.rearrange("p (b k) -> p b k", b=B),
                                         ps[:, 0:256].rearrange("p (b k) -> p b k", b=B), COSK, ALU.mult))
                    sure(v.tensor_tensor(K2.rearrange("p (b k) -> p b k", b=B),
                                         ps[:, 512:768].rearrange("p (b k) -> p b k", b=B), SINK, ALU.mult),
                         *S.read("keys0", p, i))
                    for h in range(2):
                        half = slice(64 * h, 64 * h + 64)
                        ins = v.tensor_tensor(KBD0[half, :, i, 64 * h:64 * h + 64],
                                              K1[half, :].rearrange("p (b k) -> p b k", b=B),
                                              K2[half, :].rearrange("p (b k) -> p b k", b=B), ALU.add)
                        if h == 0:
                            step(ins)
                    sure(ins, *keys0_ready.at(p, i))
                    if i == 0:
                        dve.wait_ge(loaded["consts"], 16)
                        dve.wait_ge(loaded["mask0"], 16)
                        sure(v.tensor_scalar(FILL0[:, :, :], M0[:, :, :], 0.0, FILL, ALU.is_equal, ALU.mult), fills, 1)
                elif stage == "query0":
                    j = i % TPB
                    if i == 0:
                        dve.wait_ge(loaded["consts"], 16)
                    dve.wait_ge(*S.full("query0", p, i))
                    if i > 0:
                        dve.wait_ge(*rotated.at(p, i - 1))
                    ps = S.slot("query0", p, i)[:, :].rearrange("p (h d) -> p h d", h=H)
                    t1, t2 = (t.rearrange("p (h d) -> p h d", h=H) for t in (T1, T2))

                    def table(t, lo, hi):
                        return t[:, j, lo:hi].unsqueeze(1).broadcast_to([P, H, hi - lo])
                    step(v.tensor_tensor(t1, ps, table(COSQ, 0, D0), ALU.mult))
                    step(v.tensor_tensor(t2[:, :, 0:32], ps[:, :, 32:64], table(SINQ, 0, 32), ALU.mult))
                    sure(v.tensor_tensor(t2[:, :, 32:64], ps[:, :, 0:32], table(SINQ, 32, 64), ALU.mult),
                         *S.read("query0", p, i))
                elif stage == "scores":
                    a = ATT.index(p) * T + i
                    b = i // TPB
                    sm = SM[:, a % 4, :, :]
                    if p == 0:
                        if i >= 4:
                            dve.wait_ge(*TR.full("probsT1", p, i - 4))
                        dve.wait_ge(*S.full("scores", p, i))
                        dve.wait_ge(*relmasked.at(p, i))
                        sure(v.scalar_tensor_tensor(sm, S.slot("scores", p, i)[:, :].rearrange("p (h k) -> p h k", h=H),
                                                    float(D0) ** -0.5, RELM[:, i % 2, :, :], ALU.mult, ALU.add),
                             *S.read("scores", p, i))
                    else:
                        dve.wait_ge(*S.read("scores", p, i))
                    if a >= 3:
                        dve.wait_ge(*shifted.at(*((p, i - 3) if i >= 3 else (ATT[ATT.index(p) - 1], T - 3 + i))))
                    sure(v.tensor_reduce(MX[:, a % 3, :], sm, X_AXIS, ALU.max), *masked.at(p, i))
                elif stage == "sum":
                    a = ATT.index(p) * T + i
                    dve.wait_ge(*exped.at(p, i))
                    if i >= 2:
                        dve.wait_ge(*weighed.at(p, i - 2))
                    step(v.tensor_reduce(SUM[:, i % 2, :], SM[:, a % 4, :, :], X_AXIS, ALU.add))
                    sure(v.reciprocal(RCP[:, i % 2, :], SUM[:, i % 2, :]), *summed.at(p, i))
                elif stage == "values" and p == 0:
                    add_to_x(M, "values", p, i, i)
                    if i == 0:
                        dve.wait_ge(loaded["mask1"], 16)
                        dve.wait_ge(loaded["mask2"], 16)
                        for n, (fill, m) in enumerate(((FILL1, M1), (FILL2, M2))):
                            sure(v.tensor_scalar(fill[:, :].rearrange("p (t k) -> p t k", k=SK), m[:, :, :], 0.0, FILL,
                                                 ALU.is_equal, ALU.mult), masks_ready, n + 1)
                        sure(v.tensor_copy(IDENT_R[:, :], IDENT), masks_ready, 3)
                elif stage == "values":
                    k = i % 2
                    if p == 2 and i < 2:
                        dve.wait_ge(*weighed.at(0, T - 2 + i))
                    dve.wait_ge(*M.full("values", p, i))
                    ps = M.slot("values", p, i)
                    step(v.reciprocal(RCP[:, k, :], ps[:, D:VX]))
                    if i >= 2:
                        dve.wait_ge(*TR.full("outT", p, i - 2))
                    sure(v.tensor_tensor(AO[:, k, :].rearrange("p (h d) -> p h d", h=H),
                                         ps[:, 0:D].rearrange("p (h d) -> p h d", h=H),
                                         RCP[:, k, :].unsqueeze(2).broadcast_to([P, H, DH]), ALU.mult),
                         *M.read("values", p, i))
                elif stage == "project":
                    if i % TPB == 0:
                        dve.wait_ge(*biased.at(p, i // TPB))
                    add_to_x(M, "project", p, i, i)
                elif stage == "logits":
                    gate(p, i)
                elif stage == "tanh":
                    b, j = i // TPB, i % TPB
                    dve.wait_ge(*S.full("hidden0", p, i))
                    if i >= 2:
                        dve.wait_ge(*gated_ready.at(p, i - 2))
                    step(v.tensor_tensor(UP[i % 2].rearrange("p (e f) -> p e f", e=E),
                                         S.slot("hidden0", p, i)[:, 512:1024].rearrange("p (e f) -> p e f", e=E),
                                         GATE[:, b % 2, j, 0:E].unsqueeze(2).broadcast_to([P, E, I0]), ALU.mult))
                elif stage == "gated":
                    dve.wait_ge(*tanh_ready.at(p, i))
                    sure(v.scalar_tensor_tensor(GP[i % 2], TH[i % 2], 1.0, S.slot("hidden0", p, i)[:, 0:512],
                                                ALU.add, ALU.mult), *S.read("hidden0", p, i))
                elif stage == "down0":
                    add_to_x(M, "down0", p, i, i)
                elif stage == "bias2":
                    dve.wait_ge(*M.full("bias2", p, i))
                    both = X[:, TPB * i:TPB * i + TPB, :]
                    sure(v.tensor_tensor(both, M.slot("bias2", p, i)[:, 0:TPB * D].rearrange("p (j d) -> p j d", j=TPB),
                                         both, ALU.add), *M.read("bias2", p, i))
                elif stage == "expert":
                    b, e = i
                    dve.wait_ge(*M.full("expert", p, i))
                    for j in range(TPB):
                        t = TPB * b + j
                        ins = v.scalar_tensor_tensor(X[:, t, :], M.slot("expert", p, i)[:, j * D:j * D + D],
                                                     GATE[:, b % 2, j, e:e + 1], X[:, t, :], ALU.mult, ALU.add)
                        if j < TPB - 1:
                            mark(ins)
                    sure(ins, *M.read("expert", p, i))
                elif stage == "back":
                    add_to_x(TR, "back", p, i, i)

        @block.gpsimd
        def _(pool):
            g = nc.gpsimd
            def sure(ins, sem_, n):
                ins.then_inc(sem_, 1)
                pool.wait_ge(sem_, n)

            sure(g.memset(KBD0, 0.0), zeroed_tables, 1)
            sure(g.memset(VTD0, 0.0), zeroed_tables, 2)
            sure(g.memset(ROW[:, :, :], 0.0), zeroed_rows, 1)
            sure(g.memset(BIAS2[:, :, :], 0.0), zeroed_rows, 2)
            sure(g.memset(VEX[:, :, :, :], 0.0), zeroed_values, 1)
            for r in range(2):
                for h in range(2):
                    sure(g.memset(diagonal(slice(64 * h, 64 * h + 64), r, D + h, 2, 1), 1.0),
                         zeroed_values, 2 + 2 * r + h)

            for stage, p, i in SCHEDULE:
                if stage == "query0":
                    b, j = i // TPB, i % TPB
                    pool.wait_ge(*S.read("query0", p, i))
                    if i >= 2:
                        pool.wait_ge(*TR.full("queryT1", p, i - 2))
                    sure(g.tensor_tensor(QR[:, i % 2, :], T1, T2, ALU.add), *rotated.at(p, i))
                    if i == 0:
                        pool.wait_ge(loaded["rel"], 16)
                        pool.wait_ge(fills, 1)
                    if i >= 2:
                        pool.wait_ge(*masked.at(p, i - 2))
                    sure(g.tensor_tensor(RELM[:, i % 2, :, :], REL[:, j, :, :],
                                         FILL0[:, b, :].unsqueeze(1).broadcast_to([P, H, SK]), ALU.add),
                         *relmasked.at(p, i))
                elif stage == "keys":
                    b = i
                    if (p, b) == (2, 0):
                        pool.wait_ge(loaded["consts"], 16)
                        pool.wait_ge(loaded["ctxT"], 16)
                    if p > 2 and b == 0:
                        pool.wait_ge(*M.read("keys", p, 0))
                    if b >= 2 or p > 2:
                        q, c = (p, b - 2) if b >= 2 else (p - 2, b + 2)
                        pool.wait_ge(*S.full("scores", q, TPB * c + 1))
                    src = CTXT[:, b, 0, :] if p == 2 else KT[:, b, :]
                    sure(g.tensor_tensor(KBD[:, b % 2, :, :], src.unsqueeze(1).broadcast_to([P, H, SK]), HEADS,
                                         ALU.mult), *kbd_ready.at(p, b))
                elif stage == "scores":
                    a = ATT.index(p) * T + i
                    pool.wait_ge(*masked.at(p, i))
                    sure(g.tensor_tensor(SM[:, a % 4, :, :], SM[:, a % 4, :, :],
                                         MX[:, a % 3, :].unsqueeze(2).broadcast_to([P, H, SK]), ALU.subtract),
                         *shifted.at(p, i))
                elif stage == "sum":
                    a = ATT.index(p) * T + i
                    pool.wait_ge(*summed.at(p, i))
                    sure(g.tensor_tensor(SM[:, a % 4, :, :], SM[:, a % 4, :, :],
                                         RCP[:, i % 2, :].unsqueeze(2).broadcast_to([P, H, SK]), ALU.mult),
                         *weighed.at(p, i))
                elif stage == "wsplit":
                    if i == 0:
                        pool.wait_ge(loaded[f"w1_{p}"], 16)
                        if p == 3:
                            pool.wait_ge(*masked.at(0, T - 1))
                        else:
                            pool.wait_ge(*S.full("hidden", 3, (B - 1, E - 1)))
                    part = slice(CHUNK * i, CHUNK * i + CHUNK)
                    w = W1_ALL[p][:, part]
                    sure(g.tensor_tensor(W1_HI[p][:, part], w, const("one").broadcast_to([P, CHUNK]), ALU.mult), *w_rounded.at(p, i))
                    sure(g.tensor_tensor(W1_LO[p][:, part], w, W1_HI[p][:, part].bitcast(F32), ALU.subtract),
                         *w_split.at(p, i))
                elif stage == "xsplit":
                    pool.wait_ge(*TR.read("xT", p, TPB * i + 1))
                    if i >= 2:
                        pool.wait_ge(*S.full("hidden", p, (i - 2, E - 1)))
                    xt = XT[:, TPB * i:TPB * i + TPB, :].rearrange("p j q -> p (j q)")
                    sure(g.tensor_tensor(X_HI[:, i % 2, :], xt, const("one").broadcast_to([P, TPB * P]), ALU.mult), *x_rounded.at(p, i))
                    sure(g.tensor_tensor(X_LO[:, i % 2, :], xt, X_HI[:, i % 2, :].bitcast(F32), ALU.subtract),
                         *x_split.at(p, i))
                elif stage == "bias":
                    if (p, i) == (2, 0):
                        pool.wait_ge(loaded["xbias"], 16)
                    pool.wait_ge(*normed.at(p, i))
                    both = X[:, TPB * i:TPB * i + TPB, :]
                    sure(g.tensor_tensor(both, both, XBIAS[:, (2, 4, 6).index(p), :].unsqueeze(1)
                                         .broadcast_to([P, TPB, D]), ALU.add), *biased.at(p, i))
                elif stage == "gated":
                    pool.wait_ge(*S.read("hidden0", p, i))
                    sure(g.tensor_tensor(TH[i % 2], GP[i % 2], UP[i % 2], ALU.mult), *gated_ready.at(p, i))


def _constants():
    c = np.zeros((P, NCONST), np.float32)

    def put(name, a):
        o, n = CONSTS[name]
        c[:, o:o + n] = np.asarray(a, np.float32).reshape(P, n)

    put("ident", np.eye(P))
    row0 = np.zeros((P, P))
    row0[0] = 1
    put("row0", row0)
    put("heads", np.arange(P)[:, None] // DH == np.arange(H)[None, :])
    put("one", np.ones(P))
    put("iota", np.tile(np.arange(E), (P, 1)))
    inv = (1.0 / np.float32(10000.0) ** (np.arange(0, D0, 2, dtype=np.float32) / np.float32(D0))).astype(np.float32)
    angle = np.repeat(np.outer(np.arange(SQ, dtype=np.float32), inv).astype(np.float32), 2, axis=-1)
    cos, sin = np.cos(angle), np.sin(angle)
    sin[:, :D0 // 2] *= -1
    put("cosq", cos.reshape(TPB, P, D0).transpose(1, 0, 2))
    put("sinq", sin.reshape(TPB, P, D0).transpose(1, 0, 2))
    put("cosk", np.tile(cos[:SK].T, (2, 1)))
    put("sink", np.tile(sin[:SK].T, (2, 1)))
    return c


def _layout(a):
    f = {}
    f["x"] = a["x"][ORDER].reshape(T, P, D).transpose(1, 0, 2)
    ctx = a["ctx_1024"][ORDER]
    f["ctxT"] = np.tile(ctx.transpose(2, 0, 1)[:, :, None], (1, 1, 2, 1))
    f["ctx2"] = np.tile(ctx.transpose(1, 0, 2), (2, 1, 1))
    f["consts"] = _constants()
    zero = np.zeros((P, NCOLS), np.float32)

    def cols(v):
        return v.reshape(-1, P).T

    for name, v in (("bq4", a["L2_xattn_bq"]), ("bk4", a["L2_xattn_bk"]), ("bq6", a["L3_xattn_bq"]),
                    ("bk6", a["L3_xattn_bk"]), ("ln_scale", a["L2_ffn_ln_scale"]), ("ln_bias", a["L2_ffn_ln_bias"]),
                    ("attn_b", a["L2_ffn_attn_b"]), ("next_b", a["L2_ffn_next_b"]), ("b1_3", a["L1_ffn_b1"]),
                    ("b1_5", a["L2_ffn_b1"]), ("b2_5", a["L2_ffn_b2"]), ("b1_7", a["L3_ffn_b1"])):
        v = cols(v)
        zero[:, COLS[name]:COLS[name] + v.shape[1]] = v
    f["cols"] = zero
    m = {"w2": a["L1_xattn_W_fc"].T, "q4": a["L2_xattn_Wq"].T, "k4": a["L2_xattn_Wk"].T, "v4": a["L2_xattn_Wv"].T,
         "w4": a["L2_xattn_Wo"].T, "attn": a["L2_ffn_attn_w"].T, "next": a["L2_ffn_next_w"].T,
         "q6": a["L3_xattn_Wq"], "k6": a["L3_xattn_Wk"], "v6": a["L3_xattn_Wv"], "w6": a["L3_xattn_Wo"],
         "gate1": a["L0_ffn_gate_w"].T, "gate3": a["L1_ffn_Wg"], "gate7": a["L3_ffn_Wr"]}
    mats = np.zeros((P, len(MATS), P), np.float32)
    for n, name in enumerate(MATS):
        mats[:, n, :m[name].shape[1]] = m[name]
    f["mats"] = mats
    r = {"b2": "L1_xattn_b_fc", "v4": "L2_xattn_bv", "b4": "L2_xattn_bo", "v6": "L3_xattn_bv", "b6": "L3_xattn_bo"}
    f["rows"] = np.stack([a[r[n]] for n in ROWS])[None]
    f["xbias"] = np.tile(np.stack([a[r[n]] for n in XBIASES])[None], (P, 1, 1))
    f["bias2"] = np.stack([a["L1_ffn_b2"], a["L3_ffn_b2"]], axis=1)
    f["gbias"] = np.tile(np.stack([a["L1_ffn_bg"], a["L3_ffn_br"]])[None], (P, 1, 1))
    away = np.abs(np.arange(SQ)[:, None] - np.arange(SK)[None, :])
    rel = a["L0_xattn_rel_pos_bias"][:, away]
    f["relpos"] = rel.reshape(H, TPB, P, SK).transpose(2, 1, 0, 3)
    f["mask0"] = np.tile(a["mask_BxS2_bf1"][ORDER].view(np.uint8)[None], (P, 1, 1))
    f["mask1"] = a["mask_Bx1xSxS2_ik1"][ORDER].reshape(T, P, SK).transpose(1, 0, 2)
    f["mask2"] = np.tile(a["mask_Bx1x1xS2_ik0"][ORDER].reshape(1, B, SK), (P, 1, 1))
    f["wq0"] = a["L0_xattn_Wq"]
    wk = a["L0_xattn_Wk"].reshape(D, KV0, D0)
    f["wk0"] = np.tile(wk, (1, 1, 2))
    f["wk0r"] = np.tile(np.roll(wk, D0 // 2, axis=-1), (1, 1, 2))
    f["wv0"] = np.tile(a["L0_xattn_Wv"].reshape(D, KV0, D0), (1, 1, 2))
    f["wo0"] = a["L0_xattn_Wo"].reshape(NPAIR, P, D).transpose(1, 0, 2)
    f["wg0"] = a["L0_ffn_w_gate"].transpose(2, 0, 1).reshape(D, E * I0)
    f["wu0"] = a["L0_ffn_w_up"].transpose(2, 0, 1).reshape(D, E * I0)
    f["wd0"] = a["L0_ffn_w_down"].transpose(0, 2, 1).reshape(4, P, D).transpose(1, 0, 2)
    for p, n in ((3, "L1_ffn_W1"), (5, "L2_ffn_w1"), (7, "L3_ffn_W1")):
        f[f"w1_{p}"] = a[n].transpose(1, 0, 2)
    for p, n in ((3, "L1_ffn_W2"), (5, "L2_ffn_w2"), (7, "L3_ffn_W2")):
        f[f"w2_{p}"] = a[n].reshape(E, HID[p] // P, P, D).transpose(2, 0, 1, 3)
    return {k: np.ascontiguousarray(v) for k, v in f.items()}


NAMES = ["x", "ctxT", "ctx2", "consts", "cols", "mats", "rows", "xbias", "bias2", "gbias", "relpos", "mask0", "mask1", "mask2",
         "wq0", "wk0", "wk0r", "wv0", "wo0", "wg0", "wu0", "wd0", "w1_3", "w2_3", "w1_5", "w2_5", "w1_7", "w2_7"]


def kernel(**inputs):
    import concourse.bacc as bacc
    from concourse.bass_utils import run_bass_kernel_spmd

    laid = _layout({k: np.asarray(v) for k, v in inputs.items()})
    nc = bacc.Bacc("TRN2", target_bir_lowering=False, num_devices=1)
    arrays, args = {}, []
    for name in NAMES:
        v = laid[name]
        arrays[f"in_{name}"] = v
        args.append(nc.dram_tensor(f"in_{name}", v.shape, mybir.dt.from_np(v.dtype), kind="ExternalInput").ap())
    args.append(nc.dram_tensor("out_x", (P, T, D), F32, kind="ExternalOutput").ap())
    build(nc, *args)
    r = run_bass_kernel_spmd(nc, [arrays], core_ids=[0])
    return np.ascontiguousarray(r.results[0]["out_x"].transpose(1, 0, 2).reshape(B, SQ, D)[ORDER])
```
